# Optimizing a Trainium2 kernel written in Bass

```python
import numpy as np
import jax
import jax.numpy as jnp

def _softmax(x, axis=-1):
    return jax.nn.softmax(x, axis=axis)

def _gelu(x):
    return jax.nn.gelu(x, approximate=True)

def _silu(x):
    return jax.nn.silu(x)

def _sigmoid(x):
    return jax.nn.sigmoid(x)

def _layernorm(x, axis=-1, eps=1e-05):
    m = jnp.mean(x, axis=axis, keepdims=True)
    v = jnp.var(x, axis=axis, keepdims=True)
    return (x - m) / jnp.sqrt(v + eps)

def _scatter_add(tgt, idx, src, axis=0):
    return tgt.at[idx].add(src)

def _segment_sum(src, seg, n):
    return jax.ops.segment_sum(src, seg, n)
kernel_name = 'mk_gnn_resnorm_d4_gnn_r32_4737c1'

def setup_inputs(seed: int=0):
    np.random.seed(seed)
    _w = jnp.asarray

    def _rec_inputs():
        import jax
        import jax.numpy as jnp
        _gk = jax.random.key(seed)
        x = -0.0003713 + 1 * jax.random.normal(jax.random.fold_in(_gk, 1), (3125, 128), jnp.float32)
        _s = jax.random.randint(jax.random.fold_in(_gk, 2), (50000,), 0, 3125, jnp.int32)
        _d = jax.random.randint(jax.random.fold_in(_gk, 3), (50000,), 0, 3125, jnp.int32)
        _loop = jnp.arange(3125, dtype=jnp.int32)
        src = jnp.concatenate([_s, _d, _loop])
        dst = jnp.concatenate([_d, _s, _loop])
        _o = jnp.argsort(dst, stable=True)
        src = src[_o]
        dst = dst[_o]
        edge_attr_3 = 0.000844983 + 0.999762 * jax.random.normal(jax.random.fold_in(_gk, 11), (103125, 3), jnp.float32)
        edge_attr_64 = 0.000102155 + 1.00015 * jax.random.normal(jax.random.fold_in(_gk, 12), (103125, 64), jnp.float32)
        edge_weight = jax.random.uniform(jax.random.fold_in(_gk, 14), (103125,), jnp.float32, 0.0, 0.999999)
        edge_weight1 = jax.random.uniform(jax.random.fold_in(_gk, 15), (103125, 1), jnp.float32, 0.0, 5.99999)
        return (x, src, dst, edge_attr_3, edge_attr_64, edge_weight, edge_weight1)
    x, src, dst, edge_attr_3, edge_attr_64, edge_weight, edge_weight1 = _rec_inputs()

    def _L0_gnn_setup():
        import jax, jax.numpy as jnp
        import numpy as np
        N_NODES = 3125
        N_EDGES = 15625
        IN_CH = 128
        EDGE_CH = 64

        def _glorot(key, shape):
            fan_in, fan_out = (shape[0], shape[1])
            lim = (6.0 / (fan_in + fan_out)) ** 0.5
            return jax.random.uniform(key, shape, jnp.float32, -lim, lim)
        key = jax.random.key(seed)
        ks = jax.random.split(key, 14)
        x = jax.random.normal(ks[0], (N_NODES, IN_CH), jnp.float32)
        edge_index = jax.random.randint(ks[1], (2, N_EDGES), 0, N_NODES, jnp.int64)
        edge_attr = jax.random.normal(ks[2], (N_EDGES, EDGE_CH), jnp.float32)
        timestamps = jax.random.uniform(ks[3], (N_EDGES,), jnp.float32)
        We1 = _glorot(ks[4], (EDGE_CH, 2 * EDGE_CH))
        be1 = jnp.zeros((2 * EDGE_CH,), jnp.float32)
        We2 = _glorot(ks[5], (2 * EDGE_CH, IN_CH))
        be2 = jnp.zeros((IN_CH,), jnp.float32)
        Wt = _glorot(ks[6], (1, IN_CH))
        bt = jnp.zeros((IN_CH,), jnp.float32)
        Wn1 = _glorot(ks[7], (2 * IN_CH, IN_CH))
        bn1 = jnp.zeros((IN_CH,), jnp.float32)
        Wn2 = _glorot(ks[8], (IN_CH, IN_CH))
        bn2 = jnp.zeros((IN_CH,), jnp.float32)
        return {'x': x, 'edge_index': edge_index, 'edge_attr': edge_attr, 'timestamps': timestamps, 'We1': We1, 'be1': be1, 'We2': We2, 'be2': be2, 'Wt': Wt, 'bt': bt, 'Wn1': Wn1, 'bn1': bn1, 'Wn2': Wn2, 'bn2': bn2}
    _L0_gnn_all = _L0_gnn_setup()
    _L0_gnn_in = {k: v for k, v in _L0_gnn_all.items() if k in ('We1', 'be1', 'We2', 'be2', 'Wt', 'bt', 'Wn1', 'bn1', 'Wn2', 'bn2')}
    del _L0_gnn_all

    def _L1_gnn_setup():
        import jax, jax.numpy as jnp
        import numpy as np
        import math
        N = 1250
        E = 20000
        HID = 128
        H = 8
        HD = HID // H
        CUTOFF = 5.0
        LN_EPS = 1e-05

        def _linear_params(key, out_d, in_d):
            k1, k2 = jax.random.split(key)
            s = 1.0 / np.sqrt(in_d)
            W = jax.random.uniform(k1, (out_d, in_d), minval=-s, maxval=s, dtype=jnp.float32)
            b = jax.random.uniform(k2, (out_d,), minval=-s, maxval=s, dtype=jnp.float32)
            return (W, b)
        key = jax.random.key(seed)
        ks = jax.random.split(key, 12)
        x = jax.random.normal(ks[0], (N, HID), dtype=jnp.float32)
        edge_index = jax.random.randint(ks[1], (2, E), 0, N, dtype=jnp.int64)
        edge_vec = jax.random.normal(ks[2], (E, 3), dtype=jnp.float32)
        edge_length = jax.random.uniform(ks[3], (E, 1), dtype=jnp.float32) * 6.0
        Wq, bq = _linear_params(ks[4], HID, HID)
        Wk, bk = _linear_params(ks[5], HID, HID)
        Wv, bv = _linear_params(ks[6], HID, HID)
        We1, be1 = _linear_params(ks[7], HID, 1)
        We2, be2 = _linear_params(ks[8], H, HID)
        Wo, bo = _linear_params(ks[9], HID, HID)
        ln_g = jnp.ones((HID,), jnp.float32)
        ln_b = jnp.zeros((HID,), jnp.float32)
        return {'x': x, 'edge_vec': edge_vec, 'edge_length': edge_length, 'Wq': Wq, 'bq': bq, 'Wk': Wk, 'bk': bk, 'Wv': Wv, 'bv': bv, 'We1': We1, 'be1': be1, 'We2': We2, 'be2': be2, 'Wo': Wo, 'bo': bo, 'ln_g': ln_g, 'ln_b': ln_b, 'edge_index': edge_index}
    _L1_gnn_all = _L1_gnn_setup()
    _L1_gnn_in = {k: v for k, v in _L1_gnn_all.items() if k in ('Wq', 'bq', 'Wk', 'bk', 'Wv', 'bv', 'We1', 'be1', 'We2', 'be2', 'Wo', 'bo', 'ln_g', 'ln_b')}
    del _L1_gnn_all

    def _L2_gnn_setup():
        import jax, jax.numpy as jnp
        import numpy as np
        N = 50000
        E = 25000
        IN_DIM = 128
        OUT_DIM = 128
        key = jax.random.key(seed)
        k1, k2, k3, k4, k5, k6 = jax.random.split(key, 6)
        x = jax.random.normal(k1, (N, IN_DIM), dtype=jnp.float32)
        edge_index = jax.random.randint(k2, (2, E), 0, N, dtype=jnp.int64)
        bound = 1.0 / np.sqrt(IN_DIM)
        w_self = jax.random.uniform(k3, (OUT_DIM, IN_DIM), minval=-bound, maxval=bound, dtype=jnp.float32)
        b_self = jax.random.uniform(k4, (OUT_DIM,), minval=-bound, maxval=bound, dtype=jnp.float32)
        w_neigh = jax.random.uniform(k5, (OUT_DIM, IN_DIM), minval=-bound, maxval=bound, dtype=jnp.float32)
        b_neigh = jax.random.uniform(k6, (OUT_DIM,), minval=-bound, maxval=bound, dtype=jnp.float32)
        return {'x': x, 'edge_index': edge_index, 'w_self': w_self, 'b_self': b_self, 'w_neigh': w_neigh, 'b_neigh': b_neigh}
    _L2_gnn_all = _L2_gnn_setup()
    _L2_gnn_in = {k: v for k, v in _L2_gnn_all.items() if k in ('w_self', 'b_self', 'w_neigh', 'b_neigh')}
    del _L2_gnn_all

    def _L3_gnn_setup():
        import jax, jax.numpy as jnp
        import numpy as np
        N_NODES = 3125
        IN_CH = 128
        HID_CH = 128
        N_EDGES = 50000

        def gcn_conv(x, edge_index, W, b):
            n = x.shape[0]
            loops = jnp.arange(n, dtype=edge_index.dtype)
            row = jnp.concatenate([edge_index[0], loops])
            col = jnp.concatenate([edge_index[1], loops])
            deg = jax.ops.segment_sum(jnp.ones_like(col, dtype=x.dtype), col, num_segments=n)
            dinv = jnp.where(deg > 0, jax.lax.rsqrt(deg), 0.0)
            norm = dinv[row] * dinv[col]
            h = x @ W
            msg = h[row] * norm[:, None]
            out = jax.ops.segment_sum(msg, col, num_segments=n)
            return out + b

        def mish(x):
            return x * jnp.tanh(jax.nn.softplus(x))
        key = jax.random.key(seed)
        k1, k2, k3, k4 = jax.random.split(key, 4)
        x = jax.random.normal(k1, (N_NODES, IN_CH), dtype=jnp.float32)
        edge_index = jax.random.randint(k2, (2, N_EDGES), 0, N_NODES, dtype=jnp.int64)
        limit = float(np.sqrt(6.0 / (IN_CH + HID_CH)))
        W = jax.random.uniform(k3, (IN_CH, HID_CH), minval=-limit, maxval=limit, dtype=jnp.float32)
        b = jnp.zeros((HID_CH,), dtype=jnp.float32)
        return {'x': x, 'edge_index': edge_index, 'W': W, 'b': b}
    _L3_gnn_all = _L3_gnn_setup()
    _L3_gnn_in = {k: v for k, v in _L3_gnn_all.items() if k in ('W', 'b')}
    del _L3_gnn_all
    return {'x': x, 'src': src, 'dst': dst, 'edge_attr_3': edge_attr_3, 'edge_attr_64': edge_attr_64, 'edge_weight': edge_weight, 'edge_weight1': edge_weight1, 'L0_gnn_We1': _L0_gnn_in['We1'], 'L0_gnn_be1': _L0_gnn_in['be1'], 'L0_gnn_We2': _L0_gnn_in['We2'], 'L0_gnn_be2': _L0_gnn_in['be2'], 'L0_gnn_Wt': _L0_gnn_in['Wt'], 'L0_gnn_bt': _L0_gnn_in['bt'], 'L0_gnn_Wn1': _L0_gnn_in['Wn1'], 'L0_gnn_bn1': _L0_gnn_in['bn1'], 'L0_gnn_Wn2': _L0_gnn_in['Wn2'], 'L0_gnn_bn2': _L0_gnn_in['bn2'], 'L1_gnn_Wq': _L1_gnn_in['Wq'], 'L1_gnn_bq': _L1_gnn_in['bq'], 'L1_gnn_Wk': _L1_gnn_in['Wk'], 'L1_gnn_bk': _L1_gnn_in['bk'], 'L1_gnn_Wv': _L1_gnn_in['Wv'], 'L1_gnn_bv': _L1_gnn_in['bv'], 'L1_gnn_We1': _L1_gnn_in['We1'], 'L1_gnn_be1': _L1_gnn_in['be1'], 'L1_gnn_We2': _L1_gnn_in['We2'], 'L1_gnn_be2': _L1_gnn_in['be2'], 'L1_gnn_Wo': _L1_gnn_in['Wo'], 'L1_gnn_bo': _L1_gnn_in['bo'], 'L1_gnn_ln_g': _L1_gnn_in['ln_g'], 'L1_gnn_ln_b': _L1_gnn_in['ln_b'], 'L2_gnn_w_self': _L2_gnn_in['w_self'], 'L2_gnn_b_self': _L2_gnn_in['b_self'], 'L2_gnn_w_neigh': _L2_gnn_in['w_neigh'], 'L2_gnn_b_neigh': _L2_gnn_in['b_neigh'], 'L3_gnn_W': _L3_gnn_in['W'], 'L3_gnn_b': _L3_gnn_in['b']}

def reference(x, src, dst, edge_attr_3, edge_attr_64, edge_weight, edge_weight1, L0_gnn_We1, L0_gnn_be1, L0_gnn_We2, L0_gnn_be2, L0_gnn_Wt, L0_gnn_bt, L0_gnn_Wn1, L0_gnn_bn1, L0_gnn_Wn2, L0_gnn_bn2, L1_gnn_Wq, L1_gnn_bq, L1_gnn_Wk, L1_gnn_bk, L1_gnn_Wv, L1_gnn_bv, L1_gnn_We1, L1_gnn_be1, L1_gnn_We2, L1_gnn_be2, L1_gnn_Wo, L1_gnn_bo, L1_gnn_ln_g, L1_gnn_ln_b, L2_gnn_w_self, L2_gnn_b_self, L2_gnn_w_neigh, L2_gnn_b_neigh, L3_gnn_W, L3_gnn_b):
    import jax
    import jax.numpy as jnp

    def _L0_gnn_ref(x, edge_index, edge_attr, timestamps, We1, be1, We2, be2, Wt, bt, Wn1, bn1, Wn2, bn2):
        import jax, jax.numpy as jnp
        import numpy as np
        N_NODES = 3125
        N_EDGES = 15625
        IN_CH = 128
        EDGE_CH = 64

        def _glorot(key, shape):
            fan_in, fan_out = (shape[0], shape[1])
            lim = (6.0 / (fan_in + fan_out)) ** 0.5
            return jax.random.uniform(key, shape, jnp.float32, -lim, lim)
        ts = timestamps[:, None]
        ef = jax.nn.relu(edge_attr @ We1 + be1) @ We2 + be2
        tw = jax.nn.sigmoid(ts @ Wt + bt)
        ef = ef * tw
        row, col = (edge_index[0], edge_index[1])
        combined = jnp.concatenate([x[row], ef], axis=1)
        msg = jax.nn.relu(combined @ Wn1 + bn1) @ Wn2 + bn2
        out = jax.ops.segment_sum(msg, col, num_segments=x.shape[0])
        return out + x

    def _L1_gnn_ref(x, edge_vec, edge_length, Wq, bq, Wk, bk, Wv, bv, We1, be1, We2, be2, Wo, bo, ln_g, ln_b, edge_index):
        import jax, jax.numpy as jnp
        import numpy as np
        import math
        N = 1250
        E = 20000
        HID = 128
        H = 8
        HD = HID // H
        CUTOFF = 5.0
        LN_EPS = 1e-05

        def _linear_params(key, out_d, in_d):
            k1, k2 = jax.random.split(key)
            s = 1.0 / np.sqrt(in_d)
            W = jax.random.uniform(k1, (out_d, in_d), minval=-s, maxval=s, dtype=jnp.float32)
            b = jax.random.uniform(k2, (out_d,), minval=-s, maxval=s, dtype=jnp.float32)
            return (W, b)
        row, col = (edge_index[0], edge_index[1])
        n = x.shape[0]
        q = (x @ Wq.T + bq).reshape(n, H, HD)
        k = (x @ Wk.T + bk).reshape(n, H, HD)
        v = (x @ Wv.T + bv).reshape(n, H, HD)
        attn = jnp.einsum('ehd,ehd->eh', q[row], k[col]) / math.sqrt(HD)
        edge_bias = jax.nn.silu(edge_length @ We1.T + be1) @ We2.T + be2
        attn = attn + edge_bias
        cut = 0.5 * (jnp.cos(edge_length * math.pi / CUTOFF) + 1.0)
        cut = cut * (edge_length < CUTOFF).astype(jnp.float32)
        attn = attn * cut
        attn_exp = jnp.exp(attn - jnp.max(attn, axis=0, keepdims=True))
        attn_sum = jax.ops.segment_sum(attn_exp, row, num_segments=n)
        attn = attn_exp / (attn_sum[row] + 1e-08)
        out = jax.ops.segment_sum(attn[:, :, None] * v[col], row, num_segments=n)
        out = out.reshape(n, HID) @ Wo.T + bo
        h = x + out
        mu = jnp.mean(h, axis=-1, keepdims=True)
        var = jnp.mean(jnp.square(h - mu), axis=-1, keepdims=True)
        return (h - mu) / jnp.sqrt(var + LN_EPS) * ln_g + ln_b

    def _L2_gnn_ref(x, edge_index, w_self, b_self, w_neigh, b_neigh):
        import jax, jax.numpy as jnp
        import numpy as np
        N = 50000
        E = 25000
        IN_DIM = 128
        OUT_DIM = 128
        src = edge_index[0]
        dst = edge_index[1]
        n = x.shape[0]
        agg = jax.ops.segment_sum(x[src], dst, num_segments=n)
        deg = jax.ops.segment_sum(jnp.ones((src.shape[0],), dtype=x.dtype), dst, num_segments=n)
        deg = jnp.maximum(deg, 1.0)[:, None]
        mean_neigh = agg / deg
        return x @ w_self.T + b_self + mean_neigh @ w_neigh.T + b_neigh

    def _L3_gnn_ref(x, edge_index, W, b):
        import jax, jax.numpy as jnp
        import numpy as np
        N_NODES = 3125
        IN_CH = 128
        HID_CH = 128
        N_EDGES = 50000

        def gcn_conv(x, edge_index, W, b):
            n = x.shape[0]
            loops = jnp.arange(n, dtype=edge_index.dtype)
            row = jnp.concatenate([edge_index[0], loops])
            col = jnp.concatenate([edge_index[1], loops])
            deg = jax.ops.segment_sum(jnp.ones_like(col, dtype=x.dtype), col, num_segments=n)
            dinv = jnp.where(deg > 0, jax.lax.rsqrt(deg), 0.0)
            norm = dinv[row] * dinv[col]
            h = x @ W
            msg = h[row] * norm[:, None]
            out = jax.ops.segment_sum(msg, col, num_segments=n)
            return out + b

        def mish(x):
            return x * jnp.tanh(jax.nn.softplus(x))
        return mish(gcn_conv(x, edge_index, W, b))
    edge_index = jnp.stack([src, dst])
    x = _layernorm(x + _L0_gnn_ref(x, edge_index, edge_attr_64, edge_weight, L0_gnn_We1, L0_gnn_be1, L0_gnn_We2, L0_gnn_be2, L0_gnn_Wt, L0_gnn_bt, L0_gnn_Wn1, L0_gnn_bn1, L0_gnn_Wn2, L0_gnn_bn2), axis=-1)
    x = _layernorm(x + _L1_gnn_ref(x, edge_attr_3, edge_weight1, L1_gnn_Wq, L1_gnn_bq, L1_gnn_Wk, L1_gnn_bk, L1_gnn_Wv, L1_gnn_bv, L1_gnn_We1, L1_gnn_be1, L1_gnn_We2, L1_gnn_be2, L1_gnn_Wo, L1_gnn_bo, L1_gnn_ln_g, L1_gnn_ln_b, edge_index), axis=-1)
    x = _layernorm(x + _L2_gnn_ref(x, edge_index, L2_gnn_w_self, L2_gnn_b_self, L2_gnn_w_neigh, L2_gnn_b_neigh), axis=-1)
    x = _layernorm(x + _L3_gnn_ref(x, edge_index, L3_gnn_W, L3_gnn_b), axis=-1)
    return x

_drawn_inputs = setup_inputs


def setup_inputs(seed=0):
    import zlib

    import numpy as np

    out = dict(_drawn_inputs(seed))
    spreads = {'L0_gnn_be1': (0.0, 0.278),
     'L0_gnn_be2': (0.0, 0.1),
     'L0_gnn_bt': (0.0, 2.0),
     'L0_gnn_bn1': (0.0, 0.1),
     'L0_gnn_bn2': (0.0, 0.1),
     'L1_gnn_ln_g': (1.0, 0.2),
     'L1_gnn_ln_b': (0.0, 0.1),
     'L3_gnn_b': (0.0, 0.1)}
    factors = {'edge_weight': 106.552,
     'edge_weight1': 8.0,
     'L0_gnn_Wt': 8.0,
     'L1_gnn_Wq': 8.0,
     'L1_gnn_bq': 27.245,
     'L1_gnn_Wk': 8.0,
     'L1_gnn_bk': 64.0,
     'L1_gnn_bv': 4.601,
     'L1_gnn_We1': 8.0,
     'L1_gnn_be1': 8.0,
     'L1_gnn_We2': 8.0,
     'L1_gnn_be2': 179.797,
     'L1_gnn_bo': 2.735}
    for name, (base, spread) in spreads.items():
        noise = np.random.default_rng([zlib.crc32(name.encode()), seed]).standard_normal(out[name].shape)
        drawn = base * np.exp(spread * noise) if base else spread * noise
        out[name] = jnp.asarray(drawn.astype(out[name].dtype))
    for name, factor in factors.items():
        out[name] = (out[name] * factor).astype(out[name].dtype)
    return out
```

```python
from contextlib import ExitStack

import numpy as np

import concourse.bass as bass
from concourse import mybir

F32 = mybir.dt.float32
I32 = mybir.dt.int32
ALU = mybir.AluOpType
ACT = mybir.ActivationFunctionType
AX = mybir.AxisListType.X

P = 125
K = 15
GK = 3
G = K // GK
C = 128
H = 8
W = C + H
TABLES = 5
LN_EPS = 1e-5
CUTOFF = 5.0


def bcast(ap, n):
    return ap.unsqueeze(2).to_broadcast([ap.shape[0], ap.shape[1], n])


def rows(ap, a):
    return ap.unsqueeze(1).to_broadcast([ap.shape[0], a, ap.shape[1]])


class Gnn:

    def __init__(self, nc, ins, out):
        self.nc, self.ins, self.out = nc, ins, out
        self.N = ins["x"].shape[0]
        self.E = ins["src"].shape[0]
        self.NB = self.N // P
        self.S = self.E // (P * K)
        assert self.N == P * self.NB and self.E == P * K * self.S
        self.used, self.names = [], {}

    def unique(self, name):
        self.names[name] = self.names.get(name, 0) + 1
        return name if self.names[name] == 1 else f"{name}_{self.names[name]}"

    def sbuf(self, name, shape, dt):
        return self.nc.sbuf_tensor(self.unique(name), shape, dt)

    def psum(self, name, shape, dt):
        return self.nc.psum_tensor(self.unique(name), shape, dt)

    def sem(self, ctx, name):
        s = ctx.enter_context(self.nc.semaphore(name))
        self.used.append(s)
        return s

    def clear_semaphores(self):
        used, self.used = self.used, []
        with self.nc.Block() as block:
            @block.gpsimd
            def _(pool):
                for s in used:
                    pool.sem_clear(s)


def load_and_lay_out(g, ctx):
    nc, ins, NB, S, N = g.nc, g.ins, g.NB, g.S, g.N

    def sb(name, shape, dt=F32):
        t = ctx.enter_context(g.sbuf(name, shape, dt))
        tensors[name] = t
        return t

    tensors = {}
    g.t = tensors
    loads = []
    for name in ("L0_gnn_We1", "L0_gnn_We2", "L0_gnn_Wn2", "L3_gnn_W"):
        loads.append((sb(name, list(ins[name].shape))[:], ins[name]))
    wn1 = ins["L0_gnn_Wn1"]
    loads.append((sb("Wn1_node", [C, C])[:], wn1[0:C, :]))
    loads.append((sb("Wn1_edge", [C, C])[:], wn1[C:2 * C, :]))
    turned = {"L1_gnn_Wq": C, "L1_gnn_Wk": C, "L1_gnn_Wv": C, "L1_gnn_Wo": C,
              "L2_gnn_w_self": C, "L2_gnn_w_neigh": C, "L1_gnn_We2": H}
    for name, n in turned.items():
        loads.append((sb(name, [n, C])[:], ins[name]))
        sb(name + "_T", [C, n])
    for name in ("L0_gnn_be1", "L0_gnn_be2", "L0_gnn_bt", "L1_gnn_be1"):
        loads.append((sb(name, [C, 1])[:], ins[name].rearrange("(p o) -> p o", o=1)))
    for name in ("L0_gnn_bn1", "L0_gnn_bn2", "L1_gnn_bq", "L1_gnn_bk", "L1_gnn_bv", "L1_gnn_bo",
                 "L1_gnn_ln_g", "L1_gnn_ln_b", "L2_gnn_b_self", "L2_gnn_b_neigh", "L3_gnn_b"):
        loads.append((sb(name, [P, C])[:], ins[name].partition_broadcast(P)))
    loads.append((sb("Wt_row", [1, C])[:], ins["L0_gnn_Wt"]))
    loads.append((sb("We1_row", [1, C])[:], ins["L1_gnn_We1"].rearrange("n o -> o n")))
    loads.append((sb("be2_row", [1, H])[:], ins["L1_gnn_be2"].rearrange("(o n) -> o n", o=1)))
    loads.append((sb("x_sb", [P, NB, C])[:], ins["x"].rearrange("(p j) c -> p j c", p=P)))
    for key in ("src", "dst"):
        loads.append((sb(key + "_i", [P, S + 1, K], I32)[:, 0:S, :],
                      ins[key].rearrange("(s p k) -> p s k", p=P, k=K)))
        sb(key + "_f", [P, S, K])
        sb(key + "_once", [P, S, K], I32)
    ident = sb("ident", [C, C])
    ones = sb("ones", [C, C])
    lower = sb("lower", [P, P])
    part_i = sb("part_i", [P, 1], I32)
    trash = sb("trash", [P, 1])
    b_l2 = sb("b_l2", [P, C])
    zeros = sb("zeros", [P, 26 * W])

    with ExitStack() as ph:
        loaded = g.sem(ph, "loaded")
        pool_ready = g.sem(ph, "pool_ready")
        pool_step = g.sem(ph, "pool_step")
        turned_ps = g.sem(ph, "turned_ps")
        dve_done = g.sem(ph, "dve_done")
        turn = ph.enter_context(g.psum("turn", [C, 8, 512], F32))
        block = ph.enter_context(nc.Block())

        @block.sync
        def _(sp):
            for to, of in loads:
                sp.dma_start(to, of).then_inc(loaded, 16)
            sp.wait_ge(loaded, 16 * len(loads))

        @block.gpsimd
        def _(pool):
            pool.memset(ident[:], 0.0).then_inc(pool_step, 1)
            pool.memset(ones[:], 1.0).then_inc(pool_step, 1)
            pool.memset(lower[:], 1.0).then_inc(pool_step, 1)
            pool.memset(zeros[:], 0.0).then_inc(pool_step, 1)
            pool.wait_ge(pool_step, 4)
            pool.affine_select(out=ident[:], in_=ident[:], compare_op=ALU.not_equal, fill=1.0, base=0,
                               pattern=[[-1, C]], channel_multiplier=1).then_inc(pool_ready, 1)
            pool.affine_select(out=lower[:], in_=lower[:], compare_op=ALU.is_gt, fill=0.0, base=0,
                               pattern=[[-1, P]], channel_multiplier=1).then_inc(pool_ready, 1)
            pool.iota(part_i[:], pattern=[[0, 1]], base=N, channel_multiplier=1).then_inc(pool_ready, 1)

        @block.tensor
        def _(pe):
            pe.wait_ge(loaded, 16 * len(loads))
            pe.wait_ge(pool_ready, 3)
            for i, (name, n) in enumerate(turned.items()):
                pe.transpose(turn[:, i, 0:n], g.t[name][:], ident[0:n, 0:n]).then_inc(turned_ps, 1)

        @block.vector
        def _(dve):
            for i, (name, n) in enumerate(turned.items()):
                dve.wait_ge(turned_ps, i + 1)
                dve.tensor_copy(g.t[name + "_T"][:], turn[:, i, 0:n])
            dve.tensor_tensor(b_l2[:], g.t["L2_gnn_b_self"][:], g.t["L2_gnn_b_neigh"][:], ALU.add)
            for key in ("src", "dst"):
                dve.memset(g.t[key + "_i"][:, S, :], 0)
                dve.tensor_copy(g.t[key + "_f"][:], g.t[key + "_i"][:, 0:S, :])
            dve.tensor_copy(trash[:], part_i[:]).then_inc(dve_done, 1)
            dve.wait_ge(dve_done, 1)


def mark_duplicates(g):
    nc, S, N = g.nc, g.S, g.N
    with ExitStack() as ph:
        key_slot = ph.enter_context(g.sbuf("key_slot", [P, K], F32))
        same = ph.enter_context(g.sbuf("same", [P, GK, P], F32))
        late = ph.enter_context(g.sbuf("late", [P, K], F32))
        shift = ph.enter_context(g.sbuf("shift", [P, K], F32))
        key_ps = ph.enter_context(g.psum("key_ps", [P, GK, 128], F32))
        for key in ("dst", "src"):
            key_f, once = g.t[key + "_f"], g.t[key + "_once"]
            staged = g.sem(ph, "staged_" + key)
            rows_ready = g.sem(ph, "rows_ready_" + key)
            compared = g.sem(ph, "compared_" + key)
            chain = g.sem(ph, "chain_" + key)
            block = nc.Block()
            with block:
                @block.tensor
                def _(pe):
                    with pe.Fori(0, S) as s:
                        for i in range(G):
                            pe.wait_ge(staged, s + 1)
                            pe.wait_ge(compared, s * G + (i + 1))
                            for k in range(GK):
                                ins = pe.transpose(key_ps[:, k, 0:P],
                                                   key_slot[:, i * GK + k:i * GK + k + 1].to_broadcast([P, P]),
                                                   g.t["ident"][0:P, 0:P])
                            ins.then_inc(rows_ready, 1)

                @block.vector
                def _(dve):
                    dve.sem_inc(compared, 1)
                    per = 3 * G + 4
                    with dve.Fori(0, S) as s:
                        dve.tensor_copy(key_slot[:], key_f[:, bass.ds(s, 1), :].rearrange("p o k -> p (o k)"))\
                            .then_inc(staged, 1)
                        dve.wait_ge(staged, s + 1)
                        for i in range(G):
                            dve.wait_ge(rows_ready, s * G + (i + 1))
                            dve.tensor_tensor(same[:], key_ps[:, :, 0:P], bcast(key_slot[:, i * GK:(i + 1) * GK], P),
                                              ALU.is_equal).then_inc(chain, 1)
                            dve.wait_ge(chain, s * per + (3 * i + 1))
                            dve.tensor_tensor(same[:], same[:], rows(g.t["lower"][:], GK), ALU.mult).then_inc(chain, 1)
                            dve.wait_ge(chain, s * per + (3 * i + 2))
                            dve.tensor_reduce(late[:, i * GK:(i + 1) * GK], same[:], AX, ALU.max).then_inc(chain, 1)
                            dve.wait_ge(chain, s * per + (3 * i + 3))
                            dve.sem_inc(compared, 1)
                        dve.tensor_scalar(shift[:], key_slot[:], -1.0, g.t["trash"][:, 0:1], ALU.mult, ALU.add)\
                            .then_inc(chain, 1)
                        dve.wait_ge(chain, s * per + (3 * G + 1))
                        dve.tensor_tensor(shift[:], shift[:], late[:], ALU.mult).then_inc(chain, 1)
                        dve.wait_ge(chain, s * per + (3 * G + 2))
                        dve.tensor_tensor(late[:], shift[:], key_slot[:], ALU.add).then_inc(chain, 1)
                        dve.wait_ge(chain, s * per + (3 * G + 3))
                        dve.tensor_copy(once[:, bass.ds(s, 1), :].rearrange("p o k -> p (o k)"), late[:])\
                            .then_inc(chain, 1)
                        dve.wait_ge(chain, s * per + per)
    g.clear_semaphores()


def node_linear(g, name, src, outs):
    nc, NB = g.nc, g.NB
    B = 5
    assert NB % B == 0 and len(outs) <= 3
    with ExitStack() as ph:
        stage = ph.enter_context(g.sbuf(name + "_stage", [P, B, C], F32))
        turned = ph.enter_context(g.sbuf(name + "_turned", [C, B, P], F32))
        turn_ps = ph.enter_context(g.psum(name + "_turn_ps", [C, B + 3, 128], F32))
        out_ps = [ph.enter_context(g.psum(f"{name}_out_ps{i}", [P, B + 3, 128], F32))
                  for i in range(len(outs))]
        staged = g.sem(ph, name + "_staged")
        turned_ready = g.sem(ph, name + "_turned_ready")
        copied = g.sem(ph, name + "_copied")
        product_ready = g.sem(ph, name + "_product_ready")
        stored = g.sem(ph, name + "_stored")
        block = ph.enter_context(nc.Block())

        @block.scalar
        def _(act):
            with act.Fori(0, NB // B) as i:
                act.wait_ge(turned_ready, i + 1)
                act.copy(stage[:], src[:, bass.ds(i * B, B), :]).then_inc(staged, 1)

        @block.tensor
        def _(pe):
            pe.sem_inc(turned_ready, 1)
            with pe.Fori(0, NB // B) as i:
                pe.wait_ge(staged, i + 1)
                pe.wait_ge(copied, i + 1)
                for b in range(B):
                    ins = pe.transpose(turn_ps[:, b, 0:P], stage[:, b, :], g.t["ident"][0:P, 0:P])
                ins.then_inc(turned_ready, 1)
                pe.wait_ge(copied, i + 2)
                pe.wait_ge(stored, i + 1)
                for o, (weight, _, _) in enumerate(outs):
                    for b in range(B):
                        ins = pe.matmul(out_ps[o][:, b, :], turned[:, b, :], weight[:], start=True, stop=True)
                ins.then_inc(product_ready, 1)

        @block.vector
        def _(dve):
            dve.sem_inc(copied, 1)
            dve.sem_inc(stored, 1)
            with dve.Fori(0, NB // B) as i:
                dve.wait_ge(turned_ready, i + 2)
                dve.tensor_copy(turned[:], turn_ps[:, 0:B, 0:P]).then_inc(copied, 1)
                dve.wait_ge(product_ready, i + 1)
                for o, (_, added, dst) in enumerate(outs):
                    more = rows(added[:], B) if len(added.shape) == 2 else added[:, bass.ds(i * B, B), :]
                    ins = dve.tensor_tensor(dst[:, bass.ds(i * B, B), :], out_ps[o][:, 0:B, :], more, ALU.add)
                ins.then_inc(stored, 1)
            dve.wait_ge(stored, NB // B + 1)


def to_table(g, pairs):
    with ExitStack() as ph:
        written = g.sem(ph, "written")
        block = ph.enter_context(g.nc.Block())

        @block.sync
        def _(sp):
            for table, feats in pairs:
                sp.dma_start(table.rearrange("(p j) c -> p j c", p=P), feats[:]).then_inc(written, 16)
            sp.wait_ge(written, 16 * len(pairs))


class Chain:

    def __init__(self, eng, sem):
        self.eng, self.sem, self.n = eng, sem, 0

    def __call__(self, ins):
        self.n += 1
        ins.then_inc(self.sem, 1)
        self.eng.wait_ge(self.sem, self.n)


def layer_norm(g, h, scratch, dst=None, scale=None, shift=None):
    nc, NB = g.nc, g.NB
    dst = h if dst is None else dst
    with ExitStack() as ph:
        m = ph.enter_context(g.sbuf("ln_m", [P, NB], F32))
        v = ph.enter_context(g.sbuf("ln_v", [P, NB], F32))
        chain = g.sem(ph, "ln_chain")
        var_ready = g.sem(ph, "ln_var_ready")
        root_ready = g.sem(ph, "ln_root_ready")
        block = ph.enter_context(nc.Block())

        @block.vector
        def _(dve):
            link = Chain(dve, chain)
            link(dve.tensor_reduce(m[:], h[:], AX, ALU.add))
            link(dve.tensor_scalar(m[:], m[:], 1.0 / C, None, ALU.mult))
            link(dve.tensor_tensor(h[:], h[:], bcast(m[:], C), ALU.subtract))
            link(dve.tensor_tensor(scratch[:], h[:], h[:], ALU.mult))
            link(dve.tensor_reduce(v[:], scratch[:], AX, ALU.add))
            dve.tensor_scalar(v[:], v[:], 1.0 / C, LN_EPS, ALU.mult, ALU.add).then_inc(var_ready, 1)
            dve.wait_ge(root_ready, 1)
            link(dve.reciprocal(m[:], v[:]))
            link(dve.tensor_tensor(dst[:], h[:], bcast(m[:], C), ALU.mult))
            if scale is not None:
                link(dve.tensor_tensor(dst[:], dst[:], rows(scale[:], NB), ALU.mult))
                link(dve.tensor_tensor(dst[:], dst[:], rows(shift[:], NB), ALU.add))

        @block.scalar
        def _(act):
            act.wait_ge(var_ready, 1)
            act.activation(v[:], v[:], ACT.Sqrt).then_inc(root_ready, 1)


def clear_tables(g):
    with ExitStack() as ph:
        cleared = g.sem(ph, "cleared")
        block = ph.enter_context(g.nc.Block())

        @block.sync
        def _(sp):
            for table in g.sums:
                sp.dma_start(table.rearrange("(p j) c -> p (j c)", p=P), g.t["zeros"][:]).then_inc(cleared, 16)
            sp.wait_ge(cleared, 16 * TABLES)


def collect_sums(g, total, scratch):
    nc, NB, N = g.nc, g.NB, g.N
    with ExitStack() as ph:
        loaded = [g.sem(ph, f"sums_loaded{u}") for u in range(TABLES)]
        chain = g.sem(ph, "sums_chain")
        block = ph.enter_context(nc.Block())

        @block.sync
        def _(sp):
            for u, table in enumerate(g.sums):
                to = total if u == 0 else scratch[(u - 1) % 2]
                if u >= 3:
                    sp.wait_ge(chain, u - 2)
                sp.dma_start(to[:], table[0:N, :].rearrange("(p j) c -> p j c", p=P)).then_inc(loaded[u], 16)

        @block.vector
        def _(dve):
            link = Chain(dve, chain)
            dve.wait_ge(loaded[0], 16)
            for u in range(1, TABLES):
                dve.wait_ge(loaded[u], 16)
                link(dve.tensor_tensor(total[:], total[:], scratch[(u - 1) % 2][:], ALU.add))


class Scatter:

    def __init__(self, g, ph, key):
        nc = g.nc
        self.g, self.key_f, self.once = g, g.t[key + "_f"], g.t[key + "_once"]
        sb = lambda name, shape, dt=F32: ph.enter_context(g.sbuf(name, shape, dt))
        self.key_slot = sb("key_slot", [P, K])
        self.once_slot = sb("once_slot", [P, K], I32)
        self.same = sb("same", [P, K, P])
        self.msg = sb("msg", [P, K, W])
        self.tile_sums = sb("tile_sums", [P, K, W])
        self.key_ps = ph.enter_context(g.psum("key_ps", [P, GK + 1, 128], F32))
        self.sum_ps = ph.enter_context(g.psum("sum_ps", [P, 512], F32))
        sem = lambda name: g.sem(ph, name)
        self.keys_staged, self.key_rows, self.same_ready = sem("keys_staged"), sem("key_rows"), sem("same_ready")
        self.msg_ready, self.summed, self.sums_out = sem("msg_ready"), sem("summed"), sem("sums_out")
        self.once_staged, self.rows_out, self.tick = sem("once_staged"), sem("rows_out"), sem("tick")
        self.scattered, self.base = g.scattered, g.scattered_so_far
        g.scattered_so_far += 16 * g.S * (K // TABLES)

    def stage_keys(self, dve, s):
        dve.wait_ge(self.summed, s * G + 1)
        dve.tensor_copy(self.key_slot[:], self.key_f[:, bass.ds(s, 1), :].rearrange("p o k -> p (o k)"))\
            .then_inc(self.keys_staged, 1)

    def compare(self, dve, s):
        for i in range(G):
            at = slice(i * GK, (i + 1) * GK)
            dve.wait_ge(self.key_rows, s * G + (i + 1))
            dve.wait_ge(self.keys_staged, s + 1)
            dve.tensor_tensor(self.same[:, at, :], self.key_ps[:, 0:GK, 0:P], bcast(self.key_slot[:, at], P),
                              ALU.is_equal).then_inc(self.same_ready, 1)

    def stage_once(self, dve, s):
        dve.wait_ge(self.rows_out, s + 1)
        dve.tensor_copy(self.once_slot[:], self.once[:, bass.ds(s, 1), :].rearrange("p o k -> p (o k)"))\
            .then_inc(self.once_staged, 1)

    def key_rows_and_sums(self, pe, s):
        for i in range(G):
            pe.wait_ge(self.keys_staged, s + 1)
            pe.wait_ge(self.same_ready, s * G + (i + 1))
            for k in range(GK):
                ins = pe.transpose(self.key_ps[:, k, 0:P],
                                   self.key_slot[:, i * GK + k:i * GK + k + 1].to_broadcast([P, P]),
                                   self.g.t["ident"][0:P, 0:P])
            ins.then_inc(self.key_rows, 1)
        for i in range(G):
            pe.wait_ge(self.same_ready, s * G + (i + 2))
            pe.wait_ge(self.msg_ready, s * G + (i + 1))
            pe.wait_ge(self.sums_out, s * G + (i + 1))
            for k in range(GK):
                t = i * GK + k
                ins = pe.matmul(self.sum_ps[:, k * W:(k + 1) * W], self.same[:, t, :], self.msg[:, t, :],
                                start=True, stop=True)
            ins.then_inc(self.summed, 1)

    def sums_to_sbuf(self, act, s):
        for i in range(G):
            act.wait_ge(self.summed, s * G + (i + 2))
            act.wait_ge(self.rows_out, s + 1)
            act.copy(self.tile_sums[:, i * GK:(i + 1) * GK, :].rearrange("p k w -> p (k w)"),
                     self.sum_ps[:, 0:GK * W]).then_inc(self.sums_out, 1)

    def release(self, pool, s):
        if s is not None:
            for u in range(TABLES):
                pool.wait_ge(self.scattered[u], self.base + 16 * (s * (K // TABLES)))
        pool.sem_inc(self.rows_out, 1)

    def scatter(self, pool, s):
        for k in range(K):
            u = k % TABLES
            pool.wait_ge(self.sums_out, s * G + (k // GK + 2))
            pool.wait_ge(self.once_staged, s + 1)
            if k >= TABLES:
                pool.wait_ge(self.scattered[u], self.base + 16 * (s * (K // TABLES) + k // TABLES))
            pool.sem_inc(self.tick, 1)
            pool.indirect_dma_start(out=self.g.sums[u][:, :],
                                    out_offset=bass.IndirectOffsetOnAxis(ap=self.once_slot[:, k:k + 1], axis=0),
                                    in_=self.tile_sums[:, k, :], in_offset=None, compute_op=ALU.add)\
                .then_inc(self.scattered[u], 16)

    def give_ahead(self, eng, who):
        if who == "dve":
            eng.sem_inc(self.same_ready, 1)
        if who == "act":
            eng.sem_inc(self.sums_out, 1)
        if who == "pe":
            eng.sem_inc(self.summed, 1)


class Gather:

    def __init__(self, g, ph, name, table, key, arrived=0):
        self.table, self.key_i = table, g.t[key + "_i"]
        self.slot = ph.enter_context(g.sbuf(name + "_slot", [P, K], I32))
        self.got = ph.enter_context(g.sbuf(name + "_got", [P, K, C], F32))
        self.staged = g.sem(ph, name + "_staged")
        self.used = g.sem(ph, name + "_used")
        self.tick = g.sem(ph, name + "_tick")
        self.arrived, self.base = g.arrived[arrived], g.arrived_so_far[arrived]
        g.arrived_so_far[arrived] += 16 * GK * g.S

    def stage(self, dve, s):
        dve.tensor_copy(self.slot[:], self.key_i[:, bass.ds(s, 1), :].rearrange("p o k -> p (o k)"))\
            .then_inc(self.staged, 1)

    def gather(self, pool, s):
        for k in range(K):
            if k % GK == 0:
                pool.wait_ge(self.staged, s + 1)
                pool.wait_ge(self.used, s * G + 1)
                pool.sem_inc(self.tick, 1)
            pool.indirect_dma_start(out=self.got[:, k, :], out_offset=None, in_=self.table[:, :],
                                    in_offset=bass.IndirectOffsetOnAxis(ap=self.slot[:, k:k + 1], axis=0))\
                .then_inc(self.arrived[k // GK], 16)


def edges_l0(g):
    nc, S = g.nc, g.S
    t = g.t
    ea_dram = g.ins["edge_attr_64"].rearrange("(s p k) c -> s p k c", p=P, k=K)
    ts_dram = g.ins["edge_weight"].rearrange("(s n) -> s n", n=P * K)
    D = ea_dram.shape[3]
    with ExitStack() as ph:
        sb = lambda name, shape: ph.enter_context(g.sbuf(name, shape, F32))
        ps = lambda name: ph.enter_context(g.psum(name, [C, 512], F32))
        sc = Scatter(g, ph, "dst")
        ga = Gather(g, ph, "xa", g.xa, "src")
        ea = sb("ea", [P, K, D])
        ts = sb("ts", [1, P * K])
        eaT = sb("eaT", [D, K, P])
        h1T = sb("h1T", [C, K, P])
        gateT = sb("gateT", [C, K, P])
        efT = sb("efT", [C, K, P])
        ea_ps, h1_ps, ts_ps, ef_ps, pre_ps = ps("ea_ps"), ps("h1_ps"), ps("ts_ps"), ps("ef_ps"), ps("pre_ps")
        sem = lambda name: g.sem(ph, name)
        ea_in, ea_turned, eaT_out = sem("ea_in"), sem("ea_turned"), sem("eaT_out")
        ts_in, ts_spread, gate_out = sem("ts_in"), sem("ts_spread"), sem("gate_out")
        h1_ready, h1_out, ef_ready, ef_out = sem("h1_ready"), sem("h1_out"), sem("ef_ready"), sem("ef_out")
        pre_ready, added, tick = sem("pre_ready"), sem("added"), sem("pe_tick")
        block = ph.enter_context(nc.Block())
        ts_tiles = ts[:].rearrange("o (p k) -> o k p", k=K)

        @block.sync
        def _(sp):
            with sp.Fori(0, S) as s:
                sp.wait_ge(ea_turned, s * G + 1)
                sp.dma_start(ea[:], ea_dram[bass.ds(s, 1)].rearrange("o p k c -> p (o k) c")).then_inc(ea_in, 16)
                sp.wait_ge(ts_spread, s * G + 1)
                sp.dma_start(ts[:], ts_dram[bass.ds(s, 1), :]).then_inc(ts_in, 16)

        @block.tensor
        def _(pe):
            pe.sem_inc(ea_turned, 1)
            pe.sem_inc(ts_spread, 1)
            sc.give_ahead(pe, "pe")
            with pe.Fori(0, S) as s:
                for i in range(G):
                    pe.wait_ge(ea_in, 16 * s + 16)
                    pe.wait_ge(eaT_out, s * G + (i + 1))
                    pe.sem_inc(tick, 1)
                    for k in range(GK):
                        ins = pe.transpose(ea_ps[0:D, k * P:(k + 1) * P], ea[:, i * GK + k, :], t["ident"][0:P, 0:P])
                    ins.then_inc(ea_turned, 1)
                    pe.wait_ge(ts_in, 16 * s + 16)
                    pe.wait_ge(gate_out, s * G + (i + 1))
                    pe.matmul(ts_ps[:, 0:GK * P], t["Wt_row"][:], ts_tiles[:, i * GK:(i + 1) * GK, :],
                              start=True, stop=True).then_inc(ts_spread, 1)
                for i in range(G):
                    pe.wait_ge(eaT_out, s * G + (i + 2))
                    pe.wait_ge(h1_out, s * G + (i + 1))
                    pe.matmul(h1_ps[:, 0:GK * P], t["L0_gnn_We1"][:],
                              eaT[:, i * GK:(i + 1) * GK, :].rearrange("c k p -> c (k p)"),
                              start=True, stop=True).then_inc(h1_ready, 1)
                for i in range(G):
                    pe.wait_ge(h1_out, s * G + (i + 2))
                    pe.wait_ge(ef_out, s * G + (i + 1))
                    pe.matmul(ef_ps[:, 0:GK * P], t["L0_gnn_We2"][:],
                              h1T[:, i * GK:(i + 1) * GK, :].rearrange("c k p -> c (k p)"),
                              start=True, stop=True).then_inc(ef_ready, 1)
                for i in range(G):
                    pe.wait_ge(ef_out, s * G + (i + 2))
                    pe.wait_ge(added, s * G + (i + 1))
                    for k in range(GK):
                        ins = pe.matmul(pre_ps[0:P, k * C:(k + 1) * C], efT[:, i * GK + k, :], t["Wn1_edge"][:],
                                        start=True, stop=True)
                    ins.then_inc(pre_ready, 1)
                sc.key_rows_and_sums(pe, s)

        @block.scalar
        def _(act):
            for x in (eaT_out, gate_out, h1_out):
                act.sem_inc(x, 1)
            sc.give_ahead(act, "act")
            with act.Fori(0, S) as s:
                for i in range(G):
                    at = slice(i * GK, (i + 1) * GK)
                    act.wait_ge(ea_turned, s * G + (i + 2))
                    act.copy(eaT[:, at, :].rearrange("c k p -> c (k p)"), ea_ps[0:D, 0:GK * P]).then_inc(eaT_out, 1)
                    act.wait_ge(ts_spread, s * G + (i + 2))
                    act.activation(gateT[:, at, :].rearrange("c k p -> c (k p)"), ts_ps[:, 0:GK * P], ACT.Sigmoid,
                                   bias=t["L0_gnn_bt"][:, 0:1]).then_inc(gate_out, 1)
                for i in range(G):
                    act.wait_ge(h1_ready, s * G + (i + 1))
                    act.activation(h1T[:, i * GK:(i + 1) * GK, :].rearrange("c k p -> c (k p)"), h1_ps[:, 0:GK * P],
                                   ACT.Relu, bias=t["L0_gnn_be1"][:, 0:1]).then_inc(h1_out, 1)
                for i in range(G):
                    at = slice(i * GK, (i + 1) * GK)
                    act.wait_ge(added, s * G + (i + 2))
                    act.activation(sc.msg[:, at, 0:C], ga.got[:, at, :], ACT.Relu).then_inc(sc.msg_ready, 1)
                    act.wait_ge(sc.msg_ready, s * G + (i + 1))
                    act.sem_inc(ga.used, 1)
                sc.sums_to_sbuf(act, s)

        @block.vector
        def _(dve):
            dve.sem_inc(ef_out, 1)
            dve.sem_inc(added, 1)
            dve.memset(sc.msg[:, :, C:W], 1.0)
            sc.give_ahead(dve, "dve")
            ga.stage(dve, 0)
            with dve.Fori(0, S) as s:
                sc.stage_keys(dve, s)
                for i in range(G):
                    at = slice(i * GK, (i + 1) * GK)
                    dve.wait_ge(ef_ready, s * G + (i + 1))
                    dve.wait_ge(gate_out, s * G + (i + 2))
                    dve.scalar_tensor_tensor(out=efT[:, at, :].rearrange("c k p -> c (k p)"), in0=ef_ps[:, 0:GK * P],
                                             scalar=t["L0_gnn_be2"][:, 0:1],
                                             in1=gateT[:, at, :].rearrange("c k p -> c (k p)"),
                                             op0=ALU.add, op1=ALU.mult).then_inc(ef_out, 1)
                for i in range(G):
                    at = slice(i * GK, (i + 1) * GK)
                    dve.wait_ge(pre_ready, s * G + (i + 1))
                    dve.wait_ge(ga.arrived[i], 16 * GK * s + (ga.base + 16 * GK))
                    dve.tensor_tensor(ga.got[:, at, :].rearrange("p k c -> p (k c)"), pre_ps[0:P, 0:GK * C],
                                      ga.got[:, at, :].rearrange("p k c -> p (k c)"), ALU.add).then_inc(added, 1)
                sc.compare(dve, s)
                ga.stage(dve, s + 1)
                sc.stage_once(dve, s)

        @block.gpsimd
        def _(pool):
            pool.sem_inc(ga.used, 1)
            sc.release(pool, None)
            ga.gather(pool, 0)
            ga.gather(pool, 1)
            sc.scatter(pool, 0)
            with pool.Fori(1, S - 1) as s:
                ga.gather(pool, s + 1)
                sc.release(pool, s)
                sc.scatter(pool, s)
            sc.release(pool, S - 1)
            sc.scatter(pool, S - 1)
            for u in range(TABLES):
                pool.wait_ge(sc.scattered[u], sc.base + 16 * S * (K // TABLES))
    g.clear_semaphores()


def edges_l1_scores(g):
    nc, S, t = g.nc, g.S, g.t
    len_dram = g.ins["edge_weight1"].rearrange("(s n) o -> s (n o)", n=P * K)
    with ExitStack() as ph:
        sb = lambda name, shape: ph.enter_context(g.sbuf(name, shape, F32))
        gq = Gather(g, ph, "q", g.q, "src")
        gk = Gather(g, ph, "k", g.k, "dst", arrived=1)
        row = sb("len_row", [1, P * K])
        hidT = sb("hidT", [C, K, P])
        dots = sb("dots", [P, K, H])
        len_ps = ph.enter_context(g.psum("len_ps", [C, 512], F32))
        bias_ps = ph.enter_context(g.psum("bias_ps", [P, GK, H], F32))
        sem = lambda name: g.sem(ph, name)
        row_in, spread, hid_out = sem("row_in"), sem("spread"), sem("hid_out")
        bias_ready, chain, scored = sem("bias_ready"), sem("chain"), sem("scored")
        block = ph.enter_context(nc.Block())
        row_tiles = row[:].rearrange("o (p k) -> o k p", k=K)

        @block.sync
        def _(sp):
            with sp.Fori(0, S) as s:
                sp.wait_ge(spread, s * G + 1)
                sp.dma_start(row[:], len_dram[bass.ds(s, 1), :]).then_inc(row_in, 16)

        @block.tensor
        def _(pe):
            pe.sem_inc(spread, 1)
            with pe.Fori(0, S) as s:
                for i in range(G):
                    pe.wait_ge(row_in, 16 * s + 16)
                    pe.wait_ge(hid_out, s * G + (i + 1))
                    pe.matmul(len_ps[:, 0:GK * P], t["We1_row"][:], row_tiles[:, i * GK:(i + 1) * GK, :],
                              start=True, stop=True).then_inc(spread, 1)
                for i in range(G):
                    pe.wait_ge(hid_out, s * G + (i + 2))
                    pe.wait_ge(scored, s * G + (i + 1))
                    for k in range(GK):
                        pe.matmul(bias_ps[:, k, :], hidT[:, i * GK + k, :], t["L1_gnn_We2_T"][:], start=True, stop=False)
                        ins = pe.matmul(bias_ps[:, k, :], t["ones"][0:1, 0:P], t["be2_row"][:], start=False, stop=True)
                    ins.then_inc(bias_ready, 1)

        @block.scalar
        def _(act):
            act.sem_inc(hid_out, 1)
            with act.Fori(0, S) as s:
                act.wait_ge(bias_ready, s * G + 1)
                for i in range(G):
                    act.wait_ge(spread, s * G + (i + 2))
                    act.activation(hidT[:, i * GK:(i + 1) * GK, :].rearrange("c k p -> c (k p)"), len_ps[:, 0:GK * P],
                                   ACT.Silu, bias=t["L1_gnn_be1"][:, 0:1]).then_inc(hid_out, 1)

        @block.vector
        def _(dve):
            dve.sem_inc(scored, 1)
            dve.sem_inc(bias_ready, 1)
            gq.stage(dve, 0)
            gk.stage(dve, 0)
            with dve.Fori(0, S) as s:
                for i in range(G):
                    at = slice(i * GK, (i + 1) * GK)
                    step = s * (4 * G) + 4 * i
                    dve.wait_ge(gq.arrived[i], 16 * GK * s + (gq.base + 16 * GK))
                    dve.wait_ge(gk.arrived[i], 16 * GK * s + (gk.base + 16 * GK))
                    dve.tensor_tensor(gq.got[:, at, :], gq.got[:, at, :], gk.got[:, at, :], ALU.mult).then_inc(chain, 1)
                    dve.wait_ge(chain, step + 1)
                    dve.tensor_reduce(dots[:, at, :].rearrange("p k h -> p (k h)"),
                                      gq.got[:, at, :].rearrange("p k (h d) -> p (k h) d", h=H), AX, ALU.add)\
                        .then_inc(chain, 1)
                    dve.wait_ge(chain, step + 2)
                    dve.sem_inc(gq.used, 1)
                    dve.sem_inc(gk.used, 1)
                    dve.wait_ge(bias_ready, s * G + (i + 2))
                    dve.scalar_tensor_tensor(out=dots[:, at, :], in0=dots[:, at, :], scalar=float((C // H) ** -0.5),
                                             in1=bias_ps[:], op0=ALU.mult, op1=ALU.add).then_inc(chain, 1)
                    dve.wait_ge(chain, step + 3)
                    dve.sem_inc(scored, 1)
                    dve.tensor_tensor(g.scores[:, bass.ds(s * K + i * GK, GK), :], dots[:, at, :],
                                      bcast(g.cut[:, bass.ds(s * K + i * GK, GK)], H), ALU.mult).then_inc(chain, 1)
                    dve.wait_ge(chain, step + 4)
                nxt = s + 1
                gq.stage(dve, nxt)
                gk.stage(dve, nxt)

        @block.gpsimd
        def _(pool):
            pool.sem_inc(gq.used, 1)
            pool.sem_inc(gk.used, 1)
            with pool.Fori(0, S) as s:
                gq.gather(pool, s)
                gk.gather(pool, s)
            for i in range(G):
                pool.wait_ge(gq.arrived[i], gq.base + 16 * GK * S)
                pool.wait_ge(gk.arrived[i], gk.base + 16 * GK * S)
    g.clear_semaphores()


def cutoff(g):
    nc, S = g.nc, g.S
    with ExitStack() as ph:
        sb = lambda name: ph.enter_context(g.sbuf(name, [P, S * K], F32))
        length, folded, inside = sb("length"), sb("folded"), sb("inside")
        periods = ph.enter_context(g.sbuf("periods", [P, S * K], I32))
        loaded, chain = g.sem(ph, "len_loaded"), g.sem(ph, "cut_chain")
        folded_ready, sin_ready, bias_set = g.sem(ph, "folded_ready"), g.sem(ph, "sin_ready"), g.sem(ph, "bias_set")
        block = ph.enter_context(nc.Block())
        per = 2.0 * CUTOFF

        @block.sync
        def _(sp):
            sp.dma_start(length[:].rearrange("p (s k) -> p s k", k=K),
                         g.ins["edge_weight1"].rearrange("(s p k) o -> p s (k o)", p=P, k=K)).then_inc(loaded, 16)

        @block.vector
        def _(dve):
            link = Chain(dve, chain)
            dve.wait_ge(loaded, 16)
            link(dve.tensor_scalar(inside[:], length[:], CUTOFF, 0.5, ALU.is_lt, ALU.mult))
            link(dve.tensor_scalar(folded[:], length[:], 1.0 / per, None, ALU.mult))
            link(dve.tensor_copy(periods[:], folded[:]))
            link(dve.tensor_copy(folded[:], periods[:]))
            link(dve.scalar_tensor_tensor(out=length[:], in0=folded[:], scalar=-per, in1=length[:],
                                          op0=ALU.mult, op1=ALU.add))
            link(dve.tensor_scalar(folded[:], length[:], -1.0, None, ALU.mult))
            link(dve.tensor_tensor(folded[:], folded[:], length[:], ALU.max))
            link(dve.tensor_scalar(folded[:], folded[:], -CUTOFF, None, ALU.add))
            link(dve.tensor_scalar(length[:], folded[:], -1.0, None, ALU.mult))
            link(dve.tensor_tensor(folded[:], folded[:], length[:], ALU.max))
            dve.tensor_scalar(folded[:], folded[:], float(np.pi / CUTOFF), float(-np.pi / 2), ALU.mult, ALU.add)\
                .then_inc(folded_ready, 1)
            dve.wait_ge(sin_ready, 1)
            link(dve.tensor_scalar(folded[:], folded[:], 1.0, None, ALU.add))
            link(dve.tensor_tensor(g.cut[:], folded[:], inside[:], ALU.mult))

        @block.scalar
        def _(act):
            act.wait_ge(folded_ready, 1)
            act.activation(folded[:], folded[:], ACT.Sin).then_inc(sin_ready, 1)


def head_maximum(g):
    nc = g.nc
    with ExitStack() as ph:
        m = ph.enter_context(g.sbuf("m", [P, H], F32))
        mT = ph.enter_context(g.sbuf("mT", [H, 1], F32))
        diag = ph.enter_context(g.sbuf("diag", [H, H], F32))
        ps = ph.enter_context(g.psum("max_ps", [P, 2, 512], F32))
        dve_step, pe_step = g.sem(ph, "max_dve"), g.sem(ph, "max_pe")
        block = ph.enter_context(nc.Block())

        @block.vector
        def _(dve):
            dve.tensor_reduce(m[:], g.scores[:].rearrange("p t h -> p h t"), AX, ALU.max).then_inc(dve_step, 1)
            dve.wait_ge(pe_step, 1)
            dve.tensor_reduce(mT[:], ps[0:H, 0, 0:P], AX, ALU.max).then_inc(dve_step, 1)
            dve.wait_ge(dve_step, 2)
            dve.tensor_scalar(diag[:], g.t["ident"][0:H, 0:H], mT[:, 0:1], None, ALU.mult).then_inc(dve_step, 1)
            dve.wait_ge(pe_step, 2)
            dve.tensor_copy(g.top[:], ps[:, 1, 0:H]).then_inc(dve_step, 1)
            dve.wait_ge(dve_step, 4)

        @block.tensor
        def _(pe):
            pe.wait_ge(dve_step, 1)
            pe.transpose(ps[0:H, 0, 0:P], m[:], g.t["ident"][0:P, 0:P]).then_inc(pe_step, 1)
            pe.wait_ge(dve_step, 3)
            pe.matmul(ps[:, 1, 0:H], g.t["ones"][0:H, 0:P], diag[:], start=True, stop=True).then_inc(pe_step, 1)


def edges_simple(g, table, key_from, key_to, weighted):
    nc, S, t = g.nc, g.S, g.t
    with ExitStack() as ph:
        sc = Scatter(g, ph, key_to)
        ga = Gather(g, ph, "row", table, key_from)
        chain, exp_in, exp_out = g.sem(ph, "chain"), g.sem(ph, "exp_in"), g.sem(ph, "exp_out")
        below = ph.enter_context(g.sbuf("below", [P, K, H], F32))
        expd = ph.enter_context(g.sbuf("expd", [P, K, H], F32))
        block = ph.enter_context(nc.Block())

        @block.tensor
        def _(pe):
            sc.give_ahead(pe, "pe")
            with pe.Fori(0, S) as s:
                sc.key_rows_and_sums(pe, s)

        @block.scalar
        def _(act):
            sc.give_ahead(act, "act")
            with act.Fori(0, S) as s:
                if weighted:
                    act.wait_ge(exp_in, s + 1)
                    act.activation(expd[:], below[:], ACT.Exp).then_inc(exp_out, 1)
                sc.sums_to_sbuf(act, s)

        @block.vector
        def _(dve):
            if not weighted:
                dve.memset(sc.msg[:, :, C:W], 0.0)
            sc.give_ahead(dve, "dve")
            ga.stage(dve, 0)
            with dve.Fori(0, S) as s:
                sc.stage_keys(dve, s)
                if weighted:
                    dve.tensor_tensor(below[:], g.scores[:, bass.ds(s * K, K), :], rows(g.top[:], K), ALU.subtract)\
                        .then_inc(exp_in, 1)
                    dve.wait_ge(exp_out, s + 1)
                    dve.tensor_copy(sc.msg[:, :, C:W], expd[:]).then_inc(chain, 1)
                for i in range(G):
                    at = slice(i * GK, (i + 1) * GK)
                    dve.wait_ge(ga.arrived[i], 16 * GK * s + (ga.base + 16 * GK))
                    if weighted:
                        dve.wait_ge(chain, s + 1)
                        ins = dve.tensor_tensor(
                            sc.msg[:, at, 0:C].rearrange("p k (h d) -> p k h d", h=H),
                            ga.got[:, at, :].rearrange("p k (h d) -> p k h d", h=H),
                            expd[:, at, :].unsqueeze(3).to_broadcast([P, GK, H, C // H]), ALU.mult)
                    else:
                        ins = dve.tensor_copy(sc.msg[:, at, 0:C], ga.got[:, at, :])
                    ins.then_inc(sc.msg_ready, 1)
                    dve.wait_ge(sc.msg_ready, s * G + (i + 1))
                    dve.sem_inc(ga.used, 1)
                sc.compare(dve, s)
                ga.stage(dve, s + 1)
                sc.stage_once(dve, s)

        @block.gpsimd
        def _(pool):
            pool.sem_inc(ga.used, 1)
            sc.release(pool, None)
            ga.gather(pool, 0)
            ga.gather(pool, 1)
            sc.scatter(pool, 0)
            with pool.Fori(1, S - 1) as s:
                ga.gather(pool, s + 1)
                sc.release(pool, s)
                sc.scatter(pool, s)
            sc.release(pool, S - 1)
            sc.scatter(pool, S - 1)
            for u in range(TABLES):
                pool.wait_ge(sc.scattered[u], sc.base + 16 * S * (K // TABLES))
    g.clear_semaphores()


def on_vector(g, steps):
    with ExitStack() as ph:
        done = g.sem(ph, "step_done")
        block = ph.enter_context(g.nc.Block())

        @block.vector
        def _(dve):
            for n, (who, f) in enumerate(steps):
                if who == "dve":
                    if n:
                        dve.wait_ge(done, n)
                    f(dve).then_inc(done, 1)
            dve.wait_ge(done, len(steps))

        @block.scalar
        def _(act):
            for n, (who, f) in enumerate(steps):
                if who == "act":
                    if n:
                        act.wait_ge(done, n)
                    f(act).then_inc(done, 1)


def gnn(nc, ins, out):
    g = Gnn(nc, ins, out)
    N, NB, S = g.N, g.NB, g.S
    table = lambda name, n, w: nc.dram_tensor(name, (n, w), F32, kind="Internal").ap()
    g.xa, g.q, g.k, g.v = (table(n + "_table", N, C) for n in ("xa", "q", "k", "v"))
    g.x2, g.h3 = table("x2_table", N, C), table("h3_table", N, C)
    g.sums = [table(f"sums_table{u}", N + P, W) for u in range(TABLES)]
    with ExitStack() as ctx:
        g.scattered = [ctx.enter_context(nc.semaphore(f"scattered{u}")) for u in range(TABLES)]
        g.arrived = [[ctx.enter_context(nc.semaphore(f"arrived{w}{i}")) for i in range(G)] for w in range(2)]
        g.scattered_so_far, g.arrived_so_far = 0, [0, 0]
        load_and_lay_out(g, ctx)
        g.clear_semaphores()
        t = g.t
        x = t["x_sb"]
        sb = lambda c, name, shape: c.enter_context(g.sbuf(name, shape, F32))
        count = sb(ctx, "count", [P, NB])
        dinv = sb(ctx, "dinv", [P, NB])
        with ExitStack() as ph:
            xa = sb(ph, "xa_sb", [P, NB, C])
            node_linear(g, "xa", x, [(t["Wn1_node"], t["L0_gnn_bn1"], xa)])
            to_table(g, [(g.xa, xa)])
            clear_tables(g)
        mark_duplicates(g)
        edges_l0(g)
        with ExitStack() as ph:
            total = sb(ph, "total", [P, NB, W])
            part = [sb(ph, f"part{i}", [P, NB, W]) for i in range(2)]
            hid = sb(ph, "hid", [P, NB, C])
            scr = sb(ph, "scr", [P, NB, C])
            collect_sums(g, total, part)
            on_vector(g, [
                ("dve", lambda e: e.tensor_copy(count[:], total[:, :, C:C + 1].rearrange("p j o -> p (j o)"))),
                ("dve", lambda e: e.tensor_copy(hid[:], total[:, :, 0:C])),
                ("dve", lambda e: e.tensor_tensor(scr[:], bcast(count[:], C), rows(t["L0_gnn_bn2"][:], NB), ALU.mult)),
                ("dve", lambda e: e.tensor_tensor(scr[:], scr[:], x[:], ALU.add)),
                ("dve", lambda e: e.tensor_tensor(scr[:], scr[:], x[:], ALU.add)),
            ])
            node_linear(g, "l0", hid, [(t["L0_gnn_Wn2"], scr, scr)])
            layer_norm(g, scr, hid, dst=x)
        g.clear_semaphores()
        with ExitStack() as lay:
            g.scores = sb(lay, "scores", [P, S * K, H])
            g.top = sb(lay, "top", [P, H])
            with ExitStack() as ph:
                qkv = [sb(ph, n, [P, NB, C]) for n in ("q_sb", "k_sb", "v_sb")]
                node_linear(g, "qkv", x, [(t[f"L1_gnn_W{n}_T"], t[f"L1_gnn_b{n}"], o) for n, o in zip("qkv", qkv)])
                to_table(g, list(zip((g.q, g.k, g.v), qkv)))
                clear_tables(g)
            with ExitStack() as ph:
                g.cut = sb(ph, "cut", [P, S * K])
                cutoff(g)
                g.clear_semaphores()
                edges_l1_scores(g)
            head_maximum(g)
            edges_simple(g, g.v, "dst", "src", weighted=True)
        with ExitStack() as ph:
            total = sb(ph, "total", [P, NB, W])
            part = [sb(ph, f"part{i}", [P, NB, W]) for i in range(2)]
            hid = sb(ph, "hid", [P, NB, C])
            scr = sb(ph, "scr", [P, NB, C])
            den = sb(ph, "den", [P, NB, H])
            collect_sums(g, total, part)
            on_vector(g, [
                ("dve", lambda e: e.tensor_scalar(den[:], total[:, :, C:W], 1e-8, None, ALU.add)),
                ("dve", lambda e: e.reciprocal(den[:], den[:])),
                ("dve", lambda e: e.tensor_tensor(hid[:].rearrange("p j (h d) -> p j h d", h=H),
                                                  total[:, :, 0:C].rearrange("p j (h d) -> p j h d", h=H),
                                                  den[:].unsqueeze(3).to_broadcast([P, NB, H, C // H]), ALU.mult)),
                ("dve", lambda e: e.tensor_tensor(scr[:], x[:], rows(t["L1_gnn_bo"][:], NB), ALU.add)),
            ])
            node_linear(g, "l1", hid, [(t["L1_gnn_Wo_T"], scr, scr)])
            layer_norm(g, scr, hid, scale=t["L1_gnn_ln_g"], shift=t["L1_gnn_ln_b"])
            on_vector(g, [("dve", lambda e: e.tensor_tensor(scr[:], scr[:], x[:], ALU.add))])
            layer_norm(g, scr, hid, dst=x)
        to_table(g, [(g.x2, x)])
        clear_tables(g)
        g.clear_semaphores()
        edges_simple(g, g.x2, "src", "dst", weighted=False)
        with ExitStack() as ph:
            total = sb(ph, "total", [P, NB, W])
            part = [sb(ph, f"part{i}", [P, NB, W]) for i in range(2)]
            hid = sb(ph, "hid", [P, NB, C])
            scr = sb(ph, "scr", [P, NB, C])
            per = sb(ph, "per", [P, NB])
            collect_sums(g, total, part)
            on_vector(g, [
                ("dve", lambda e: e.tensor_scalar(per[:], count[:], 1.0, None, ALU.max)),
                ("dve", lambda e: e.reciprocal(per[:], per[:])),
                ("dve", lambda e: e.tensor_tensor(hid[:], total[:, :, 0:C], bcast(per[:], C), ALU.mult)),
                ("dve", lambda e: e.tensor_tensor(scr[:], x[:], rows(t["b_l2"][:], NB), ALU.add)),
                ("dve", lambda e: e.tensor_scalar(dinv[:], count[:], 1.0, None, ALU.add)),
                ("act", lambda e: e.activation(dinv[:], dinv[:], ACT.Sqrt)),
                ("dve", lambda e: e.reciprocal(dinv[:], dinv[:])),
            ])
            node_linear(g, "l2n", hid, [(t["L2_gnn_w_neigh_T"], scr, scr)])
            node_linear(g, "l2s", x, [(t["L2_gnn_w_self_T"], scr, scr)])
            layer_norm(g, scr, hid, dst=x)
        with ExitStack() as lay:
            h3 = sb(lay, "h3_sb", [P, NB, C])
            zero_row = sb(lay, "zero_row", [P, C])
            on_vector(g, [("dve", lambda e: e.memset(zero_row[:], 0.0))])
            node_linear(g, "h3", x, [(t["L3_gnn_W"], zero_row, h3)])
            on_vector(g, [("dve", lambda e: e.tensor_tensor(h3[:], h3[:], bcast(dinv[:], C), ALU.mult))])
            to_table(g, [(g.h3, h3)])
            clear_tables(g)
            g.clear_semaphores()
            edges_simple(g, g.h3, "src", "dst", weighted=False)
            total = sb(lay, "total", [P, NB, W])
            part = [sb(lay, f"part{i}", [P, NB, W]) for i in range(2)]
            hid = sb(lay, "hid", [P, NB, C])
            scr = sb(lay, "scr", [P, NB, C])
            collect_sums(g, total, part)
            on_vector(g, [
                ("dve", lambda e: e.tensor_tensor(scr[:], total[:, :, 0:C], h3[:], ALU.add)),
                ("dve", lambda e: e.tensor_tensor(scr[:], scr[:], bcast(dinv[:], C), ALU.mult)),
                ("dve", lambda e: e.tensor_tensor(scr[:], scr[:], rows(t["L3_gnn_b"][:], NB), ALU.add)),
                ("dve", lambda e: e.tensor_scalar(hid[:], scr[:], 20.0, None, ALU.min)),
                ("act", lambda e: e.activation(hid[:], hid[:], ACT.Exp)),
                ("dve", lambda e: e.scalar_tensor_tensor(out=hid[:], in0=hid[:], scalar=2.0, in1=hid[:],
                                                         op0=ALU.add, op1=ALU.mult)),
                ("dve", lambda e: e.tensor_tensor(scr[:], scr[:], hid[:], ALU.mult)),
                ("dve", lambda e: e.tensor_scalar(hid[:], hid[:], 2.0, None, ALU.add)),
                ("dve", lambda e: e.reciprocal(hid[:], hid[:])),
                ("dve", lambda e: e.tensor_tensor(scr[:], scr[:], hid[:], ALU.mult)),
                ("dve", lambda e: e.tensor_tensor(scr[:], scr[:], x[:], ALU.add)),
            ])
            layer_norm(g, scr, hid, dst=x)
        to_table(g, [(g.out, x)])


_INS = ["x", "src", "dst", "edge_attr_64", "edge_weight", "edge_weight1",
        "L0_gnn_We1", "L0_gnn_be1", "L0_gnn_We2", "L0_gnn_be2", "L0_gnn_Wt", "L0_gnn_bt",
        "L0_gnn_Wn1", "L0_gnn_bn1", "L0_gnn_Wn2", "L0_gnn_bn2",
        "L1_gnn_Wq", "L1_gnn_bq", "L1_gnn_Wk", "L1_gnn_bk", "L1_gnn_Wv", "L1_gnn_bv",
        "L1_gnn_We1", "L1_gnn_be1", "L1_gnn_We2", "L1_gnn_be2", "L1_gnn_Wo", "L1_gnn_bo",
        "L1_gnn_ln_g", "L1_gnn_ln_b", "L2_gnn_w_self", "L2_gnn_b_self", "L2_gnn_w_neigh",
        "L2_gnn_b_neigh", "L3_gnn_W", "L3_gnn_b"]


def kernel(**inputs):
    import numpy as _np
    import concourse.bacc as _bacc
    from concourse import mybir as _mybir
    from concourse.bass_utils import run_bass_kernel_spmd as _run

    nc = _bacc.Bacc("TRN2", target_bir_lowering=False, num_devices=1)
    arrays, args = {}, {}
    for name in _INS:
        a = _np.ascontiguousarray(inputs[name])
        arrays[f"in_{name}_dram"] = a
        args[name] = nc.dram_tensor(f"in_{name}_dram", a.shape, _mybir.dt.from_np(a.dtype), kind="ExternalInput").ap()
    out = nc.dram_tensor("out_dram", inputs["x"].shape, _mybir.dt.float32, kind="ExternalOutput").ap()
    gnn(nc, args, out)
    r = _run(nc, [arrays], core_ids=[0])
    return r.results[0]["out_dram"]
```

```python
from contextlib import ExitStack

import numpy as np

import concourse.bass as bass
from concourse import mybir

F32 = mybir.dt.float32
BF16 = mybir.dt.bfloat16
F16 = mybir.dt.float16
I32 = mybir.dt.int32
ALU = mybir.AluOpType
ACT = mybir.ActivationFunctionType
AX = mybir.AxisListType.X

P = 125
K = 15
GK = 3
G = K // GK
C = 128
H = 8
W = C + H
TABLES = 5
R = 64
HALF = (13, 12)
FLAG_STEP = 9
LN_EPS = 1e-5
CUTOFF = 5.0


def bcast(ap, n):
    return ap.unsqueeze(2).to_broadcast([ap.shape[0], ap.shape[1], n])


def rows(ap, a):
    return ap.unsqueeze(1).to_broadcast([ap.shape[0], a, ap.shape[1]])


class Gnn:

    def __init__(self, nc, ins, out):
        self.nc, self.ins, self.out = nc, ins, out
        self.N = ins["x"].shape[0]
        self.E = ins["src"].shape[0]
        self.NB = self.N // P
        self.S = self.E // (P * K)
        assert self.N == P * self.NB and self.E == P * K * self.S
        self.used, self.names = [], {}

    def unique(self, name):
        self.names[name] = self.names.get(name, 0) + 1
        return name if self.names[name] == 1 else f"{name}_{self.names[name]}"

    def sbuf(self, name, shape, dt):
        return self.nc.sbuf_tensor(self.unique(name), shape, dt)

    def psum(self, name, shape, dt):
        return self.nc.psum_tensor(self.unique(name), shape, dt)

    def sem(self, ctx, name):
        s = ctx.enter_context(self.nc.semaphore(name))
        self.used.append(s)
        return s

    def clear_semaphores(self):
        used, self.used = self.used, []
        with self.nc.Block() as block:
            @block.gpsimd
            def _(pool):
                for s in used:
                    pool.sem_clear(s)


def load_and_lay_out(g, ctx):
    nc, ins, NB, S, N = g.nc, g.ins, g.NB, g.S, g.N

    def sb(name, shape, dt=F32):
        t = ctx.enter_context(g.sbuf(name, shape, dt))
        tensors[name] = t
        return t

    tensors = {}
    g.t = tensors
    loads = []
    for name in ("L0_gnn_We1", "L0_gnn_We2", "L0_gnn_Wn2", "L3_gnn_W"):
        loads.append((sb(name, list(ins[name].shape))[:], ins[name]))
    wn1 = ins["L0_gnn_Wn1"]
    loads.append((sb("Wn1_node", [C, C])[:], wn1[0:C, :]))
    loads.append((sb("Wn1_edge", [C, C])[:], wn1[C:2 * C, :]))
    turned = {"L1_gnn_Wq": C, "L1_gnn_Wk": C, "L1_gnn_Wv": C, "L1_gnn_Wo": C,
              "L2_gnn_w_self": C, "L2_gnn_w_neigh": C, "L1_gnn_We2": H}
    for name, n in turned.items():
        loads.append((sb(name, [n, C])[:], ins[name]))
        sb(name + "_T", [C, n])
    for name in ("L0_gnn_be1", "L0_gnn_be2", "L0_gnn_bt", "L1_gnn_be1"):
        loads.append((sb(name, [C, 1])[:], ins[name].rearrange("(p o) -> p o", o=1)))
    for name in ("L0_gnn_bn1", "L0_gnn_bn2", "L1_gnn_bq", "L1_gnn_bk", "L1_gnn_bv", "L1_gnn_bo",
                 "L1_gnn_ln_g", "L1_gnn_ln_b", "L2_gnn_b_self", "L2_gnn_b_neigh", "L3_gnn_b"):
        loads.append((sb(name, [P, C])[:], ins[name].partition_broadcast(P)))
    loads.append((sb("Wt_row", [1, C])[:], ins["L0_gnn_Wt"]))
    loads.append((sb("We1_row", [1, C])[:], ins["L1_gnn_We1"].rearrange("n o -> o n")))
    loads.append((sb("be2_row", [1, H])[:], ins["L1_gnn_be2"].rearrange("(o n) -> o n", o=1)))
    loads.append((sb("x_sb", [P, NB, C])[:], ins["x"].rearrange("(p j) c -> p j c", p=P)))
    for key in ("src", "dst"):
        loads.append((sb(key + "_i", [P, S + 1, K], I32)[:, 0:S, :],
                      ins[key].rearrange("(s p k) -> p s k", p=P, k=K)))
        sb(key + "_f", [P, S, K])
        sb(key + "_once", [P, S, K], I32)
    ident = sb("ident", [C, C])
    ones = sb("ones", [C, C])
    lower = sb("lower", [P, P])
    part_i = sb("part_i", [P, 1], I32)
    trash = sb("trash", [P, 1])
    b_l2 = sb("b_l2", [P, C])
    zeros = sb("zeros", [P, 26 * W])

    with ExitStack() as ph:
        loaded = g.sem(ph, "loaded")
        pool_ready = g.sem(ph, "pool_ready")
        pool_step = g.sem(ph, "pool_step")
        turned_ps = g.sem(ph, "turned_ps")
        dve_done = g.sem(ph, "dve_done")
        turn = ph.enter_context(g.psum("turn", [C, 8, 512], F32))
        block = ph.enter_context(nc.Block())

        @block.sync
        def _(sp):
            for to, of in loads:
                sp.dma_start(to, of).then_inc(loaded, 16)
            sp.wait_ge(loaded, 16 * len(loads))

        @block.gpsimd
        def _(pool):
            pool.memset(ident[:], 0.0).then_inc(pool_step, 1)
            pool.memset(ones[:], 1.0).then_inc(pool_step, 1)
            pool.memset(lower[:], 1.0).then_inc(pool_step, 1)
            pool.memset(zeros[:], 0.0).then_inc(pool_step, 1)
            pool.wait_ge(pool_step, 4)
            pool.affine_select(out=ident[:], in_=ident[:], compare_op=ALU.not_equal, fill=1.0, base=0,
                               pattern=[[-1, C]], channel_multiplier=1).then_inc(pool_ready, 1)
            pool.affine_select(out=lower[:], in_=lower[:], compare_op=ALU.is_gt, fill=0.0, base=0,
                               pattern=[[-1, P]], channel_multiplier=1).then_inc(pool_ready, 1)
            pool.iota(part_i[:], pattern=[[0, 1]], base=N, channel_multiplier=1).then_inc(pool_ready, 1)

        @block.tensor
        def _(pe):
            pe.wait_ge(loaded, 16 * len(loads))
            pe.wait_ge(pool_ready, 3)
            for i, (name, n) in enumerate(turned.items()):
                pe.transpose(turn[:, i, 0:n], g.t[name][:], ident[0:n, 0:n]).then_inc(turned_ps, 1)

        @block.vector
        def _(dve):
            for i, (name, n) in enumerate(turned.items()):
                dve.wait_ge(turned_ps, i + 1)
                dve.tensor_copy(g.t[name + "_T"][:], turn[:, i, 0:n])
            dve.tensor_tensor(b_l2[:], g.t["L2_gnn_b_self"][:], g.t["L2_gnn_b_neigh"][:], ALU.add)
            for key in ("src", "dst"):
                dve.memset(g.t[key + "_i"][:, S, :], 0)
                dve.tensor_copy(g.t[key + "_f"][:], g.t[key + "_i"][:, 0:S, :])
            dve.tensor_copy(trash[:], part_i[:]).then_inc(dve_done, 1)
            dve.wait_ge(dve_done, 1)


def mark_duplicates(g):
    nc, S, N = g.nc, g.S, g.N
    with ExitStack() as ph:
        key_slot = ph.enter_context(g.sbuf("key_slot", [P, K], F32))
        same = ph.enter_context(g.sbuf("same", [P, GK, P], F32))
        late = ph.enter_context(g.sbuf("late", [P, K], F32))
        shift = ph.enter_context(g.sbuf("shift", [P, K], F32))
        key_ps = ph.enter_context(g.psum("key_ps", [P, GK, 128], F32))
        for key in ("dst", "src"):
            key_f, once = g.t[key + "_f"], g.t[key + "_once"]
            staged = g.sem(ph, "staged_" + key)
            rows_ready = g.sem(ph, "rows_ready_" + key)
            compared = g.sem(ph, "compared_" + key)
            chain = g.sem(ph, "chain_" + key)
            block = nc.Block()
            with block:
                @block.tensor
                def _(pe):
                    with pe.Fori(0, S) as s:
                        for i in range(G):
                            pe.wait_ge(staged, s + 1)
                            pe.wait_ge(compared, s * G + (i + 1))
                            for k in range(GK):
                                ins = pe.transpose(key_ps[:, k, 0:P],
                                                   key_slot[:, i * GK + k:i * GK + k + 1].to_broadcast([P, P]),
                                                   g.t["ident"][0:P, 0:P])
                            ins.then_inc(rows_ready, 1)

                @block.vector
                def _(dve):
                    dve.sem_inc(compared, 1)
                    per = 3 * G + 4
                    with dve.Fori(0, S) as s:
                        dve.tensor_copy(key_slot[:], key_f[:, bass.ds(s, 1), :].rearrange("p o k -> p (o k)"))\
                            .then_inc(staged, 1)
                        dve.wait_ge(staged, s + 1)
                        for i in range(G):
                            dve.wait_ge(rows_ready, s * G + (i + 1))
                            dve.tensor_tensor(same[:], key_ps[:, :, 0:P], bcast(key_slot[:, i * GK:(i + 1) * GK], P),
                                              ALU.is_equal).then_inc(chain, 1)
                            dve.wait_ge(chain, s * per + (3 * i + 1))
                            dve.tensor_tensor(same[:], same[:], rows(g.t["lower"][:], GK), ALU.mult).then_inc(chain, 1)
                            dve.wait_ge(chain, s * per + (3 * i + 2))
                            dve.tensor_reduce(late[:, i * GK:(i + 1) * GK], same[:], AX, ALU.max).then_inc(chain, 1)
                            dve.wait_ge(chain, s * per + (3 * i + 3))
                            dve.sem_inc(compared, 1)
                        dve.tensor_scalar(shift[:], key_slot[:], -1.0, g.t["trash"][:, 0:1], ALU.mult, ALU.add)\
                            .then_inc(chain, 1)
                        dve.wait_ge(chain, s * per + (3 * G + 1))
                        dve.tensor_tensor(shift[:], shift[:], late[:], ALU.mult).then_inc(chain, 1)
                        dve.wait_ge(chain, s * per + (3 * G + 2))
                        dve.tensor_tensor(late[:], shift[:], key_slot[:], ALU.add).then_inc(chain, 1)
                        dve.wait_ge(chain, s * per + (3 * G + 3))
                        dve.tensor_copy(once[:, bass.ds(s, 1), :].rearrange("p o k -> p (o k)"), late[:])\
                            .then_inc(chain, 1)
                        dve.wait_ge(chain, s * per + per)
    g.clear_semaphores()


def node_linear(g, name, src, outs):
    nc, NB = g.nc, g.NB
    B = 5
    assert NB % B == 0 and len(outs) <= 3
    with ExitStack() as ph:
        stage = ph.enter_context(g.sbuf(name + "_stage", [P, B, C], F32))
        turned = ph.enter_context(g.sbuf(name + "_turned", [C, B, P], F32))
        turn_ps = ph.enter_context(g.psum(name + "_turn_ps", [C, B + 3, 128], F32))
        out_ps = [ph.enter_context(g.psum(f"{name}_out_ps{i}", [P, B + 3, 128], F32))
                  for i in range(len(outs))]
        staged = g.sem(ph, name + "_staged")
        turned_ready = g.sem(ph, name + "_turned_ready")
        copied = g.sem(ph, name + "_copied")
        product_ready = g.sem(ph, name + "_product_ready")
        stored = g.sem(ph, name + "_stored")
        block = ph.enter_context(nc.Block())

        @block.scalar
        def _(act):
            with act.Fori(0, NB // B) as i:
                act.wait_ge(turned_ready, i + 1)
                act.copy(stage[:], src[:, bass.ds(i * B, B), :]).then_inc(staged, 1)

        @block.tensor
        def _(pe):
            pe.sem_inc(turned_ready, 1)
            with pe.Fori(0, NB // B) as i:
                pe.wait_ge(staged, i + 1)
                pe.wait_ge(copied, i + 1)
                for b in range(B):
                    ins = pe.transpose(turn_ps[:, b, 0:P], stage[:, b, :], g.t["ident"][0:P, 0:P])
                ins.then_inc(turned_ready, 1)
                pe.wait_ge(copied, i + 2)
                pe.wait_ge(stored, i + 1)
                for o, (weight, _, _) in enumerate(outs):
                    for b in range(B):
                        ins = pe.matmul(out_ps[o][:, b, :], turned[:, b, :], weight[:], start=True, stop=True)
                ins.then_inc(product_ready, 1)

        @block.vector
        def _(dve):
            dve.sem_inc(copied, 1)
            dve.sem_inc(stored, 1)
            with dve.Fori(0, NB // B) as i:
                dve.wait_ge(turned_ready, i + 2)
                dve.tensor_copy(turned[:], turn_ps[:, 0:B, 0:P]).then_inc(copied, 1)
                dve.wait_ge(product_ready, i + 1)
                for o, (_, added, dst) in enumerate(outs):
                    more = rows(added[:], B) if len(added.shape) == 2 else added[:, bass.ds(i * B, B), :]
                    ins = dve.tensor_tensor(dst[:, bass.ds(i * B, B), :], out_ps[o][:, 0:B, :], more, ALU.add)
                ins.then_inc(stored, 1)
            dve.wait_ge(stored, NB // B + 1)


def to_table(g, pairs):
    with ExitStack() as ph:
        written = g.sem(ph, "written")
        block = ph.enter_context(g.nc.Block())

        @block.sync
        def _(sp):
            for table, feats in pairs:
                sp.dma_start(table.rearrange("(p j) c -> p j c", p=P), feats[:]).then_inc(written, 16)
            sp.wait_ge(written, 16 * len(pairs))


class Chain:

    def __init__(self, eng, sem):
        self.eng, self.sem, self.n = eng, sem, 0

    def __call__(self, ins):
        self.n += 1
        ins.then_inc(self.sem, 1)
        self.eng.wait_ge(self.sem, self.n)


def layer_norm(g, h, scratch, dst=None, scale=None, shift=None):
    nc, NB = g.nc, g.NB
    dst = h if dst is None else dst
    with ExitStack() as ph:
        m = ph.enter_context(g.sbuf("ln_m", [P, NB], F32))
        v = ph.enter_context(g.sbuf("ln_v", [P, NB], F32))
        chain = g.sem(ph, "ln_chain")
        var_ready = g.sem(ph, "ln_var_ready")
        root_ready = g.sem(ph, "ln_root_ready")
        block = ph.enter_context(nc.Block())

        @block.vector
        def _(dve):
            link = Chain(dve, chain)
            link(dve.tensor_reduce(m[:], h[:], AX, ALU.add))
            link(dve.tensor_scalar(m[:], m[:], 1.0 / C, None, ALU.mult))
            link(dve.tensor_tensor(h[:], h[:], bcast(m[:], C), ALU.subtract))
            link(dve.tensor_tensor(scratch[:], h[:], h[:], ALU.mult))
            link(dve.tensor_reduce(v[:], scratch[:], AX, ALU.add))
            dve.tensor_scalar(v[:], v[:], 1.0 / C, LN_EPS, ALU.mult, ALU.add).then_inc(var_ready, 1)
            dve.wait_ge(root_ready, 1)
            link(dve.reciprocal(m[:], v[:]))
            link(dve.tensor_tensor(dst[:], h[:], bcast(m[:], C), ALU.mult))
            if scale is not None:
                link(dve.tensor_tensor(dst[:], dst[:], rows(scale[:], NB), ALU.mult))
                link(dve.tensor_tensor(dst[:], dst[:], rows(shift[:], NB), ALU.add))

        @block.scalar
        def _(act):
            act.wait_ge(var_ready, 1)
            act.activation(v[:], v[:], ACT.Sqrt).then_inc(root_ready, 1)


def clear_tables(g):
    with ExitStack() as ph:
        cleared = g.sem(ph, "cleared")
        block = ph.enter_context(g.nc.Block())

        @block.sync
        def _(sp):
            for table in g.sums:
                sp.dma_start(table.rearrange("(p j) c -> p (j c)", p=P), g.t["zeros"][:]).then_inc(cleared, 16)
            sp.wait_ge(cleared, 16 * TABLES)


def collect_sums(g, total, scratch, tables):
    nc, NB, N = g.nc, g.NB, g.N
    with ExitStack() as ph:
        loaded = [g.sem(ph, f"sums_loaded{u}") for u in range(len(tables))]
        chain = g.sem(ph, "sums_chain")
        block = ph.enter_context(nc.Block())
        B = len(scratch) if scratch else 1

        @block.sync
        def _(sp):
            for u, table in enumerate(tables):
                to = total if u == 0 else scratch[(u - 1) % B]
                if u > B:
                    sp.wait_ge(chain, u - B)
                sp.dma_start(to[:], table[0:N, :].rearrange("(p j) c -> p j c", p=P)).then_inc(loaded[u], 16)
            sp.wait_ge(loaded[0], 16)

        @block.vector
        def _(dve):
            link = Chain(dve, chain)
            dve.wait_ge(loaded[0], 16)
            for u in range(1, len(tables)):
                dve.wait_ge(loaded[u], 16)
                link(dve.tensor_tensor(total[:], total[:], scratch[(u - 1) % B][:], ALU.add))


class Scatter:

    def __init__(self, g, ph, key):
        nc = g.nc
        self.g, self.key_f, self.once = g, g.t[key + "_f"], g.t[key + "_once"]
        sb = lambda name, shape, dt=F32: ph.enter_context(g.sbuf(name, shape, dt))
        self.key_slot = sb("key_slot", [P, K])
        self.once_slot = sb("once_slot", [P, K], I32)
        self.same = sb("same", [P, K, P])
        self.msg = sb("msg", [P, K, W])
        self.tile_sums = sb("tile_sums", [P, K, W])
        self.key_ps = ph.enter_context(g.psum("key_ps", [P, GK + 1, 128], F32))
        self.sum_ps = ph.enter_context(g.psum("sum_ps", [P, 512], F32))
        sem = lambda name: g.sem(ph, name)
        self.keys_staged, self.key_rows, self.same_ready = sem("keys_staged"), sem("key_rows"), sem("same_ready")
        self.msg_ready, self.summed, self.sums_out = sem("msg_ready"), sem("summed"), sem("sums_out")
        self.once_staged, self.rows_out, self.tick = sem("once_staged"), sem("rows_out"), sem("tick")
        self.scattered, self.base = g.scattered, g.scattered_so_far
        g.scattered_so_far += 16 * g.S * (K // TABLES)

    def stage_keys(self, dve, s):
        dve.wait_ge(self.summed, s * G + 1)
        dve.tensor_copy(self.key_slot[:], self.key_f[:, bass.ds(s, 1), :].rearrange("p o k -> p (o k)"))\
            .then_inc(self.keys_staged, 1)

    def compare(self, dve, s):
        for i in range(G):
            at = slice(i * GK, (i + 1) * GK)
            dve.wait_ge(self.key_rows, s * G + (i + 1))
            dve.wait_ge(self.keys_staged, s + 1)
            dve.tensor_tensor(self.same[:, at, :], self.key_ps[:, 0:GK, 0:P], bcast(self.key_slot[:, at], P),
                              ALU.is_equal).then_inc(self.same_ready, 1)

    def stage_once(self, dve, s):
        dve.wait_ge(self.rows_out, s + 1)
        dve.tensor_copy(self.once_slot[:], self.once[:, bass.ds(s, 1), :].rearrange("p o k -> p (o k)"))\
            .then_inc(self.once_staged, 1)

    def key_rows_and_sums(self, pe, s):
        for i in range(G):
            pe.wait_ge(self.keys_staged, s + 1)
            pe.wait_ge(self.same_ready, s * G + (i + 1))
            for k in range(GK):
                ins = pe.transpose(self.key_ps[:, k, 0:P],
                                   self.key_slot[:, i * GK + k:i * GK + k + 1].to_broadcast([P, P]),
                                   self.g.t["ident"][0:P, 0:P])
            ins.then_inc(self.key_rows, 1)
        for i in range(G):
            pe.wait_ge(self.same_ready, s * G + (i + 2))
            pe.wait_ge(self.msg_ready, s * G + (i + 1))
            pe.wait_ge(self.sums_out, s * G + (i + 1))
            for k in range(GK):
                t = i * GK + k
                ins = pe.matmul(self.sum_ps[:, k * W:(k + 1) * W], self.same[:, t, :], self.msg[:, t, :],
                                start=True, stop=True)
            ins.then_inc(self.summed, 1)

    def sums_to_sbuf(self, act, s):
        for i in range(G):
            act.wait_ge(self.summed, s * G + (i + 2))
            act.wait_ge(self.rows_out, s + 1)
            act.copy(self.tile_sums[:, i * GK:(i + 1) * GK, :].rearrange("p k w -> p (k w)"),
                     self.sum_ps[:, 0:GK * W]).then_inc(self.sums_out, 1)

    def release(self, pool, s):
        if s is not None:
            for u in range(TABLES):
                pool.wait_ge(self.scattered[u], self.base + 16 * (s * (K // TABLES)))
        pool.sem_inc(self.rows_out, 1)

    def scatter(self, pool, s):
        for k in range(K):
            u = k % TABLES
            pool.wait_ge(self.sums_out, s * G + (k // GK + 2))
            pool.wait_ge(self.once_staged, s + 1)
            if k >= TABLES:
                pool.wait_ge(self.scattered[u], self.base + 16 * (s * (K // TABLES) + k // TABLES))
            pool.sem_inc(self.tick, 1)
            pool.indirect_dma_start(out=self.g.sums[u][:, :],
                                    out_offset=bass.IndirectOffsetOnAxis(ap=self.once_slot[:, k:k + 1], axis=0),
                                    in_=self.tile_sums[:, k, :], in_offset=None, compute_op=ALU.add)\
                .then_inc(self.scattered[u], 16)

    def give_ahead(self, eng, who):
        if who == "dve":
            eng.sem_inc(self.same_ready, 1)
        if who == "act":
            eng.sem_inc(self.sums_out, 1)
        if who == "pe":
            eng.sem_inc(self.summed, 1)


class Gather:

    def __init__(self, g, ph, name, table, key, arrived=0):
        self.table, self.key_i = table, g.t[key + "_i"]
        self.slot = ph.enter_context(g.sbuf(name + "_slot", [P, K], I32))
        self.got = ph.enter_context(g.sbuf(name + "_got", [P, K, C], F32))
        self.staged = g.sem(ph, name + "_staged")
        self.used = g.sem(ph, name + "_used")
        self.tick = g.sem(ph, name + "_tick")
        self.arrived, self.base = g.arrived[arrived], g.arrived_so_far[arrived]
        g.arrived_so_far[arrived] += 16 * GK * g.S

    def stage(self, dve, s):
        dve.tensor_copy(self.slot[:], self.key_i[:, bass.ds(s, 1), :].rearrange("p o k -> p (o k)"))\
            .then_inc(self.staged, 1)

    def gather(self, pool, s):
        for k in range(K):
            if k % GK == 0:
                pool.wait_ge(self.staged, s + 1)
                pool.wait_ge(self.used, s * G + 1)
                pool.sem_inc(self.tick, 1)
            pool.indirect_dma_start(out=self.got[:, k, :], out_offset=None, in_=self.table[:, :],
                                    in_offset=bass.IndirectOffsetOnAxis(ap=self.slot[:, k:k + 1], axis=0))\
                .then_inc(self.arrived[k // GK], 16)


def edges_l0(g):
    nc, S = g.nc, g.S
    t = g.t
    ea_dram = g.ins["edge_attr_64"].rearrange("(s p k) c -> s p k c", p=P, k=K)
    ts_dram = g.ins["edge_weight"].rearrange("(s n) -> s n", n=P * K)
    D = ea_dram.shape[3]
    with ExitStack() as ph:
        sb = lambda name, shape: ph.enter_context(g.sbuf(name, shape, F32))
        ps = lambda name: ph.enter_context(g.psum(name, [C, 512], F32))
        sc = Scatter(g, ph, "dst")
        ga = Gather(g, ph, "xa", g.xa, "src")
        ea = sb("ea", [P, K, D])
        ts = sb("ts", [1, P * K])
        eaT = sb("eaT", [D, K, P])
        h1T = sb("h1T", [C, K, P])
        gateT = sb("gateT", [C, K, P])
        efT = sb("efT", [C, K, P])
        ea_ps, h1_ps, ts_ps, ef_ps, pre_ps = ps("ea_ps"), ps("h1_ps"), ps("ts_ps"), ps("ef_ps"), ps("pre_ps")
        sem = lambda name: g.sem(ph, name)
        ea_in, ea_turned, eaT_out = sem("ea_in"), sem("ea_turned"), sem("eaT_out")
        ts_in, ts_spread, gate_out = sem("ts_in"), sem("ts_spread"), sem("gate_out")
        h1_ready, h1_out, ef_ready, ef_out = sem("h1_ready"), sem("h1_out"), sem("ef_ready"), sem("ef_out")
        pre_ready, added, tick = sem("pre_ready"), sem("added"), sem("pe_tick")
        block = ph.enter_context(nc.Block())
        ts_tiles = ts[:].rearrange("o (p k) -> o k p", k=K)

        @block.sync
        def _(sp):
            with sp.Fori(0, S) as s:
                sp.wait_ge(ea_turned, s * G + 1)
                sp.dma_start(ea[:], ea_dram[bass.ds(s, 1)].rearrange("o p k c -> p (o k) c")).then_inc(ea_in, 16)
                sp.wait_ge(ts_spread, s * G + 1)
                sp.dma_start(ts[:], ts_dram[bass.ds(s, 1), :]).then_inc(ts_in, 16)

        @block.tensor
        def _(pe):
            pe.sem_inc(ea_turned, 1)
            pe.sem_inc(ts_spread, 1)
            sc.give_ahead(pe, "pe")
            with pe.Fori(0, S) as s:
                for i in range(G):
                    pe.wait_ge(ea_in, 16 * s + 16)
                    pe.wait_ge(eaT_out, s * G + (i + 1))
                    pe.sem_inc(tick, 1)
                    for k in range(GK):
                        ins = pe.transpose(ea_ps[0:D, k * P:(k + 1) * P], ea[:, i * GK + k, :], t["ident"][0:P, 0:P])
                    ins.then_inc(ea_turned, 1)
                    pe.wait_ge(ts_in, 16 * s + 16)
                    pe.wait_ge(gate_out, s * G + (i + 1))
                    pe.matmul(ts_ps[:, 0:GK * P], t["Wt_row"][:], ts_tiles[:, i * GK:(i + 1) * GK, :],
                              start=True, stop=True).then_inc(ts_spread, 1)
                for i in range(G):
                    pe.wait_ge(eaT_out, s * G + (i + 2))
                    pe.wait_ge(h1_out, s * G + (i + 1))
                    pe.matmul(h1_ps[:, 0:GK * P], t["L0_gnn_We1"][:],
                              eaT[:, i * GK:(i + 1) * GK, :].rearrange("c k p -> c (k p)"),
                              start=True, stop=True).then_inc(h1_ready, 1)
                for i in range(G):
                    pe.wait_ge(h1_out, s * G + (i + 2))
                    pe.wait_ge(ef_out, s * G + (i + 1))
                    pe.matmul(ef_ps[:, 0:GK * P], t["L0_gnn_We2"][:],
                              h1T[:, i * GK:(i + 1) * GK, :].rearrange("c k p -> c (k p)"),
                              start=True, stop=True).then_inc(ef_ready, 1)
                for i in range(G):
                    pe.wait_ge(ef_out, s * G + (i + 2))
                    pe.wait_ge(added, s * G + (i + 1))
                    for k in range(GK):
                        ins = pe.matmul(pre_ps[0:P, k * C:(k + 1) * C], efT[:, i * GK + k, :], t["Wn1_edge"][:],
                                        start=True, stop=True)
                    ins.then_inc(pre_ready, 1)
                sc.key_rows_and_sums(pe, s)

        @block.scalar
        def _(act):
            for x in (eaT_out, gate_out, h1_out):
                act.sem_inc(x, 1)
            sc.give_ahead(act, "act")
            with act.Fori(0, S) as s:
                for i in range(G):
                    at = slice(i * GK, (i + 1) * GK)
                    act.wait_ge(ea_turned, s * G + (i + 2))
                    act.copy(eaT[:, at, :].rearrange("c k p -> c (k p)"), ea_ps[0:D, 0:GK * P]).then_inc(eaT_out, 1)
                    act.wait_ge(ts_spread, s * G + (i + 2))
                    act.activation(gateT[:, at, :].rearrange("c k p -> c (k p)"), ts_ps[:, 0:GK * P], ACT.Sigmoid,
                                   bias=t["L0_gnn_bt"][:, 0:1]).then_inc(gate_out, 1)
                for i in range(G):
                    act.wait_ge(h1_ready, s * G + (i + 1))
                    act.activation(h1T[:, i * GK:(i + 1) * GK, :].rearrange("c k p -> c (k p)"), h1_ps[:, 0:GK * P],
                                   ACT.Relu, bias=t["L0_gnn_be1"][:, 0:1]).then_inc(h1_out, 1)
                for i in range(G):
                    at = slice(i * GK, (i + 1) * GK)
                    act.wait_ge(added, s * G + (i + 2))
                    act.activation(sc.msg[:, at, 0:C], ga.got[:, at, :], ACT.Relu).then_inc(sc.msg_ready, 1)
                    act.wait_ge(sc.msg_ready, s * G + (i + 1))
                    act.sem_inc(ga.used, 1)
                sc.sums_to_sbuf(act, s)

        @block.vector
        def _(dve):
            dve.sem_inc(ef_out, 1)
            dve.sem_inc(added, 1)
            dve.memset(sc.msg[:, :, C:W], 1.0)
            sc.give_ahead(dve, "dve")
            ga.stage(dve, 0)
            with dve.Fori(0, S) as s:
                sc.stage_keys(dve, s)
                for i in range(G):
                    at = slice(i * GK, (i + 1) * GK)
                    dve.wait_ge(ef_ready, s * G + (i + 1))
                    dve.wait_ge(gate_out, s * G + (i + 2))
                    dve.scalar_tensor_tensor(out=efT[:, at, :].rearrange("c k p -> c (k p)"), in0=ef_ps[:, 0:GK * P],
                                             scalar=t["L0_gnn_be2"][:, 0:1],
                                             in1=gateT[:, at, :].rearrange("c k p -> c (k p)"),
                                             op0=ALU.add, op1=ALU.mult).then_inc(ef_out, 1)
                for i in range(G):
                    at = slice(i * GK, (i + 1) * GK)
                    dve.wait_ge(pre_ready, s * G + (i + 1))
                    dve.wait_ge(ga.arrived[i], 16 * GK * s + (ga.base + 16 * GK))
                    dve.tensor_tensor(ga.got[:, at, :].rearrange("p k c -> p (k c)"), pre_ps[0:P, 0:GK * C],
                                      ga.got[:, at, :].rearrange("p k c -> p (k c)"), ALU.add).then_inc(added, 1)
                sc.compare(dve, s)
                ga.stage(dve, s + 1)
                sc.stage_once(dve, s)

        @block.gpsimd
        def _(pool):
            pool.sem_inc(ga.used, 1)
            sc.release(pool, None)
            ga.gather(pool, 0)
            ga.gather(pool, 1)
            sc.scatter(pool, 0)
            with pool.Fori(1, S - 1) as s:
                ga.gather(pool, s + 1)
                sc.release(pool, s)
                sc.scatter(pool, s)
            sc.release(pool, S - 1)
            sc.scatter(pool, S - 1)
            for u in range(TABLES):
                pool.wait_ge(sc.scattered[u], sc.base + 16 * S * (K // TABLES))
    g.clear_semaphores()


def edges_l1_scores(g):
    nc, S, t = g.nc, g.S, g.t
    len_dram = g.ins["edge_weight1"].rearrange("(s n) o -> s (n o)", n=P * K)
    with ExitStack() as ph:
        sb = lambda name, shape: ph.enter_context(g.sbuf(name, shape, F32))
        gq = Gather(g, ph, "q", g.q, "src")
        gk = Gather(g, ph, "k", g.k, "dst", arrived=1)
        row = sb("len_row", [1, P * K])
        hidT = sb("hidT", [C, K, P])
        dots = sb("dots", [P, K, H])
        len_ps = ph.enter_context(g.psum("len_ps", [C, 512], F32))
        bias_ps = ph.enter_context(g.psum("bias_ps", [P, GK, H], F32))
        sem = lambda name: g.sem(ph, name)
        row_in, spread, hid_out = sem("row_in"), sem("spread"), sem("hid_out")
        bias_ready, chain, scored = sem("bias_ready"), sem("chain"), sem("scored")
        block = ph.enter_context(nc.Block())
        row_tiles = row[:].rearrange("o (p k) -> o k p", k=K)

        @block.sync
        def _(sp):
            with sp.Fori(0, S) as s:
                sp.wait_ge(spread, s * G + 1)
                sp.dma_start(row[:], len_dram[bass.ds(s, 1), :]).then_inc(row_in, 16)

        @block.tensor
        def _(pe):
            pe.sem_inc(spread, 1)
            with pe.Fori(0, S) as s:
                for i in range(G):
                    pe.wait_ge(row_in, 16 * s + 16)
                    pe.wait_ge(hid_out, s * G + (i + 1))
                    pe.matmul(len_ps[:, 0:GK * P], t["We1_row"][:], row_tiles[:, i * GK:(i + 1) * GK, :],
                              start=True, stop=True).then_inc(spread, 1)
                for i in range(G):
                    pe.wait_ge(hid_out, s * G + (i + 2))
                    pe.wait_ge(scored, s * G + (i + 1))
                    for k in range(GK):
                        pe.matmul(bias_ps[:, k, :], hidT[:, i * GK + k, :], t["L1_gnn_We2_T"][:], start=True, stop=False)
                        ins = pe.matmul(bias_ps[:, k, :], t["ones"][0:1, 0:P], t["be2_row"][:], start=False, stop=True)
                    ins.then_inc(bias_ready, 1)

        @block.scalar
        def _(act):
            act.sem_inc(hid_out, 1)
            with act.Fori(0, S) as s:
                act.wait_ge(bias_ready, s * G + 1)
                for i in range(G):
                    act.wait_ge(spread, s * G + (i + 2))
                    act.activation(hidT[:, i * GK:(i + 1) * GK, :].rearrange("c k p -> c (k p)"), len_ps[:, 0:GK * P],
                                   ACT.Silu, bias=t["L1_gnn_be1"][:, 0:1]).then_inc(hid_out, 1)

        @block.vector
        def _(dve):
            dve.sem_inc(scored, 1)
            dve.sem_inc(bias_ready, 1)
            gq.stage(dve, 0)
            gk.stage(dve, 0)
            with dve.Fori(0, S) as s:
                for i in range(G):
                    at = slice(i * GK, (i + 1) * GK)
                    step = s * (4 * G) + 4 * i
                    dve.wait_ge(gq.arrived[i], 16 * GK * s + (gq.base + 16 * GK))
                    dve.wait_ge(gk.arrived[i], 16 * GK * s + (gk.base + 16 * GK))
                    dve.tensor_tensor(gq.got[:, at, :], gq.got[:, at, :], gk.got[:, at, :], ALU.mult).then_inc(chain, 1)
                    dve.wait_ge(chain, step + 1)
                    dve.tensor_reduce(dots[:, at, :].rearrange("p k h -> p (k h)"),
                                      gq.got[:, at, :].rearrange("p k (h d) -> p (k h) d", h=H), AX, ALU.add)\
                        .then_inc(chain, 1)
                    dve.wait_ge(chain, step + 2)
                    dve.sem_inc(gq.used, 1)
                    dve.sem_inc(gk.used, 1)
                    dve.wait_ge(bias_ready, s * G + (i + 2))
                    dve.scalar_tensor_tensor(out=dots[:, at, :], in0=dots[:, at, :], scalar=float((C // H) ** -0.5),
                                             in1=bias_ps[:], op0=ALU.mult, op1=ALU.add).then_inc(chain, 1)
                    dve.wait_ge(chain, step + 3)
                    dve.sem_inc(scored, 1)
                    dve.tensor_tensor(g.scores[:, bass.ds(s * K + i * GK, GK), :], dots[:, at, :],
                                      bcast(g.cut[:, bass.ds(s * K + i * GK, GK)], H), ALU.mult).then_inc(chain, 1)
                    dve.wait_ge(chain, step + 4)
                nxt = s + 1
                gq.stage(dve, nxt)
                gk.stage(dve, nxt)

        @block.gpsimd
        def _(pool):
            pool.sem_inc(gq.used, 1)
            pool.sem_inc(gk.used, 1)
            with pool.Fori(0, S) as s:
                gq.gather(pool, s)
                gk.gather(pool, s)
            for i in range(G):
                pool.wait_ge(gq.arrived[i], gq.base + 16 * GK * S)
                pool.wait_ge(gk.arrived[i], gk.base + 16 * GK * S)
    g.clear_semaphores()


def cutoff(g):
    nc, S = g.nc, g.S
    with ExitStack() as ph:
        sb = lambda name: ph.enter_context(g.sbuf(name, [P, S * K], F32))
        length, folded, inside = sb("length"), sb("folded"), sb("inside")
        periods = ph.enter_context(g.sbuf("periods", [P, S * K], I32))
        loaded, chain = g.sem(ph, "len_loaded"), g.sem(ph, "cut_chain")
        folded_ready, sin_ready, bias_set = g.sem(ph, "folded_ready"), g.sem(ph, "sin_ready"), g.sem(ph, "bias_set")
        block = ph.enter_context(nc.Block())
        per = 2.0 * CUTOFF

        @block.sync
        def _(sp):
            sp.dma_start(length[:].rearrange("p (s k) -> p s k", k=K),
                         g.ins["edge_weight1"].rearrange("(s p k) o -> p s (k o)", p=P, k=K)).then_inc(loaded, 16)

        @block.vector
        def _(dve):
            link = Chain(dve, chain)
            dve.wait_ge(loaded, 16)
            link(dve.tensor_scalar(inside[:], length[:], CUTOFF, 0.5, ALU.is_lt, ALU.mult))
            link(dve.tensor_scalar(folded[:], length[:], 1.0 / per, None, ALU.mult))
            link(dve.tensor_copy(periods[:], folded[:]))
            link(dve.tensor_copy(folded[:], periods[:]))
            link(dve.scalar_tensor_tensor(out=length[:], in0=folded[:], scalar=-per, in1=length[:],
                                          op0=ALU.mult, op1=ALU.add))
            link(dve.tensor_scalar(folded[:], length[:], -1.0, None, ALU.mult))
            link(dve.tensor_tensor(folded[:], folded[:], length[:], ALU.max))
            link(dve.tensor_scalar(folded[:], folded[:], -CUTOFF, None, ALU.add))
            link(dve.tensor_scalar(length[:], folded[:], -1.0, None, ALU.mult))
            link(dve.tensor_tensor(folded[:], folded[:], length[:], ALU.max))
            dve.tensor_scalar(folded[:], folded[:], float(np.pi / CUTOFF), float(-np.pi / 2), ALU.mult, ALU.add)\
                .then_inc(folded_ready, 1)
            dve.wait_ge(sin_ready, 1)
            link(dve.tensor_scalar(folded[:], folded[:], 1.0, None, ALU.add))
            link(dve.tensor_tensor(g.cut[:], folded[:], inside[:], ALU.mult))

        @block.scalar
        def _(act):
            act.wait_ge(folded_ready, 1)
            act.activation(folded[:], folded[:], ACT.Sin).then_inc(sin_ready, 1)


def head_maximum(g):
    nc = g.nc
    with ExitStack() as ph:
        m = ph.enter_context(g.sbuf("m", [P, H], F32))
        mT = ph.enter_context(g.sbuf("mT", [H, 1], F32))
        diag = ph.enter_context(g.sbuf("diag", [H, H], F32))
        ps = ph.enter_context(g.psum("max_ps", [P, 2, 512], F32))
        dve_step, pe_step = g.sem(ph, "max_dve"), g.sem(ph, "max_pe")
        block = ph.enter_context(nc.Block())

        @block.vector
        def _(dve):
            dve.tensor_reduce(m[:], g.scores[:].rearrange("p t h -> p h t"), AX, ALU.max).then_inc(dve_step, 1)
            dve.wait_ge(pe_step, 1)
            dve.tensor_reduce(mT[:], ps[0:H, 0, 0:P], AX, ALU.max).then_inc(dve_step, 1)
            dve.wait_ge(dve_step, 2)
            dve.tensor_scalar(diag[:], g.t["ident"][0:H, 0:H], mT[:, 0:1], None, ALU.mult).then_inc(dve_step, 1)
            dve.wait_ge(pe_step, 2)
            dve.tensor_copy(g.top[:], ps[:, 1, 0:H]).then_inc(dve_step, 1)
            dve.wait_ge(dve_step, 4)

        @block.tensor
        def _(pe):
            pe.wait_ge(dve_step, 1)
            pe.transpose(ps[0:H, 0, 0:P], m[:], g.t["ident"][0:P, 0:P]).then_inc(pe_step, 1)
            pe.wait_ge(dve_step, 3)
            pe.matmul(ps[:, 1, 0:H], g.t["ones"][0:H, 0:P], diag[:], start=True, stop=True).then_inc(pe_step, 1)


def edges_simple(g, table, key_from, key_to, weighted):
    nc, S, t = g.nc, g.S, g.t
    with ExitStack() as ph:
        sc = Scatter(g, ph, key_to)
        ga = Gather(g, ph, "row", table, key_from)
        chain, exp_in, exp_out = g.sem(ph, "chain"), g.sem(ph, "exp_in"), g.sem(ph, "exp_out")
        below = ph.enter_context(g.sbuf("below", [P, K, H], F32))
        expd = ph.enter_context(g.sbuf("expd", [P, K, H], F32))
        block = ph.enter_context(nc.Block())

        @block.tensor
        def _(pe):
            sc.give_ahead(pe, "pe")
            with pe.Fori(0, S) as s:
                sc.key_rows_and_sums(pe, s)

        @block.scalar
        def _(act):
            sc.give_ahead(act, "act")
            with act.Fori(0, S) as s:
                if weighted:
                    act.wait_ge(exp_in, s + 1)
                    act.activation(expd[:], below[:], ACT.Exp).then_inc(exp_out, 1)
                sc.sums_to_sbuf(act, s)

        @block.vector
        def _(dve):
            if not weighted:
                dve.memset(sc.msg[:, :, C:W], 0.0)
            sc.give_ahead(dve, "dve")
            ga.stage(dve, 0)
            with dve.Fori(0, S) as s:
                sc.stage_keys(dve, s)
                if weighted:
                    dve.tensor_tensor(below[:], g.scores[:, bass.ds(s * K, K), :], rows(g.top[:], K), ALU.subtract)\
                        .then_inc(exp_in, 1)
                    dve.wait_ge(exp_out, s + 1)
                    dve.tensor_copy(sc.msg[:, :, C:W], expd[:]).then_inc(chain, 1)
                for i in range(G):
                    at = slice(i * GK, (i + 1) * GK)
                    dve.wait_ge(ga.arrived[i], 16 * GK * s + (ga.base + 16 * GK))
                    if weighted:
                        dve.wait_ge(chain, s + 1)
                        ins = dve.tensor_tensor(
                            sc.msg[:, at, 0:C].rearrange("p k (h d) -> p k h d", h=H),
                            ga.got[:, at, :].rearrange("p k (h d) -> p k h d", h=H),
                            expd[:, at, :].unsqueeze(3).to_broadcast([P, GK, H, C // H]), ALU.mult)
                    else:
                        ins = dve.tensor_copy(sc.msg[:, at, 0:C], ga.got[:, at, :])
                    ins.then_inc(sc.msg_ready, 1)
                    dve.wait_ge(sc.msg_ready, s * G + (i + 1))
                    dve.sem_inc(ga.used, 1)
                sc.compare(dve, s)
                ga.stage(dve, s + 1)
                sc.stage_once(dve, s)

        @block.gpsimd
        def _(pool):
            pool.sem_inc(ga.used, 1)
            sc.release(pool, None)
            ga.gather(pool, 0)
            ga.gather(pool, 1)
            sc.scatter(pool, 0)
            with pool.Fori(1, S - 1) as s:
                ga.gather(pool, s + 1)
                sc.release(pool, s)
                sc.scatter(pool, s)
            sc.release(pool, S - 1)
            sc.scatter(pool, S - 1)
            for u in range(TABLES):
                pool.wait_ge(sc.scattered[u], sc.base + 16 * S * (K // TABLES))
    g.clear_semaphores()


def on_vector(g, steps):
    with ExitStack() as ph:
        done = g.sem(ph, "step_done")
        block = ph.enter_context(g.nc.Block())

        @block.vector
        def _(dve):
            for n, (who, f) in enumerate(steps):
                if who == "dve":
                    if n:
                        dve.wait_ge(done, n)
                    f(dve).then_inc(done, 1)
            dve.wait_ge(done, len(steps))

        @block.scalar
        def _(act):
            for n, (who, f) in enumerate(steps):
                if who == "act":
                    if n:
                        act.wait_ge(done, n)
                    f(act).then_inc(done, 1)


def attention_out(g, ph, tables):
    nc, NB, t = g.nc, g.NB, g.t
    x = t["x_sb"]
    sb = lambda name, shape: ph.enter_context(g.sbuf(name, shape, F32))
    total = sb("total", [P, NB, W])
    part = [sb(f"part{i}", [P, NB, W]) for i in range(2)]
    hid, scr, den = sb("hid", [P, NB, C]), sb("scr", [P, NB, C]), sb("den", [P, NB, H])
    collect_sums(g, total, part, tables)
    on_vector(g, [
        ("dve", lambda e: e.tensor_scalar(den[:], total[:, :, C:W], 1e-8, None, ALU.add)),
        ("dve", lambda e: e.reciprocal(den[:], den[:])),
        ("dve", lambda e: e.tensor_tensor(hid[:].rearrange("p j (h d) -> p j h d", h=H),
                                          total[:, :, 0:C].rearrange("p j (h d) -> p j h d", h=H),
                                          den[:].unsqueeze(3).to_broadcast([P, NB, H, C // H]), ALU.mult)),
        ("dve", lambda e: e.tensor_tensor(scr[:], x[:], rows(t["L1_gnn_bo"][:], NB), ALU.add)),
    ])
    node_linear(g, "l1", hid, [(t["L1_gnn_Wo_T"], scr, scr)])
    layer_norm(g, scr, hid, scale=t["L1_gnn_ln_g"], shift=t["L1_gnn_ln_b"])
    on_vector(g, [("dve", lambda e: e.tensor_tensor(scr[:], scr[:], x[:], ALU.add))])
    layer_norm(g, scr, hid, dst=x)


def degrees(g, per):
    on_vector(g, [
        ("dve", lambda e: e.tensor_scalar(per[:], g.count[:], 1.0, None, ALU.max)),
        ("dve", lambda e: e.reciprocal(per[:], per[:])),
        ("dve", lambda e: e.tensor_scalar(g.dinv[:], g.count[:], 1.0, None, ALU.add)),
        ("act", lambda e: e.activation(g.dinv[:], g.dinv[:], ACT.Sqrt)),
        ("dve", lambda e: e.reciprocal(g.dinv[:], g.dinv[:])),
    ])


def convolution_out(g, total, self_loop, hid):
    x, NB, t = g.t["x_sb"], g.NB, g.t
    scr = self_loop
    on_vector(g, [
        ("dve", lambda e: e.tensor_tensor(scr[:], total, self_loop[:], ALU.add)),
        ("dve", lambda e: e.tensor_tensor(scr[:], scr[:], bcast(g.dinv[:], C), ALU.mult)),
        ("dve", lambda e: e.tensor_tensor(scr[:], scr[:], rows(t["L3_gnn_b"][:], NB), ALU.add)),
        ("dve", lambda e: e.tensor_scalar(hid[:], scr[:], 20.0, None, ALU.min)),
        ("act", lambda e: e.activation(hid[:], hid[:], ACT.Exp)),
        ("dve", lambda e: e.scalar_tensor_tensor(out=hid[:], in0=hid[:], scalar=2.0, in1=hid[:],
                                                 op0=ALU.add, op1=ALU.mult)),
        ("dve", lambda e: e.tensor_tensor(scr[:], scr[:], hid[:], ALU.mult)),
        ("dve", lambda e: e.tensor_scalar(hid[:], hid[:], 2.0, None, ALU.add)),
        ("dve", lambda e: e.reciprocal(hid[:], hid[:])),
        ("dve", lambda e: e.tensor_tensor(scr[:], scr[:], hid[:], ALU.mult)),
        ("dve", lambda e: e.tensor_tensor(scr[:], scr[:], x[:], ALU.add)),
    ])
    layer_norm(g, scr, hid, dst=x)


def general_gnn(g):
    nc, N, NB, S, t = g.nc, g.N, g.NB, g.S, g.t
    x, count, dinv = t["x_sb"], g.count, g.dinv
    sb = lambda c, name, shape: c.enter_context(g.sbuf(name, shape, F32))
    with ExitStack() as ph:
        xa = sb(ph, "xa_sb", [P, NB, C])
        node_linear(g, "xa", x, [(t["Wn1_node"], t["L0_gnn_bn1"], xa)])
        to_table(g, [(g.xa, xa)])
        clear_tables(g)
    mark_duplicates(g)
    edges_l0(g)
    with ExitStack() as ph:
        total = sb(ph, "total", [P, NB, W])
        part = [sb(ph, f"part{i}", [P, NB, W]) for i in range(2)]
        hid, scr = sb(ph, "hid", [P, NB, C]), sb(ph, "scr", [P, NB, C])
        collect_sums(g, total, part, g.sums)
        on_vector(g, [
            ("dve", lambda e: e.tensor_copy(count[:], total[:, :, C:C + 1].rearrange("p j o -> p (j o)"))),
            ("dve", lambda e: e.tensor_copy(hid[:], total[:, :, 0:C])),
            ("dve", lambda e: e.tensor_tensor(scr[:], bcast(count[:], C), rows(t["L0_gnn_bn2"][:], NB), ALU.mult)),
            ("dve", lambda e: e.scalar_tensor_tensor(out=scr[:], in0=x[:], scalar=2.0, in1=scr[:], op0=ALU.mult, op1=ALU.add)),
        ])
        node_linear(g, "l0", hid, [(t["L0_gnn_Wn2"], scr, scr)])
        layer_norm(g, scr, hid, dst=x)
    g.clear_semaphores()
    with ExitStack() as lay:
        g.scores = sb(lay, "scores", [P, S * K, H])
        g.top = sb(lay, "top", [P, H])
        with ExitStack() as ph:
            qkv = [sb(ph, n, [P, NB, C]) for n in ("q_sb", "k_sb", "v_sb")]
            node_linear(g, "qkv", x, [(t[f"L1_gnn_W{n}_T"], t[f"L1_gnn_b{n}"], o) for n, o in zip("qkv", qkv)])
            to_table(g, list(zip((g.q, g.k, g.v), qkv)))
            clear_tables(g)
        with ExitStack() as ph:
            g.cut = sb(ph, "cut", [P, S * K])
            cutoff(g)
            g.clear_semaphores()
            edges_l1_scores(g)
        head_maximum(g)
        edges_simple(g, g.v, "dst", "src", weighted=True)
    with ExitStack() as ph:
        attention_out(g, ph, g.sums)
    to_table(g, [(g.x2, x)])
    clear_tables(g)
    g.clear_semaphores()
    edges_simple(g, g.x2, "src", "dst", weighted=False)
    with ExitStack() as ph:
        total = sb(ph, "total", [P, NB, W])
        part = [sb(ph, f"part{i}", [P, NB, W]) for i in range(2)]
        hid, scr, per = sb(ph, "hid", [P, NB, C]), sb(ph, "scr", [P, NB, C]), sb(ph, "per", [P, NB])
        collect_sums(g, total, part, g.sums)
        degrees(g, per)
        on_vector(g, [
            ("dve", lambda e: e.tensor_tensor(hid[:], total[:, :, 0:C], bcast(per[:], C), ALU.mult)),
            ("dve", lambda e: e.tensor_tensor(scr[:], x[:], rows(t["b_l2"][:], NB), ALU.add)),
        ])
        node_linear(g, "l2n", hid, [(t["L2_gnn_w_neigh_T"], scr, scr)])
        node_linear(g, "l2s", x, [(t["L2_gnn_w_self_T"], scr, scr)])
        layer_norm(g, scr, hid, dst=x)
    with ExitStack() as lay:
        h3 = sb(lay, "h3_sb", [P, NB, C])
        zero_row = sb(lay, "zero_row", [P, C])
        on_vector(g, [("dve", lambda e: e.memset(zero_row[:], 0.0))])
        node_linear(g, "h3", x, [(t["L3_gnn_W"], zero_row, h3)])
        on_vector(g, [("dve", lambda e: e.tensor_tensor(h3[:], h3[:], bcast(dinv[:], C), ALU.mult))])
        to_table(g, [(g.h3, h3)])
        clear_tables(g)
        g.clear_semaphores()
        edges_simple(g, g.h3, "src", "dst", weighted=False)
        total = sb(lay, "total", [P, NB, W])
        part = [sb(lay, f"part{i}", [P, NB, W]) for i in range(2)]
        hid = sb(lay, "hid", [P, NB, C])
        collect_sums(g, total, part, g.sums)
        convolution_out(g, total[:, :, 0:C], h3, hid)
    g.clear_semaphores()


def windows(g, ctx):
    nc, S, ins, t = g.nc, g.S, g.ins, g.t
    L = P * K
    keep = lambda name, shape, dt=F32: ctx.enter_context(g.sbuf(name, shape, dt))
    t["rank_f"] = keep("rank_f", [P, S, K])
    t["cell_f"] = keep("cell_f", [P, S, K])
    t["block_f"] = keep("block_f", [P, S, K])
    t["first4"] = keep("first4", [P, S * K, 4], BF16)
    t["node_i"] = keep("node_i", [R, S + 1], I32)
    t["iota_r"] = keep("iota_r", [P, R])
    t["iota_h"] = keep("iota_h", [P, HALF[0] * R], F16)
    t["part_f"] = keep("part_f", [P, 1])
    t["Wt9"] = keep("Wt9", [9, C], BF16)
    t["We1_9"] = keep("We1_9", [9, C], BF16)
    t["be2_3"] = keep("be2_3", [3, H], BF16)
    t["ones_b"] = keep("ones_b", [3, P], BF16)
    t["fast_ok"] = keep("fast_ok", [1, 1], I32)
    dram = lambda name, shape, dt=F32: nc.dram_tensor(name, shape, dt, kind="Internal").ap()
    rank_dram, first_dram = dram("rank_dram", (S, L)), dram("first_dram", (S, L))
    g.rank_rows = dram("rank_rows", (S, L), BF16)
    g.time9, g.len9 = dram("time9", (S, 9, L), BF16), dram("len9", (S, 9, L), BF16)
    wt9_dram, we9_dram = dram("wt9_dram", (3, 3, C), BF16), dram("we9_dram", (3, 3, C), BF16)
    be3_dram = dram("be3_dram", (3, H), BF16)

    with ExitStack() as ph:
        sb = lambda name, shape, dt=F32: ph.enter_context(g.sbuf(name, shape, dt))
        raw = sb("raw", [S, L], I32)
        d, change, rank = sb("d", [S, L]), sb("change", [S, L]), sb("rank", [S, L])
        rank_b = sb("rank_b", [S, K, P], BF16)
        bad, worse = sb("bad", [S, 1]), sb("worse", [S, 1])
        row = {n: sb(n + "_in", [S, L]) for n in ("time", "len")}
        rest = sb("rest", [S, K, P])
        parts = {n: sb(n + "_parts", [S, 3, L], BF16) for n in ("time", "len")}
        wrest = sb("wrest", [1, C])
        wparts = {n: sb(n + "_parts", [1, 3, C], BF16) for n in ("Wt_row", "We1_row")}
        bparts = sb("be2_parts", [1, 3, H], BF16)
        loaded, chain, pool_done = g.sem(ph, "win_loaded"), g.sem(ph, "win_chain"), g.sem(ph, "win_pool")
        ready, stored, back = g.sem(ph, "win_ready"), g.sem(ph, "win_stored"), g.sem(ph, "win_back")
        turned, consts_in = g.sem(ph, "win_turned"), g.sem(ph, "win_consts_in")
        ints = sb("ints", [P, S, K], I32)
        quot, over, hi6 = sb("quot", [P, S, K]), sb("over", [P, S, K]), sb("hi6", [P, S, K])
        firsts = sb("firsts", [P, S, K])
        flag_ps = ph.enter_context(g.psum("flag_ps", [1, 512], F32))
        flag_f = sb("flag_f", [1, 1])
        iota_i = sb("iota_i", [P, HALF[0] * R], I32)
        block = ph.enter_context(nc.Block())

        @block.sync
        def _(sp):
            sp.dma_start(raw[:], ins["dst"].rearrange("(s n) -> s n", n=L)).then_inc(loaded, 16)
            sp.dma_start(row["time"][:], ins["edge_weight"].rearrange("(s n) -> s n", n=L)).then_inc(loaded, 16)
            sp.dma_start(row["len"][:], ins["edge_weight1"].rearrange("(s n) o -> s (n o)", n=L)).then_inc(loaded, 16)
            sp.wait_ge(ready, 1)
            sp.dma_start(rank_dram, rank[:]).then_inc(stored, 16)
            sp.dma_start(first_dram, change[:]).then_inc(stored, 16)
            sp.dma_start(g.rank_rows, rank_b[:].rearrange("s k p -> s (k p)")).then_inc(stored, 16)
            sp.wait_ge(stored, 48)
            sp.dma_start(t["rank_f"][:], rank_dram.rearrange("s (p k) -> p s k", k=K)).then_inc(back, 16)
            sp.dma_start(firsts[:], first_dram.rearrange("s (p k) -> p s k", k=K)).then_inc(back, 16)
            sp.wait_ge(ready, 2)
            for j in range(3):
                sp.dma_start(g.time9[:, 3 * j:3 * j + 3, :], parts["time"][:]).then_inc(stored, 16)
                sp.dma_start(g.len9[:, 3 * j:3 * j + 3, :], parts["len"][:]).then_inc(stored, 16)
                sp.dma_start(wt9_dram[:, j, :].unsqueeze(0), wparts["Wt_row"][:]).then_inc(stored, 16)
                sp.dma_start(we9_dram[:, j, :].unsqueeze(0), wparts["We1_row"][:]).then_inc(stored, 16)
            sp.dma_start(be3_dram.unsqueeze(0), bparts[:]).then_inc(stored, 16)
            sp.wait_ge(stored, 48 + 13 * 16)
            sp.dma_start(t["Wt9"][:], wt9_dram.rearrange("i j c -> (i j) c")).then_inc(consts_in, 16)
            sp.dma_start(t["We1_9"][:], we9_dram.rearrange("i j c -> (i j) c")).then_inc(consts_in, 16)
            sp.dma_start(t["be2_3"][:], be3_dram).then_inc(consts_in, 16)
            sp.wait_ge(consts_in, 3 * 16)
            sp.wait_ge(back, 2 * 16)

        @block.gpsimd
        def _(pool):
            pool.iota(iota_i[:], pattern=[[1, HALF[0] * R]], base=0, channel_multiplier=0).then_inc(pool_done, 1)

        @block.tensor
        def _(pe):
            pe.wait_ge(chain, FLAG_STEP)
            pe.transpose(flag_ps[0:1, 0:S], bad[:], t["ident"][0:S, 0:S]).then_inc(turned, 1)

        @block.vector
        def _(dve):
            link = Chain(dve, chain)
            dve.wait_ge(loaded, 48)
            link(dve.tensor_copy(d[:], raw[:]))
            link(dve.memset(change[:, 0:1], 0.0))
            link(dve.tensor_tensor(change[:, 1:L], d[:, 1:L], d[:, 0:L - 1], ALU.not_equal))
            link(dve.memset(rest[:], 0.0))
            link(dve.tensor_tensor_scan(rank[:], change[:], rest[:].rearrange("s k p -> s (k p)"), 0.0,
                                        ALU.add, ALU.add))
            link(dve.tensor_tensor(rest[:].rearrange("s k p -> s (k p)")[:, 1:L], d[:, 1:L], d[:, 0:L - 1], ALU.is_lt))
            link(dve.tensor_reduce(bad[:], rest[:].rearrange("s k p -> s (k p)"), AX, ALU.max))
            link(dve.tensor_scalar(worse[:], rank[:, L - 1:L], float(R) - 0.5, None, ALU.is_gt))
            link(dve.tensor_tensor(bad[:], bad[:], worse[:], ALU.max))
            assert link.n == FLAG_STEP
            link(dve.memset(change[:, 0:1], 1.0))
            dve.tensor_copy(rank_b[:], rank[:].rearrange("s (p k) -> s k p", k=K)).then_inc(ready, 1)
            dve.wait_ge(turned, 1)
            link(dve.tensor_reduce(flag_f[:], flag_ps[0:1, 0:S], AX, ALU.max))
            link(dve.tensor_scalar(flag_f[:], flag_f[:], -1.0, 1.0, ALU.mult, ALU.add))
            link(dve.tensor_copy(t["fast_ok"][:], flag_f[:]))

            def split(parts_of, x, left):
                for j in range(3):
                    link(dve.tensor_copy(parts_of(j), x if j == 0 else left))
                    if j < 2:
                        link(dve.tensor_tensor(left, x if j == 0 else left, parts_of(j), ALU.subtract))

            for n in ("time", "len"):
                split(lambda j: parts[n][:, j, :].rearrange("s (k p) -> s k p", k=K),
                      row[n][:].rearrange("s (p k) -> s k p", k=K), rest[:])
            for n in ("Wt_row", "We1_row"):
                split(lambda j: wparts[n][:, j, :], t[n][:], wrest[:])
            split(lambda j: bparts[:, j, :], t["be2_row"][:], wrest[:, 0:H])
            link(dve.memset(t["ones_b"][:], 1.0))
            dve.sem_inc(ready, 1)
            dve.wait_ge(pool_done, 1)
            link(dve.tensor_copy(t["iota_h"][:], iota_i[:]))
            link(dve.tensor_copy(t["iota_r"][:], iota_i[:, 0:R]))
            link(dve.tensor_scalar(t["part_f"][:], t["trash"][:], -float(g.N), None, ALU.add))
            link(dve.memset(t["node_i"][:, S:S + 1], 0))
            link(dve.tensor_scalar(quot[:], t["src_f"][:], 1.0 / g.NB, None, ALU.mult))
            link(dve.tensor_copy(ints[:], quot[:]))
            link(dve.tensor_copy(quot[:], ints[:]))
            link(dve.scalar_tensor_tensor(out=over[:], in0=quot[:], scalar=-float(g.NB), in1=t["src_f"][:],
                                          op0=ALU.mult, op1=ALU.add))
            link(dve.tensor_scalar(hi6[:], over[:], 0.0, None, ALU.is_lt))
            link(dve.tensor_tensor(t["block_f"][:], quot[:], hi6[:], ALU.subtract))
            link(dve.scalar_tensor_tensor(out=over[:], in0=hi6[:], scalar=float(g.NB), in1=over[:],
                                          op0=ALU.mult, op1=ALU.add))
            dve.wait_ge(back, 32)
            link(dve.scalar_tensor_tensor(out=t["cell_f"][:], in0=over[:], scalar=float(R), in1=t["rank_f"][:],
                                          op0=ALU.mult, op1=ALU.add))
            link(dve.tensor_scalar(quot[:], t["dst_f"][:], 1.0 / 64, None, ALU.mult))
            link(dve.tensor_copy(ints[:], quot[:]))
            link(dve.tensor_copy(quot[:], ints[:]))
            link(dve.tensor_scalar(hi6[:], quot[:], 64.0, None, ALU.mult))
            link(dve.tensor_tensor(over[:], t["dst_f"][:], hi6[:], ALU.subtract))
            f4 = lambda j: t["first4"][:, :, j:j + 1].rearrange("p (s k) o -> p s (k o)", k=K)
            link(dve.tensor_tensor(f4(0), hi6[:], firsts[:], ALU.mult))
            link(dve.tensor_tensor(f4(1), over[:], firsts[:], ALU.mult))
            link(dve.tensor_copy(f4(2), firsts[:]))
            link(dve.memset(t["first4"][:, :, 3:4], 1.0))


def edge_loop(eng, S, body, apart):
    for s in range(apart):
        body(s, s, False)
    with eng.Fori(apart, S - 1) as s:
        body(s, apart, False)
    body(S - 1, apart, True)


def fast_l0(g):
    nc, S, t = g.nc, g.S, g.t
    ea_dram = g.ins["edge_attr_64"].rearrange("(s p k) c -> s p k c", p=P, k=K)
    D = ea_dram.shape[3]
    table = g.fast_sums[0][0]
    with ExitStack() as ph:
        sb = lambda name, shape, dt=F32: ph.enter_context(g.sbuf(name, shape, dt))
        ps = lambda name: ph.enter_context(g.psum(name, [C, 512], F32))
        sem = lambda name: g.sem(ph, name)
        ea, ts = sb("ea", [P, K, D]), sb("ts", [9, K * P], BF16)
        eaT, h1T = sb("eaT", [D, K, P]), sb("h1T", [C, K, P])
        gateT, efT = sb("gateT", [C, K, P]), sb("efT", [C, K, P])
        xa, xa_slot = sb("xa_got", [P, K, C]), sb("xa_slot", [P, K], I32)
        msg = sb("msg", [P, K, C])
        ones_f, ones_b = sb("onehot_f", [P, K, R]), sb("onehot_b", [P, K, R], BF16)
        sumT = sb("sumT", [C, R])
        found = sb("found", [R, 4])
        spare = sb("spare", [R, 1])
        node_slot = sb("node_slot", [R, 1], I32)
        out_rows = sb("out_rows", [R, W])
        ea_ps, h1_ps, ts_ps, ef_ps = ps("ea_ps"), ps("h1_ps"), ps("ts_ps"), ps("ef_ps")
        pre_ps = [ps("pre_ps0"), ps("pre_ps1")]
        sum_ps, row_ps = ps("sum_ps"), ps("row_ps")
        ea_in, ea_turned, eaT_out = sem("ea_in"), sem("ea_turned"), sem("eaT_out")
        ts_in, ts_spread, gate_out = sem("ts_in"), sem("ts_spread"), sem("gate_out")
        h1_ready, h1_out, ef_ready, ef_out = sem("h1_ready"), sem("h1_out"), sem("ef_ready"), sem("ef_out")
        pre_ready, added, msg_ready = sem("pre_ready"), sem("added"), sem("msg_ready")
        onehot, summed, sumT_out, row_ready = sem("onehot"), sem("summed"), sem("sumT_out"), sem("row_ready")
        found_out, chain, slot_ready, row_out = sem("found_out"), sem("chain"), sem("slot_ready"), sem("row_out")
        staged, tick, pool_tick = sem("staged"), sem("pe_tick"), sem("pool_tick")
        cleared, cleared_later = sem("cleared"), sem("cleared_later")
        arrived, scattered = g.arrived[0], g.scattered[0]
        a_base, s_base = g.arrived_so_far[0], g.scatters[0]
        g.arrived_so_far[0] += 16 * GK * S
        g.scatters[0] += 16 * S
        block = ph.enter_context(nc.Block())
        grp = lambda i: slice(i * GK, (i + 1) * GK)
        flat = lambda buf, i: buf[:, grp(i), :].rearrange("c k p -> c (k p)")

        @block.sync
        def _(sp):
            def clear(tab, done):
                sp.dma_start(tab.rearrange("(p j) c -> p (j c)", p=P), t["zeros"][:, 0:26 * tab.shape[1]])\
                    .then_inc(done, 16)

            sp.dma_start(ea[:], ea_dram[0]).then_inc(ea_in, 16)
            sp.dma_start(ts[:], g.time9[0]).then_inc(ts_in, 16)
            clear(table, cleared)
            with sp.Fori(1, S) as s:
                sp.wait_ge(ea_turned, s * G)
                sp.dma_start(ea[:], ea_dram[bass.ds(s, 1)].rearrange("o p k c -> p (o k) c")).then_inc(ea_in, 16)
                sp.wait_ge(ts_spread, s * G)
                sp.dma_start(ts[:], g.time9[bass.ds(s, 1)].rearrange("o j n -> (o j) n")).then_inc(ts_in, 16)
            later = [tab for tables in g.fast_sums[1:] for tab in tables]
            for tab in later:
                clear(tab, cleared_later)
            sp.wait_ge(cleared_later, 16 * len(later))

        @block.tensor
        def _(pe):
            def turn(s, i):
                if i == 0:
                    pe.wait_ge(ea_in, 16 * s + 16)
                pe.wait_ge(eaT_out, s * G + (i + 1))
                pe.sem_inc(tick, 1)
                for k in range(GK):
                    ins = pe.transpose(ea_ps[0:D, k * P:(k + 1) * P], ea[:, i * GK + k, :], t["ident"][0:P, 0:P])
                ins.then_inc(ea_turned, 1)

            def spread(s, i):
                if i == 0:
                    pe.wait_ge(ts_in, 16 * s + 16)
                pe.wait_ge(gate_out, s * G + (i + 1))
                pe.matmul(ts_ps[:, 0:GK * P], t["Wt9"][:], ts[:, i * GK * P:(i + 1) * GK * P],
                          start=True, stop=True).then_inc(ts_spread, 1)

            def rows_through(s):
                pe.wait_ge(sumT_out, s + 2)
                pe.wait_ge(found_out, s + 2)
                pe.matmul(row_ps[0:R, 0:C], sumT[:], t["L0_gnn_Wn2"][:], start=True, stop=True).then_inc(row_ready, 1)

            def body(s, before, last):
                for i in range(G):
                    pe.wait_ge(eaT_out, s * G + (i + 2))
                    pe.wait_ge(h1_out, s * G + (i + 1))
                    pe.matmul(h1_ps[:, 0:GK * P], t["L0_gnn_We1"][:], flat(eaT, i), start=True, stop=True)\
                        .then_inc(h1_ready, 1)
                    if not last:
                        turn(s + 1, i)
                if before:
                    rows_through(s - 1)
                for i in range(G):
                    pe.wait_ge(h1_out, s * G + (i + 2))
                    pe.wait_ge(ef_out, s * G + (i + 1))
                    pe.matmul(ef_ps[:, 0:GK * P], t["L0_gnn_We2"][:], flat(h1T, i), start=True, stop=True)\
                        .then_inc(ef_ready, 1)
                    if not last:
                        spread(s + 1, i)
                for i in range(G):
                    pe.wait_ge(ef_out, s * G + (i + 2))
                    if before or i > 0:
                        pe.wait_ge(added, s * G + (i + 1 if i == 0 else i))
                    for k in range(GK):
                        ins = pe.matmul(pre_ps[i % 2][0:P, k * C:(k + 1) * C], efT[:, i * GK + k, :], t["Wn1_edge"][:],
                                        start=True, stop=True)
                    ins.then_inc(pre_ready, 1)
                pe.wait_ge(onehot, s + 1)
                pe.wait_ge(sumT_out, s + 1)
                pe.wait_ge(row_out, s + 1)
                for i in range(G):
                    pe.wait_ge(msg_ready, s * G + (i + 1))
                    for k in range(i * GK, (i + 1) * GK):
                        pe.matmul(sum_ps[:, 0:R], msg[:, k, :], ones_f[:, k, :], start=(k == 0), stop=(k == K - 1))
                        ins = pe.matmul(row_ps[0:R, C:C + 4], ones_b[:, k, :],
                                        t["first4"][:, bass.ds(s * K + k, 1), :].rearrange("p o j -> p (o j)"),
                                        start=(k == 0), stop=(k == K - 1))
                ins.then_inc(summed, 1)

            pe.sem_inc(row_out, 1)
            for i in range(G):
                turn(0, i)
                spread(0, i)
            edge_loop(pe, S, body, 2)
            rows_through(S - 1)

        @block.scalar
        def _(act):
            def turned_out(s, i):
                act.wait_ge(ea_turned, s * G + (i + 1))
                act.copy(flat(eaT, i), ea_ps[0:D, 0:GK * P]).then_inc(eaT_out, 1)

            def gate(s, i, before):
                act.wait_ge(ts_spread, s * G + (i + 1))
                if before:
                    act.wait_ge(ef_out, (s - 1) * G + (i + 2))
                act.activation(flat(gateT, i), ts_ps[:, 0:GK * P], ACT.Sigmoid, bias=t["L0_gnn_bt"][:, 0:1])\
                    .then_inc(gate_out, 1)

            def rows_out(s, before):
                act.wait_ge(row_ready, s + 1)
                if before:
                    act.wait_ge(scattered, s_base + 16 * s)
                act.copy(out_rows[:, 0:C], row_ps[0:R, 0:C]).then_inc(row_out, 1)

            def body(s, before, last):
                for i in range(G):
                    act.wait_ge(h1_ready, s * G + (i + 1))
                    act.activation(flat(h1T, i), h1_ps[:, 0:GK * P], ACT.Relu, bias=t["L0_gnn_be1"][:, 0:1])\
                        .then_inc(h1_out, 1)
                    if not last:
                        turned_out(s + 1, i)
                if before:
                    rows_out(s - 1, before > 1)
                if not last:
                    for i in range(G):
                        gate(s + 1, i, True)
                for i in range(G):
                    act.wait_ge(added, s * G + (i + 2))
                    act.activation(msg[:, grp(i), :], xa[:, grp(i), :], ACT.Relu).then_inc(msg_ready, 1)
                act.wait_ge(summed, s + 1)
                act.copy(sumT[:], sum_ps[:, 0:R]).then_inc(sumT_out, 1)

            for x in (eaT_out, gate_out, h1_out, sumT_out):
                act.sem_inc(x, 1)
            for i in range(G):
                turned_out(0, i)
                gate(0, i, False)
            edge_loop(act, S, body, 2)
            rows_out(S - 1, True)

        @block.vector
        def _(dve):
            def nodes_out(s, before):
                dve.wait_ge(summed, s + 1)
                dve.tensor_copy(found[:], row_ps[0:R, C:C + 4]).then_inc(found_out, 1)
                dve.wait_ge(found_out, s + 2)
                c = s * 4
                dve.tensor_scalar(spare[:], found[:, 2:3], -1.0, 1.0, ALU.mult, ALU.add).then_inc(chain, 1)
                dve.wait_ge(chain, c + 1)
                dve.scalar_tensor_tensor(out=spare[:], in0=spare[:], scalar=t["trash"][0:R, 0:1], in1=found[:, 0:1],
                                         op0=ALU.mult, op1=ALU.add).then_inc(chain, 1)
                dve.wait_ge(chain, c + 2)
                dve.tensor_tensor(spare[:], spare[:], found[:, 1:2], ALU.add).then_inc(chain, 1)
                dve.wait_ge(chain, c + 3)
                if before:
                    dve.wait_ge(scattered, s_base + 16 * s)
                dve.tensor_copy(out_rows[:, C:C + 1], found[:, 3:4])
                dve.tensor_copy(t["node_i"][:, bass.ds(s, 1)], spare[:]).then_inc(chain, 1)
                dve.wait_ge(chain, c + 4)
                dve.tensor_copy(node_slot[:], spare[:]).then_inc(slot_ready, 1)

            def body(s, before, last):
                if before:
                    dve.wait_ge(summed, s)
                rank = t["rank_f"][:, bass.ds(s, 1), :].rearrange("p o k -> p (o k)")
                dve.tensor_tensor(ones_f[:], rows(t["iota_r"][:], K), bcast(rank, R), ALU.is_equal)
                dve.tensor_tensor(ones_b[:], rows(t["iota_r"][:], K), bcast(rank, R), ALU.is_equal).then_inc(onehot, 1)
                if before:
                    nodes_out(s - 1, before > 1)
                for i in range(G):
                    dve.wait_ge(ef_ready, s * G + (i + 1))
                    dve.wait_ge(gate_out, s * G + (i + 2))
                    dve.scalar_tensor_tensor(out=flat(efT, i), in0=ef_ps[:, 0:GK * P], scalar=t["L0_gnn_be2"][:, 0:1],
                                             in1=flat(gateT, i), op0=ALU.add, op1=ALU.mult).then_inc(ef_out, 1)
                for i in range(G):
                    dve.wait_ge(pre_ready, s * G + (i + 1))
                    dve.wait_ge(arrived[i], 16 * GK * s + (a_base + 16 * GK))
                    dve.tensor_tensor(flat(xa, i), pre_ps[i % 2][0:P, 0:GK * C], flat(xa, i), ALU.add).then_inc(added, 1)
                    if not last:
                        dve.tensor_copy(xa_slot[:, grp(i)], t["src_i"][:, bass.ds(s + 1, 1), grp(i)]
                                        .rearrange("p o k -> p (o k)")).then_inc(staged, 1)

            dve.memset(out_rows[:], 0.0)
            for x in (ef_out, added, found_out):
                dve.sem_inc(x, 1)
            for i in range(G):
                dve.tensor_copy(xa_slot[:, grp(i)], t["src_i"][:, 0, grp(i)]).then_inc(staged, 1)
            edge_loop(dve, S, body, 2)
            nodes_out(S - 1, True)

        @block.gpsimd
        def _(pool):
            def gather(s, i, before):
                pool.wait_ge(staged, s * G + (i + 1))
                if before:
                    pool.wait_ge(msg_ready, (s - 1) * G + (i + 1))
                pool.sem_inc(pool_tick, 1)
                for k in range(i * GK, (i + 1) * GK):
                    pool.indirect_dma_start(out=xa[:, k, :], out_offset=None, in_=g.xa[:, :],
                                            in_offset=bass.IndirectOffsetOnAxis(ap=xa_slot[:, k:k + 1], axis=0))\
                        .then_inc(arrived[i], 16)

            def scatter(s, before):
                pool.wait_ge(slot_ready, s + 1)
                pool.wait_ge(row_out, s + 2)
                if before:
                    pool.wait_ge(scattered, s_base + 16 * s)
                pool.sem_inc(pool_tick, 1)
                pool.indirect_dma_start(out=table[:, :], out_offset=bass.IndirectOffsetOnAxis(ap=node_slot[:], axis=0),
                                        in_=out_rows[:], in_offset=None, compute_op=ALU.add).then_inc(scattered, 16)

            def body(s, before, last):
                for i in range(G):
                    if not last:
                        gather(s + 1, i, True)
                    if i == 3 and before:
                        scatter(s - 1, before > 1)

            pool.wait_ge(cleared, 16)
            for i in range(G):
                gather(0, i, False)
            edge_loop(pool, S, body, 2)
            scatter(S - 1, True)
            pool.wait_ge(scattered, s_base + 16 * S)
    g.clear_semaphores()


class Expand:

    def __init__(self, g, ph, table):
        nc, self.g, self.table = g.nc, g, table
        sb = lambda name, shape, dt=F32: ph.enter_context(g.sbuf(name, shape, dt))
        self.rank_row, self.onehotT = sb("rank_row", [R, K * P], BF16), sb("onehotT", [R, K, P], BF16)
        self.got, self.slot = sb("rows_got", [R, 3 * C], BF16), sb("rows_slot", [R, 1], I32)
        self.ps = [ph.enter_context(g.psum(f"spread_ps{b}", [P, 512], F32)) for b in range(2)]
        sem = lambda name: g.sem(ph, name)
        self.row_in, self.ready, self.spread, self.used = sem("rank_in"), sem("onehotT_ready"), sem("rows_spread"), sem("rows_used")
        self.staged, self.tick = sem("rows_staged"), sem("rows_tick")
        self.arrived, self.base = g.arrived[1][0], g.window_arrived
        g.window_arrived += 16 * g.S

    def load(self, sp, s, before=True):
        if before:
            sp.wait_ge(self.ready, s * G)
        sp.dma_start(self.rank_row[:], self.g.rank_rows[bass.ds(s, 1), :].rearrange("o n -> (o n)").partition_broadcast(R))\
            .then_inc(self.row_in, 16)

    def onehot(self, dve, s, i, before=True):
        if i == 0:
            dve.wait_ge(self.row_in, 16 * s + 16)
        if before:
            dve.wait_ge(self.spread, (s - 1) * G + (i + 1))
        dve.tensor_scalar(self.onehotT[:, i * GK:(i + 1) * GK, :].rearrange("r k p -> r (k p)"),
                          self.rank_row[:, i * GK * P:(i + 1) * GK * P], self.g.t["part_f"][0:R, 0:1], None, ALU.is_equal)\
            .then_inc(self.ready, 1)

    def stage(self, dve, s, before=True):
        if before:
            dve.wait_ge(self.arrived, self.base + 16 * s)
        dve.tensor_copy(self.slot[:], self.g.t["node_i"][:, bass.ds(s, 1)]).then_inc(self.staged, 1)

    def gather(self, pool, s, before=True):
        pool.wait_ge(self.staged, s + 1)
        if before:
            pool.wait_ge(self.spread, s * G)
        pool.sem_inc(self.tick, 1)
        pool.indirect_dma_start(out=self.got[:], out_offset=None, in_=self.table[:, :],
                                in_offset=bass.IndirectOffsetOnAxis(ap=self.slot[:], axis=0)).then_inc(self.arrived, 16)

    def product(self, pe, s, i, before):
        if i == 0:
            pe.wait_ge(self.arrived, 16 * s + (self.base + 16))
        pe.wait_ge(self.ready, s * G + (i + 1))
        if before or i > 0:
            pe.wait_ge(self.used, s * G + (i + 1 if i == 0 else i))
        for k in range(GK):
            for j in range(3):
                ins = pe.matmul(self.ps[i % 2][:, k * C:(k + 1) * C], self.onehotT[:, i * GK + k, :],
                                self.got[:, j * C:(j + 1) * C], start=(j == 0), stop=(j == 2))
        ins.then_inc(self.spread, 1)


class Counts:

    def __init__(self, g, ph, half):
        self.g, self.half, self.n = g, half, HALF[half] * R
        sb = lambda name, shape, dt=F16: ph.enter_context(g.sbuf(name, shape, dt))
        self.block, self.cell = sb("block_ones", [P, K, P]), sb("cell_ones", [P, K, self.n])
        self.out = sb("counts", [P, self.n])
        self.ps = ph.enter_context(g.psum("counts_ps", [P, 2, 512], F32))
        sem = lambda name: g.sem(ph, name)
        self.ready, self.summed, self.copied, self.stored = sem("cells_ready"), sem("cells_summed"), sem("counts_out"), sem("counts_stored")

    def onehots(self, dve, s, i, before):
        t = self.g.t
        if before:
            dve.wait_ge(self.summed, (s - 1) * G + (i + 1))
        for k in range(i * GK, (i + 1) * GK):
            at = bass.ds(s, 1)
            dve.tensor_scalar(self.block[:, k, :], t["iota_h"][:, 0:P],
                              t["block_f"][:, at, k:k + 1].rearrange("p o k -> p (o k)"), None, ALU.is_equal)
            ins = dve.tensor_scalar(self.cell[:, k, :], t["iota_h"][:, 0:self.n],
                                    t["cell_f"][:, at, k:k + 1].rearrange("p o k -> p (o k)"),
                                    None, ALU.is_equal)
        ins.then_inc(self.ready, 1)

    def products(self, pe, s, i):
        m = self.n // 2
        pe.wait_ge(self.ready, s * G + (i + 1))
        if i == 0:
            pe.wait_ge(self.copied, s + 1)
        for k in range(i * GK, (i + 1) * GK):
            for b in range(2):
                ins = pe.matmul(self.ps[:, b, 0:m], self.block[:, k, :], self.cell[:, k, b * m:(b + 1) * m],
                                start=(k == 0), stop=(k == K - 1))
        ins.then_inc(self.summed, 1)

    def copy_out(self, act, s, before):
        act.wait_ge(self.summed, s * G + G)
        if before:
            act.wait_ge(self.stored, 16 * s)
        act.copy(self.out[:].rearrange("p (b m) -> p b m", b=2), self.ps[:, :, 0:self.n // 2]).then_inc(self.copied, 1)

    def store(self, sp, s):
        at = R * HALF[0] * self.half
        sp.wait_ge(self.copied, s + 2)
        sp.dma_start(self.g.counts[bass.ds(s, 1), :, at:at + self.n].rearrange("o p n -> (o p) n"), self.out[:])\
            .then_inc(self.stored, 16)


def shift_cells(g):
    on_vector(g, [("dve", lambda e: e.tensor_scalar(g.t["cell_f"][:], g.t["cell_f"][:], -float(HALF[0] * R), None,
                                                    ALU.add))])


def fast_l1_scores(g):
    nc, S, t = g.nc, g.S, g.t
    with ExitStack() as ph:
        sb = lambda name, shape, dt=F32: ph.enter_context(g.sbuf(name, shape, dt))
        sem = lambda name: g.sem(ph, name)
        ex, ct = Expand(g, ph, g.k3), Counts(g, ph, 0)
        q, q_slot = sb("q_got", [P, K, C]), sb("q_slot", [P, K], I32)
        row, hidT, dots = sb("len_row", [9, K * P], BF16), sb("hidT", [C, K, P]), sb("dots", [P, K, H])
        prod = sb("prod", [P, GK, C])
        len_ps = ph.enter_context(g.psum("len_ps", [C, 512], F32))
        bias_ps = ph.enter_context(g.psum("bias_ps", [P, GK, H], F32))
        row_in, spread, hid_out, bias_ready = sem("row_in"), sem("len_spread"), sem("hid_out"), sem("bias_ready")
        chain, scored, staged, tick = sem("chain"), sem("scored"), sem("staged"), sem("pool_tick")
        arrived, a_base = g.arrived[0], g.arrived_so_far[0]
        g.arrived_so_far[0] += 16 * GK * S
        block = ph.enter_context(nc.Block())
        grp = lambda i: slice(i * GK, (i + 1) * GK)

        @block.sync
        def _(sp):
            def body(s, before, last):
                if not last:
                    sp.wait_ge(spread, (s + 1) * G)
                    sp.dma_start(row[:], g.len9[bass.ds(s + 1, 1)].rearrange("o j n -> (o j) n")).then_inc(row_in, 16)
                    ex.load(sp, s + 1)
                ct.store(sp, s)

            sp.dma_start(row[:], g.len9[0]).then_inc(row_in, 16)
            ex.load(sp, 0, False)
            edge_loop(sp, S, body, 1)
            sp.wait_ge(ct.stored, 16 * S)

        @block.tensor
        def _(pe):
            def spread_len(s, i):
                if i == 0:
                    pe.wait_ge(row_in, 16 * s + 16)
                pe.wait_ge(hid_out, s * G + (i + 1))
                pe.matmul(len_ps[:, 0:GK * P], t["We1_9"][:], row[:, i * GK * P:(i + 1) * GK * P],
                          start=True, stop=True).then_inc(spread, 1)

            def body(s, before, last):
                for i in range(G):
                    ex.product(pe, s, i, before)
                    pe.wait_ge(hid_out, s * G + (i + 2))
                    pe.wait_ge(scored, s * G + (i + 1))
                    for k in range(GK):
                        pe.matmul(bias_ps[:, k, :], hidT[:, i * GK + k, :], t["L1_gnn_We2_T"][:], start=True, stop=False)
                        ins = pe.matmul(bias_ps[:, k, :], t["ones_b"][:], t["be2_3"][:], start=False, stop=True)
                    ins.then_inc(bias_ready, 1)
                for i in range(G):
                    ct.products(pe, s, i)
                    if not last:
                        spread_len(s + 1, i)

            for i in range(G):
                spread_len(0, i)
            edge_loop(pe, S, body, 1)

        @block.scalar
        def _(act):
            def hidden(s, i):
                act.wait_ge(spread, s * G + (i + 1))
                act.activation(hidT[:, grp(i), :].rearrange("c k p -> c (k p)"), len_ps[:, 0:GK * P],
                               ACT.Silu, bias=t["L1_gnn_be1"][:, 0:1]).then_inc(hid_out, 1)

            def body(s, before, last):
                if not last:
                    for i in range(G):
                        hidden(s + 1, i)
                ct.copy_out(act, s, before)

            act.sem_inc(hid_out, 1)
            act.sem_inc(ct.copied, 1)
            for i in range(G):
                hidden(0, i)
            edge_loop(act, S, body, 1)

        @block.vector
        def _(dve):
            def body(s, before, last):
                if not last:
                    ex.stage(dve, s + 1)
                for i in range(G):
                    n = s * G + i
                    ct.onehots(dve, s, i, before)
                    dve.wait_ge(ex.spread, n + 1)
                    dve.wait_ge(arrived[i], 16 * GK * s + (a_base + 16 * GK))
                    dve.tensor_tensor(prod[:], q[:, grp(i), :],
                                      ex.ps[i % 2][:, 0:GK * C].rearrange("p (k c) -> p k c", k=GK), ALU.mult)\
                        .then_inc(ex.used, 1)
                    if not last:
                        dve.tensor_copy(q_slot[:, grp(i)], t["src_i"][:, bass.ds(s + 1, 1), grp(i)]
                                        .rearrange("p o k -> p (o k)")).then_inc(staged, 1)
                    dve.wait_ge(ex.used, n + 2)
                    dve.tensor_reduce(dots[:, grp(i), :].rearrange("p k h -> p (k h)"),
                                      prod[:].rearrange("p k (h d) -> p (k h) d", h=H), AX, ALU.add).then_inc(chain, 1)
                    if not last:
                        ex.onehot(dve, s + 1, i)
                    dve.wait_ge(chain, 2 * n + 1)
                    dve.wait_ge(bias_ready, n + 1)
                    dve.scalar_tensor_tensor(out=dots[:, grp(i), :], in0=dots[:, grp(i), :],
                                             scalar=float((C // H) ** -0.5), in1=bias_ps[:],
                                             op0=ALU.mult, op1=ALU.add).then_inc(scored, 1)
                    dve.wait_ge(scored, n + 2)
                    dve.tensor_tensor(g.scores[:, bass.ds(s * K + i * GK, GK), :], dots[:, grp(i), :],
                                      bcast(g.cut[:, bass.ds(s * K + i * GK, GK)], H), ALU.mult).then_inc(chain, 1)
                    dve.wait_ge(chain, 2 * n + 2)

            dve.sem_inc(scored, 1)
            dve.sem_inc(ex.used, 1)
            for i in range(G):
                dve.tensor_copy(q_slot[:, grp(i)], t["src_i"][:, 0, grp(i)]).then_inc(staged, 1)
                ex.onehot(dve, 0, i, False)
            ex.stage(dve, 0, False)
            edge_loop(dve, S, body, 1)

        @block.gpsimd
        def _(pool):
            def gather(s, i, before):
                pool.wait_ge(staged, s * G + (i + 1))
                if before:
                    pool.wait_ge(ex.used, (s - 1) * G + (i + 2))
                pool.sem_inc(tick, 1)
                for k in range(i * GK, (i + 1) * GK):
                    pool.indirect_dma_start(out=q[:, k, :], out_offset=None, in_=g.q[:, :],
                                            in_offset=bass.IndirectOffsetOnAxis(ap=q_slot[:, k:k + 1], axis=0))\
                        .then_inc(arrived[i], 16)

            def body(s, before, last):
                if not last:
                    for i in range(G):
                        gather(s + 1, i, True)
                        if i == 3:
                            ex.gather(pool, s + 1)

            ex.gather(pool, 0, False)
            for i in range(G):
                gather(0, i, False)
            edge_loop(pool, S, body, 1)
    g.clear_semaphores()


def fast_l1_messages(g):
    nc, S, t = g.nc, g.S, g.t
    tables = g.fast_sums[1]
    T = len(tables)
    assert T == GK
    with ExitStack() as ph:
        sb = lambda name, shape, dt=F32: ph.enter_context(g.sbuf(name, shape, dt))
        sem = lambda name: g.sem(ph, name)
        ex, ct = Expand(g, ph, g.v3), Counts(g, ph, 1)
        below, expd = sb("below", [P, K, H]), sb("expd", [P, K, H])
        key_slot, late, once = sb("key_slot", [P, K]), sb("late", [P, K]), sb("once", [P, K], I32)
        same, junk, shift = sb("same", [P, K, P]), sb("junk", [P, K, P]), sb("shift", [P, K])
        msg, tile_sums = sb("msg", [P, K, W]), sb("tile_sums", [P, K, W])
        key_ps = ph.enter_context(g.psum("key_ps", [P, GK + 1, 128], F32))
        sum_ps = [ph.enter_context(g.psum(f"sum_ps{b}", [P, 512], F32)) for b in range(2)]
        exp_in, exp_out, staged, key_rows = sem("exp_in"), sem("exp_out"), sem("staged"), sem("key_rows")
        compared, chain, once_ready = sem("compared"), sem("chain"), sem("once_ready")
        summed, sums_out, tick, w_out = sem("summed"), sem("sums_out"), sem("pool_tick"), sem("w_out")
        scattered, s_base = g.scattered, list(g.scatters)
        for u in range(T):
            g.scatters[u] += 16 * G * S
        block = ph.enter_context(nc.Block())
        grp = lambda i: slice(i * GK, (i + 1) * GK)

        def sent(eng, s, i):
            for u in range(T):
                eng.wait_ge(scattered[u], 16 * G * (s - 1) + (s_base[u] + 16 * (i + 1)))

        @block.sync
        def _(sp):
            def body(s, before, last):
                if not last:
                    ex.load(sp, s + 1)
                ct.store(sp, s)

            ex.load(sp, 0, False)
            edge_loop(sp, S, body, 1)
            sp.wait_ge(ct.stored, 16 * S)

        @block.tensor
        def _(pe):
            def body(s, before, last):
                for i in range(G):
                    if i == 0:
                        pe.wait_ge(staged, s + 1)
                    pe.wait_ge(compared, 2 * G * s + 2 * i + 1)
                    for k in range(GK):
                        ins = pe.transpose(key_ps[:, k, 0:P],
                                           key_slot[:, i * GK + k:i * GK + k + 1].to_broadcast([P, P]),
                                           t["ident"][0:P, 0:P])
                    ins.then_inc(key_rows, 1)
                    ex.product(pe, s, i, before)
                for i in range(G):
                    pe.wait_ge(compared, 2 * G * s + 2 * i + 2)
                    pe.wait_ge(ex.used, s * G + (i + 2))
                    if before or i > 0:
                        pe.wait_ge(sums_out, s * G + (i + 1 if i == 0 else i))
                    for k in range(GK):
                        ins = pe.matmul(sum_ps[i % 2][0:P, k * W:(k + 1) * W], same[:, i * GK + k, :],
                                        msg[:, i * GK + k, :], start=True, stop=True)
                    ins.then_inc(summed, 1)
                    ct.products(pe, s, i)

            edge_loop(pe, S, body, 1)

        @block.scalar
        def _(act):
            def weights(s):
                act.wait_ge(exp_in, s + 1)
                act.activation(expd[:], below[:], ACT.Exp).then_inc(exp_out, 1)

            def body(s, before, last):
                for i in range(G):
                    act.wait_ge(summed, s * G + (i + 1))
                    if before:
                        sent(act, s, i)
                    act.copy(tile_sums[:, grp(i), :].rearrange("p k w -> p (k w)"), sum_ps[i % 2][0:P, 0:GK * W])\
                        .then_inc(sums_out, 1)
                if not last:
                    weights(s + 1)
                ct.copy_out(act, s, before)

            act.sem_inc(sums_out, 1)
            act.sem_inc(ct.copied, 1)
            weights(0)
            edge_loop(act, S, body, 1)

        @block.vector
        def _(dve):
            def shifted(s):
                dve.tensor_tensor(below[:], g.scores[:, bass.ds(s * K, K), :], rows(g.top[:], K), ALU.subtract)\
                    .then_inc(exp_in, 1)

            def body(s, before, last):
                if before:
                    dve.wait_ge(summed, s * G)
                dve.tensor_copy(key_slot[:], t["src_f"][:, bass.ds(s, 1), :].rearrange("p o k -> p (o k)"))\
                    .then_inc(staged, 1)
                dve.wait_ge(exp_out, s + 1)
                dve.tensor_copy(msg[:, :, C:W], expd[:]).then_inc(w_out, 1)
                dve.wait_ge(staged, s + 1)
                if not last:
                    ex.stage(dve, s + 1)
                for i in range(G):
                    n = s * G + i
                    dve.wait_ge(key_rows, n + 1)
                    dve.tensor_tensor(same[:, grp(i), :], key_ps[:, 0:GK, 0:P], bcast(key_slot[:, grp(i)], P),
                                      ALU.is_equal).then_inc(compared, 1)
                    dve.wait_ge(compared, 2 * n + 2)
                    for k in range(i * GK, (i + 1) * GK):
                        ins = dve.scalar_tensor_tensor(out=junk[:, k, :], in0=same[:, k, :], scalar=1.0, in1=t["lower"][:],
                                                       op0=ALU.mult, op1=ALU.mult, accum_out=late[:, k:k + 1])
                    ins.then_inc(compared, 1)
                    dve.wait_ge(ex.spread, n + 1)
                    dve.tensor_tensor(
                        msg[:, grp(i), 0:C].rearrange("p k (h d) -> p k h d", h=H),
                        ex.ps[i % 2][:, 0:GK * C].rearrange("p (k h d) -> p k h d", k=GK, h=H),
                        expd[:, grp(i), :].unsqueeze(3).to_broadcast([P, GK, H, C // H]), ALU.mult).then_inc(ex.used, 1)
                    if not last:
                        ex.onehot(dve, s + 1, i)
                    ct.onehots(dve, s, i, before)
                c = s * 2
                dve.wait_ge(compared, 2 * G * s + (2 * G + 1))
                dve.tensor_scalar(late[:], late[:], 1.0, None, ALU.min).then_inc(chain, 1)
                dve.wait_ge(chain, c + 1)
                dve.scalar_tensor_tensor(out=shift[:], in0=key_slot[:], scalar=t["trash"][:, 0:1], in1=late[:],
                                         op0=ALU.subtract, op1=ALU.mult).then_inc(chain, 1)
                dve.wait_ge(chain, c + 2)
                if before:
                    sent(dve, s, G - 1)
                dve.tensor_tensor(once[:], key_slot[:], shift[:], ALU.subtract).then_inc(once_ready, 1)
                dve.wait_ge(once_ready, s + 1)
                if not last:
                    dve.wait_ge(ex.used, s * G + (G + 1))
                    shifted(s + 1)

            dve.sem_inc(compared, 1)
            dve.sem_inc(ex.used, 1)
            shifted(0)
            for i in range(G):
                ex.onehot(dve, 0, i, False)
            ex.stage(dve, 0, False)
            edge_loop(dve, S, body, 1)

        @block.gpsimd
        def _(pool):
            def body(s, before, last):
                if not last:
                    ex.gather(pool, s + 1)
                for k in range(K):
                    u = k % T
                    if k == 0:
                        pool.wait_ge(once_ready, s + 1)
                    pool.wait_ge(sums_out, s * G + (k // GK + 2))
                    if before or k >= T:
                        pool.wait_ge(scattered[u], 16 * G * s + (s_base[u] + 16 * (k // GK)))
                    pool.sem_inc(tick, 1)
                    pool.indirect_dma_start(out=tables[u][:, :],
                                            out_offset=bass.IndirectOffsetOnAxis(ap=once[:, k:k + 1], axis=0),
                                            in_=tile_sums[:, k, :], in_offset=None, compute_op=ALU.add)\
                        .then_inc(scattered[u], 16)

            ex.gather(pool, 0, False)
            edge_loop(pool, S, body, 1)
            for u in range(T):
                pool.wait_ge(scattered[u], s_base[u] + 16 * G * S)
    g.clear_semaphores()


def split_features(g, x, parts):
    left = parts[3]
    step = lambda f: ("dve", f)
    on_vector(g, [
        step(lambda e: e.tensor_copy(parts[0], x)),
        step(lambda e: e.tensor_tensor(left, x, parts[0], ALU.subtract)),
        step(lambda e: e.tensor_copy(parts[1], left)),
        step(lambda e: e.tensor_tensor(left, left, parts[1], ALU.subtract)),
        step(lambda e: e.tensor_copy(parts[2], left)),
    ])


def fast_sum_neighbours(g, x3, weight, tables):
    nc, S, NB, t = g.nc, g.S, g.NB, g.t
    WB = 5
    CB = 5
    steps, chunks = S // WB, NB // CB
    T = len(tables)
    assert S % WB == 0 and NB % CB == 0
    with ExitStack() as ph:
        sb = lambda name, shape, dt=F32: ph.enter_context(g.sbuf(name, shape, dt))
        sem = lambda name: g.sem(ph, name)
        counts = sb("counts_in", [P, WB, NB * R], F16)
        aggT, out_rows, slot = sb("aggT", [C, WB * R]), sb("agg_rows", [R, WB, C]), sb("agg_slot", [R, WB], I32)
        agg_ps = [ph.enter_context(g.psum(f"agg_ps{b}", [C, 512], F32)) for b in range(1)]
        row_ps = ph.enter_context(g.psum("agg_row_ps", [R, 2, 512], F32))
        loaded = [sem(f"counts_loaded{c}") for c in range(chunks)]
        used, agg_out, row_ready, row_out = sem("counts_used"), sem("agg_out"), sem("agg_row_ready"), sem("agg_row_out")
        staged, tick = sem("agg_staged"), sem("agg_tick")
        scattered, s_base = g.scattered, list(g.scatters)
        turns = [len(range(u, WB, T)) for u in range(T)]
        for u in range(T):
            g.scatters[u] += 16 * turns[u] * steps
        block = ph.enter_context(nc.Block())

        def sent(eng, s):
            for u in range(T):
                eng.wait_ge(scattered[u], 16 * turns[u] * s + s_base[u])

        @block.sync
        def _(sp):
            def body(s, before, last):
                for c in range(chunks):
                    if before:
                        sp.wait_ge(used, (s - 1) * chunks + (c + 1))
                    at = slice(c * CB * R, (c + 1) * CB * R)
                    sp.dma_start(counts[:, :, at], g.counts[bass.ds(s * WB, WB), :, at].rearrange("w p n -> p w n"))\
                        .then_inc(loaded[c], 16)

            edge_loop(sp, steps, body, 1)

        @block.tensor
        def _(pe):
            def body(s, before, last):
                pe.wait_ge(agg_out, s + 1)
                for c in range(chunks):
                    pe.wait_ge(loaded[c], 16 * s + 16)
                    for j in range(c * CB, (c + 1) * CB):
                        for part in range(3):
                            ins = pe.matmul(agg_ps[0][:, 0:WB * R], x3[:, j, part, :], counts[:, :, j * R:(j + 1) * R],
                                            start=(j == 0 and part == 0), stop=(j == NB - 1 and part == 2))
                    ins.then_inc(used, 1)
                pe.wait_ge(agg_out, s + 2)
                pe.wait_ge(row_out, s + 1)
                for w in range(WB):
                    ins = pe.matmul(row_ps[:, w // 4, (w % 4) * C:(w % 4 + 1) * C], aggT[:, w * R:(w + 1) * R], weight[:],
                                    start=True, stop=True)
                ins.then_inc(row_ready, 1)

            edge_loop(pe, steps, body, 1)

        @block.vector
        def _(dve):
            def body(s, before, last):
                if before:
                    sent(dve, s)
                dve.tensor_copy(slot[:], t["node_i"][:, bass.ds(s * WB, WB)]).then_inc(staged, 1)
                dve.wait_ge(used, s * chunks + chunks)
                dve.tensor_copy(aggT[:], agg_ps[0][:, 0:WB * R]).then_inc(agg_out, 1)

            dve.sem_inc(agg_out, 1)
            edge_loop(dve, steps, body, 1)

        @block.scalar
        def _(act):
            def body(s, before, last):
                act.wait_ge(row_ready, s + 1)
                if before:
                    sent(act, s)
                act.copy(out_rows[:], row_ps[:].rearrange("r b (w c) -> r (b w) c", c=C)[:, 0:WB, :]).then_inc(row_out, 1)

            act.sem_inc(row_out, 1)
            edge_loop(act, steps, body, 1)

        @block.gpsimd
        def _(pool):
            def body(s, before, last):
                pool.wait_ge(staged, s + 1)
                pool.wait_ge(row_out, s + 2)
                for w in range(WB):
                    u = w % T
                    if before or w >= T:
                        pool.wait_ge(scattered[u], 16 * turns[u] * s + (s_base[u] + 16 * (w // T)))
                    pool.sem_inc(tick, 1)
                    pool.indirect_dma_start(out=tables[u][:, :],
                                            out_offset=bass.IndirectOffsetOnAxis(ap=slot[:, w:w + 1], axis=0),
                                            in_=out_rows[:, w, :], in_offset=None, compute_op=ALU.add)\
                        .then_inc(scattered[u], 16)

            edge_loop(pool, steps, body, 1)
            for u in range(T):
                pool.wait_ge(scattered[u], s_base[u] + 16 * turns[u] * steps)
    g.clear_semaphores()


def take_branch(g):
    with ExitStack() as ph:
        entered = g.sem(ph, "entered")
        block = ph.enter_context(g.nc.Block())

        @block.sync
        def _(sp):
            sp.sem_inc(entered, 1)

        @block.gpsimd
        def _(pool):
            pool.sem_inc(entered, 1)

        @block.scalar
        def _(act):
            act.sem_inc(entered, 1)

        @block.tensor
        def _(pe):
            pe.sem_inc(entered, 1)

        @block.vector
        def _(dve):
            dve.sem_inc(entered, 1)


def fast_gnn(g):
    nc, N, NB, S, t = g.nc, g.N, g.NB, g.S, g.t
    x, count, dinv = t["x_sb"], g.count, g.dinv
    sb = lambda c, name, shape, dt=F32: c.enter_context(g.sbuf(name, shape, dt))
    with ExitStack() as ph:
        xa = sb(ph, "xa_sb", [P, NB, C])
        node_linear(g, "xa", x, [(t["Wn1_node"], t["L0_gnn_bn1"], xa)])
        to_table(g, [(g.xa, xa)])
    g.clear_semaphores()
    fast_l0(g)
    with ExitStack() as ph:
        total = sb(ph, "total", [P, NB, W])
        scr, hid = sb(ph, "scr", [P, NB, C]), sb(ph, "hid", [P, NB, C])
        collect_sums(g, total, None, g.fast_sums[0])
        on_vector(g, [
            ("dve", lambda e: e.tensor_copy(count[:], total[:, :, C:C + 1].rearrange("p j o -> p (j o)"))),
            ("dve", lambda e: e.tensor_tensor(scr[:], bcast(count[:], C), rows(t["L0_gnn_bn2"][:], NB), ALU.mult)),
            ("dve", lambda e: e.scalar_tensor_tensor(out=scr[:], in0=x[:], scalar=2.0, in1=scr[:], op0=ALU.mult, op1=ALU.add)),
            ("dve", lambda e: e.tensor_tensor(scr[:], scr[:], total[:, :, 0:C], ALU.add)),
        ])
        layer_norm(g, scr, hid, dst=x)
    g.clear_semaphores()
    with ExitStack() as lay:
        g.scores = sb(lay, "scores", [P, S * K, H])
        g.top = sb(lay, "top", [P, H])
        with ExitStack() as ph:
            qkv = [sb(ph, n, [P, NB, C]) for n in ("q_sb", "k_sb", "v_sb")]
            left = sb(ph, "left", [P, NB, C])
            k3, v3 = sb(ph, "k3", [P, NB, 3, C], BF16), sb(ph, "v3", [P, NB, 3, C], BF16)
            node_linear(g, "qkv", x, [(t[f"L1_gnn_W{n}_T"], t[f"L1_gnn_b{n}"], o) for n, o in zip("qkv", qkv)])
            for f, parts in ((qkv[1], k3), (qkv[2], v3)):
                split_features(g, f[:], [parts[:, :, j, :] for j in range(3)] + [left[:]])
            spare = t["zeros"][:].bitcast(BF16)[:, 0:3 * C].unsqueeze(1)
            to_table(g, [(g.q, qkv[0]), (g.k3[0:N, :], k3[:].rearrange("p j a c -> p j (a c)")),
                         (g.v3[0:N, :], v3[:].rearrange("p j a c -> p j (a c)")),
                         (g.k3[N:N + P, :], spare), (g.v3[N:N + P, :], spare)])
        with ExitStack() as ph:
            g.cut = sb(ph, "cut", [P, S * K])
            cutoff(g)
            g.clear_semaphores()
            fast_l1_scores(g)
        head_maximum(g)
        shift_cells(g)
        g.clear_semaphores()
        fast_l1_messages(g)
    with ExitStack() as ph:
        attention_out(g, ph, g.fast_sums[1])
    with ExitStack() as ph:
        x3, left = sb(ph, "x3", [P, NB, 3, C], BF16), sb(ph, "left", [P, NB, C])
        split_features(g, x[:], [x3[:, :, j, :] for j in range(3)] + [left[:]])
        g.clear_semaphores()
        fast_sum_neighbours(g, x3, t["L2_gnn_w_neigh_T"], g.fast_sums[2])
    with ExitStack() as ph:
        total, scr = sb(ph, "total", [P, NB, C]), sb(ph, "scr", [P, NB, C])
        part, per = sb(ph, "part", [P, NB, C]), sb(ph, "per", [P, NB])
        collect_sums(g, total, [part], g.fast_sums[2])
        degrees(g, per)
        on_vector(g, [
            ("dve", lambda e: e.tensor_tensor(total[:], total[:], bcast(per[:], C), ALU.mult)),
            ("dve", lambda e: e.tensor_tensor(scr[:], x[:], rows(t["b_l2"][:], NB), ALU.add)),
            ("dve", lambda e: e.tensor_tensor(scr[:], scr[:], total[:], ALU.add)),
        ])
        node_linear(g, "l2s", x, [(t["L2_gnn_w_self_T"], scr, scr)])
        layer_norm(g, scr, total, dst=x)
    g.clear_semaphores()
    with ExitStack() as lay:
        xd, self_loop = sb(lay, "xd", [P, NB, C]), sb(lay, "self_loop", [P, NB, C])
        zero_row = sb(lay, "zero_row", [P, C])
        on_vector(g, [("dve", lambda e: e.memset(zero_row[:], 0.0)),
                      ("dve", lambda e: e.tensor_tensor(xd[:], x[:], bcast(dinv[:], C), ALU.mult))])
        node_linear(g, "h3", xd, [(t["L3_gnn_W"], zero_row, self_loop)])
        with ExitStack() as ph:
            x3, left = sb(ph, "x3", [P, NB, 3, C], BF16), sb(ph, "left", [P, NB, C])
            split_features(g, xd[:], [x3[:, :, j, :] for j in range(3)] + [left[:]])
            g.clear_semaphores()
            fast_sum_neighbours(g, x3, t["L3_gnn_W"], g.fast_sums[3])
        total, part = sb(lay, "total", [P, NB, C]), sb(lay, "part", [P, NB, C])
        collect_sums(g, total, [part], g.fast_sums[3])
        convolution_out(g, total[:], self_loop, part)


def gnn(nc, ins, out):
    g = Gnn(nc, ins, out)
    N, NB, S = g.N, g.NB, g.S
    table = lambda name, n, w, dt=F32: nc.dram_tensor(name, (n, w), dt, kind="Internal").ap()
    g.xa, g.q, g.k, g.v = (table(n + "_table", N, C) for n in ("xa", "q", "k", "v"))
    g.k3, g.v3 = table("k3_table", N + P, 3 * C, BF16), table("v3_table", N + P, 3 * C, BF16)
    g.x2, g.h3 = table("x2_table", N, C), table("h3_table", N, C)
    g.sums = [table(f"sums_table{u}", N + P, W) for u in range(TABLES)]
    g.fast_sums = [[table(f"fast_sums{n}_{u}", N + P, w) for u in range(m)]
                   for n, (m, w) in enumerate(((1, W), (GK, W), (2, C), (2, C)))]
    g.counts = nc.dram_tensor("counts_dram", (S, P, NB * R), F16, kind="Internal").ap()
    with ExitStack() as ctx:
        g.scattered = [ctx.enter_context(nc.semaphore(f"scattered{u}")) for u in range(TABLES)]
        g.arrived = [[ctx.enter_context(nc.semaphore(f"arrived{w}{i}")) for i in range(G)] for w in range(2)]
        load_and_lay_out(g, ctx)
        g.count = ctx.enter_context(g.sbuf("count", [P, NB], F32))
        g.dinv = ctx.enter_context(g.sbuf("dinv", [P, NB], F32))
        windows(g, ctx)
        g.clear_semaphores()
        fast = nc.values_load(g.t["fast_ok"][0:1, 0:1], min_val=0, max_val=1)
        with nc.If(fast):
            g.scattered_so_far, g.arrived_so_far = 0, [0, 0]
            g.scatters, g.window_arrived = [0] * TABLES, 0
            take_branch(g)
            fast_gnn(g)
        with nc.Else():
            g.scattered_so_far, g.arrived_so_far = 0, [0, 0]
            take_branch(g)
            general_gnn(g)
        to_table(g, [(g.out, g.t["x_sb"])])


_INS = ["x", "src", "dst", "edge_attr_64", "edge_weight", "edge_weight1",
        "L0_gnn_We1", "L0_gnn_be1", "L0_gnn_We2", "L0_gnn_be2", "L0_gnn_Wt", "L0_gnn_bt",
        "L0_gnn_Wn1", "L0_gnn_bn1", "L0_gnn_Wn2", "L0_gnn_bn2",
        "L1_gnn_Wq", "L1_gnn_bq", "L1_gnn_Wk", "L1_gnn_bk", "L1_gnn_Wv", "L1_gnn_bv",
        "L1_gnn_We1", "L1_gnn_be1", "L1_gnn_We2", "L1_gnn_be2", "L1_gnn_Wo", "L1_gnn_bo",
        "L1_gnn_ln_g", "L1_gnn_ln_b", "L2_gnn_w_self", "L2_gnn_b_self", "L2_gnn_w_neigh",
        "L2_gnn_b_neigh", "L3_gnn_W", "L3_gnn_b"]


def kernel(**inputs):
    import numpy as _np
    import concourse.bacc as _bacc
    from concourse import mybir as _mybir
    from concourse.bass_utils import run_bass_kernel_spmd as _run

    nc = _bacc.Bacc("TRN2", target_bir_lowering=False, num_devices=1)
    arrays, args = {}, {}
    for name in _INS:
        a = _np.ascontiguousarray(inputs[name])
        arrays[f"in_{name}_dram"] = a
        args[name] = nc.dram_tensor(f"in_{name}_dram", a.shape, _mybir.dt.from_np(a.dtype), kind="ExternalInput").ap()
    out = nc.dram_tensor("out_dram", inputs["x"].shape, _mybir.dt.float32, kind="ExternalOutput").ap()
    gnn(nc, args, out)
    r = _run(nc, [arrays], core_ids=[0])
    return r.results[0]["out_dram"]
```

```python
from contextlib import ExitStack

import numpy as np

import concourse.bass as bass
from concourse import mybir

F32 = mybir.dt.float32
BF16 = mybir.dt.bfloat16
F16 = mybir.dt.float16
I32 = mybir.dt.int32
ALU = mybir.AluOpType
ACT = mybir.ActivationFunctionType
AX = mybir.AxisListType.X

P = 125
K = 15
GK = 3
G = K // GK
C = 128
H = 8
W = C + H
TABLES = 5
R = 64
PARTS = (3, 6, 16)
FLAG_STEP = 9
LN_EPS = 1e-5
CUTOFF = 5.0
NORM_SCALE = 4096.0


def bcast(ap, n):
    return ap.unsqueeze(2).to_broadcast([ap.shape[0], ap.shape[1], n])


def rows(ap, a):
    return ap.unsqueeze(1).to_broadcast([ap.shape[0], a, ap.shape[1]])


def wait_count(eng, sem, n):
    if not isinstance(n, int) or n > 0:
        eng.wait_ge(sem, n)


class Gnn:

    def __init__(self, nc, ins, out):
        self.nc, self.ins, self.out = nc, ins, out
        self.N = ins["x"].shape[0]
        self.E = ins["src"].shape[0]
        self.NB = self.N // P
        self.S = self.E // (P * K)
        assert self.N == P * self.NB and self.E == P * K * self.S
        self.used, self.names = [], {}

    def unique(self, name):
        self.names[name] = self.names.get(name, 0) + 1
        return name if self.names[name] == 1 else f"{name}_{self.names[name]}"

    def sbuf(self, name, shape, dt):
        return self.nc.sbuf_tensor(self.unique(name), shape, dt)

    def psum(self, name, shape, dt):
        return self.nc.psum_tensor(self.unique(name), shape, dt)

    def sem(self, ctx, name):
        s = ctx.enter_context(self.nc.semaphore(name))
        self.used.append(s)
        return s

    def clear_semaphores(self):
        used, self.used = self.used, []
        with self.nc.Block() as block:
            @block.gpsimd
            def _(pool):
                for s in used:
                    pool.sem_clear(s)


def load_and_lay_out(g, ctx):
    nc, ins, NB, S, N = g.nc, g.ins, g.NB, g.S, g.N

    def sb(name, shape, dt=F32):
        t = ctx.enter_context(g.sbuf(name, shape, dt))
        tensors[name] = t
        return t

    tensors = {}
    g.t = tensors
    loads = []
    for name in ("L0_gnn_We1", "L0_gnn_We2", "L0_gnn_Wn2", "L3_gnn_W"):
        loads.append((sb(name, list(ins[name].shape))[:], ins[name]))
    wn1 = ins["L0_gnn_Wn1"]
    loads.append((sb("Wn1_node", [C, C])[:], wn1[0:C, :]))
    loads.append((sb("Wn1_edge", [C, C])[:], wn1[C:2 * C, :]))
    turned = {"L1_gnn_Wq": C, "L1_gnn_Wk": C, "L1_gnn_Wv": C, "L1_gnn_Wo": C,
              "L2_gnn_w_self": C, "L2_gnn_w_neigh": C, "L1_gnn_We2": H}
    for name, n in turned.items():
        loads.append((sb(name, [n, C])[:], ins[name]))
        sb(name + "_T", [C, n])
    for name in ("L0_gnn_be1", "L0_gnn_be2", "L0_gnn_bt", "L1_gnn_be1"):
        loads.append((sb(name, [C, 1])[:], ins[name].rearrange("(p o) -> p o", o=1)))
    for name in ("L0_gnn_bn1", "L0_gnn_bn2", "L1_gnn_bq", "L1_gnn_bk", "L1_gnn_bv", "L1_gnn_bo",
                 "L1_gnn_ln_g", "L1_gnn_ln_b", "L2_gnn_b_self", "L2_gnn_b_neigh", "L3_gnn_b"):
        loads.append((sb(name, [P, C])[:], ins[name].partition_broadcast(P)))
    loads.append((sb("Wt_row", [1, C])[:], ins["L0_gnn_Wt"]))
    loads.append((sb("We1_row", [1, C])[:], ins["L1_gnn_We1"].rearrange("n o -> o n")))
    loads.append((sb("be2_row", [1, H])[:], ins["L1_gnn_be2"].rearrange("(o n) -> o n", o=1)))
    loads.append((sb("x_sb", [P, NB, C])[:], ins["x"].rearrange("(p j) c -> p j c", p=P)))
    for key in ("src", "dst"):
        loads.append((sb(key + "_i", [P, S + 1, K], I32)[:, 0:S, :],
                      ins[key].rearrange("(s p k) -> p s k", p=P, k=K)))
        sb(key + "_f", [P, S, K])
        sb(key + "_once", [P, S, K], I32)
    ident = sb("ident", [C, C])
    ones = sb("ones", [C, C])
    lower = sb("lower", [P, P])
    part_i = sb("part_i", [P, 1], I32)
    trash = sb("trash", [P, 1])
    b_l2 = sb("b_l2", [P, C])
    zeros = sb("zeros", [P, 26 * W])

    with ExitStack() as ph:
        loaded = g.sem(ph, "loaded")
        pool_ready = g.sem(ph, "pool_ready")
        pool_step = g.sem(ph, "pool_step")
        turned_ps = g.sem(ph, "turned_ps")
        dve_done = g.sem(ph, "dve_done")
        turn = ph.enter_context(g.psum("turn", [C, 8, 512], F32))
        block = ph.enter_context(nc.Block())

        @block.sync
        def _(sp):
            for to, of in loads:
                sp.dma_start(to, of).then_inc(loaded, 16)
            sp.wait_ge(loaded, 16 * len(loads))

        @block.gpsimd
        def _(pool):
            pool.memset(ident[:], 0.0).then_inc(pool_step, 1)
            pool.memset(ones[:], 1.0).then_inc(pool_step, 1)
            pool.memset(lower[:], 1.0).then_inc(pool_step, 1)
            pool.memset(zeros[:], 0.0).then_inc(pool_step, 1)
            pool.wait_ge(pool_step, 4)
            pool.affine_select(out=ident[:], in_=ident[:], compare_op=ALU.not_equal, fill=1.0, base=0,
                               pattern=[[-1, C]], channel_multiplier=1).then_inc(pool_ready, 1)
            pool.affine_select(out=lower[:], in_=lower[:], compare_op=ALU.is_gt, fill=0.0, base=0,
                               pattern=[[-1, P]], channel_multiplier=1).then_inc(pool_ready, 1)
            pool.iota(part_i[:], pattern=[[0, 1]], base=N, channel_multiplier=1).then_inc(pool_ready, 1)

        @block.tensor
        def _(pe):
            pe.wait_ge(loaded, 16 * len(loads))
            pe.wait_ge(pool_ready, 3)
            for i, (name, n) in enumerate(turned.items()):
                pe.transpose(turn[:, i, 0:n], g.t[name][:], ident[0:n, 0:n]).then_inc(turned_ps, 1)

        @block.vector
        def _(dve):
            for i, (name, n) in enumerate(turned.items()):
                dve.wait_ge(turned_ps, i + 1)
                dve.tensor_copy(g.t[name + "_T"][:], turn[:, i, 0:n])
            dve.tensor_tensor(b_l2[:], g.t["L2_gnn_b_self"][:], g.t["L2_gnn_b_neigh"][:], ALU.add)
            for key in ("src", "dst"):
                dve.memset(g.t[key + "_i"][:, S, :], 0)
                dve.tensor_copy(g.t[key + "_f"][:], g.t[key + "_i"][:, 0:S, :])
            dve.tensor_copy(trash[:], part_i[:]).then_inc(dve_done, 1)
            dve.wait_ge(dve_done, 1)


def mark_duplicates(g):
    nc, S, N = g.nc, g.S, g.N
    with ExitStack() as ph:
        key_slot = ph.enter_context(g.sbuf("key_slot", [P, K], F32))
        same = ph.enter_context(g.sbuf("same", [P, GK, P], F32))
        late = ph.enter_context(g.sbuf("late", [P, K], F32))
        shift = ph.enter_context(g.sbuf("shift", [P, K], F32))
        key_ps = ph.enter_context(g.psum("key_ps", [P, GK, 128], F32))
        for key in ("dst", "src"):
            key_f, once = g.t[key + "_f"], g.t[key + "_once"]
            staged = g.sem(ph, "staged_" + key)
            rows_ready = g.sem(ph, "rows_ready_" + key)
            compared = g.sem(ph, "compared_" + key)
            chain = g.sem(ph, "chain_" + key)
            block = nc.Block()
            with block:
                @block.tensor
                def _(pe):
                    with pe.Fori(0, S) as s:
                        for i in range(G):
                            pe.wait_ge(staged, s + 1)
                            pe.wait_ge(compared, s * G + (i + 1))
                            for k in range(GK):
                                ins = pe.transpose(key_ps[:, k, 0:P],
                                                   key_slot[:, i * GK + k:i * GK + k + 1].to_broadcast([P, P]),
                                                   g.t["ident"][0:P, 0:P])
                            ins.then_inc(rows_ready, 1)

                @block.vector
                def _(dve):
                    dve.sem_inc(compared, 1)
                    per = 3 * G + 4
                    with dve.Fori(0, S) as s:
                        dve.tensor_copy(key_slot[:], key_f[:, bass.ds(s, 1), :].rearrange("p o k -> p (o k)"))\
                            .then_inc(staged, 1)
                        dve.wait_ge(staged, s + 1)
                        for i in range(G):
                            dve.wait_ge(rows_ready, s * G + (i + 1))
                            dve.tensor_tensor(same[:], key_ps[:, :, 0:P], bcast(key_slot[:, i * GK:(i + 1) * GK], P),
                                              ALU.is_equal).then_inc(chain, 1)
                            dve.wait_ge(chain, s * per + (3 * i + 1))
                            dve.tensor_tensor(same[:], same[:], rows(g.t["lower"][:], GK), ALU.mult).then_inc(chain, 1)
                            dve.wait_ge(chain, s * per + (3 * i + 2))
                            dve.tensor_reduce(late[:, i * GK:(i + 1) * GK], same[:], AX, ALU.max).then_inc(chain, 1)
                            dve.wait_ge(chain, s * per + (3 * i + 3))
                            dve.sem_inc(compared, 1)
                        dve.tensor_scalar(shift[:], key_slot[:], -1.0, g.t["trash"][:, 0:1], ALU.mult, ALU.add)\
                            .then_inc(chain, 1)
                        dve.wait_ge(chain, s * per + (3 * G + 1))
                        dve.tensor_tensor(shift[:], shift[:], late[:], ALU.mult).then_inc(chain, 1)
                        dve.wait_ge(chain, s * per + (3 * G + 2))
                        dve.tensor_tensor(late[:], shift[:], key_slot[:], ALU.add).then_inc(chain, 1)
                        dve.wait_ge(chain, s * per + (3 * G + 3))
                        dve.tensor_copy(once[:, bass.ds(s, 1), :].rearrange("p o k -> p (o k)"), late[:])\
                            .then_inc(chain, 1)
                        dve.wait_ge(chain, s * per + per)
    g.clear_semaphores()


def node_linear(g, name, src, outs):
    nc, NB = g.nc, g.NB
    B = 5
    steps = NB // B
    assert NB % B == 0 and len(outs) <= 3
    deep = 2 if len(outs) == 1 else 1
    with ExitStack() as ph:
        turned = [ph.enter_context(g.sbuf(f"{name}_turned{i}", [C, B, P], F32)) for i in range(2)]
        turn_ps = ph.enter_context(g.psum(name + "_turn_ps", [C, B + 3, 128], F32))
        out_ps = [[ph.enter_context(g.psum(f"{name}_out_ps{i}_{o}", [P, B + 3, 128], F32))
                   for o in range(len(outs))] for i in range(deep)]
        turned_ready = g.sem(ph, name + "_turned_ready")
        copied = g.sem(ph, name + "_copied")
        product_ready = g.sem(ph, name + "_product_ready")
        stored = g.sem(ph, name + "_stored")
        block = ph.enter_context(nc.Block())

        @block.tensor
        def _(pe):
            def turn(i):
                wait_count(pe, copied, i)
                for b in range(B):
                    ins = pe.transpose(turn_ps[:, b, 0:P], src[:, i * B + b, :], g.t["ident"][0:P, 0:P])
                ins.then_inc(turned_ready, 1)

            turn(0)
            for i in range(steps):
                if i + 1 < steps:
                    turn(i + 1)
                pe.wait_ge(copied, i + 1)
                wait_count(pe, stored, i + 1 - deep)
                for o, (weight, _, _) in enumerate(outs):
                    for b in range(B):
                        ins = pe.matmul(out_ps[i % deep][o][:, b, :], turned[i % 2][:, b, :], weight[:],
                                        start=True, stop=True)
                ins.then_inc(product_ready, 1)

        @block.scalar
        def _(act):
            for i in range(steps):
                act.wait_ge(turned_ready, i + 1)
                wait_count(act, product_ready, i - 1)
                act.copy(turned[i % 2][:], turn_ps[:, 0:B, 0:P]).then_inc(copied, 1)

        @block.vector
        def _(dve):
            for i in range(steps):
                dve.wait_ge(product_ready, i + 1)
                for o, (_, added, dst) in enumerate(outs):
                    more = rows(added[:], B) if len(added.shape) == 2 else added[:, i * B:(i + 1) * B, :]
                    ins = dve.tensor_tensor(dst[:, i * B:(i + 1) * B, :], out_ps[i % deep][o][:, 0:B, :], more, ALU.add)
                ins.then_inc(stored, 1)
            dve.wait_ge(stored, steps)


def to_table(g, pairs):
    with ExitStack() as ph:
        written = g.sem(ph, "written")
        block = ph.enter_context(g.nc.Block())

        @block.sync
        def _(sp):
            for table, feats in pairs:
                sp.dma_start(table.rearrange("(p j) c -> p j c", p=P), feats[:]).then_inc(written, 16)
            sp.wait_ge(written, 16 * len(pairs))


class Chain:

    def __init__(self, eng, sem):
        self.eng, self.sem, self.n = eng, sem, 0

    def __call__(self, ins):
        self.n += 1
        ins.then_inc(self.sem, 1)
        self.eng.wait_ge(self.sem, self.n)


def layer_norm(g, h, scratch, dst=None, scale=None, shift=None):
    nc, NB = g.nc, g.NB
    dst = h if dst is None else dst
    halves = [slice(0, NB // 2), slice(NB // 2, NB)]
    with ExitStack() as ph:
        m = ph.enter_context(g.sbuf("ln_m", [P, NB], F32))
        v = ph.enter_context(g.sbuf("ln_v", [P, NB], F32))
        chain = g.sem(ph, "ln_chain")
        centred, squared = g.sem(ph, "ln_centred"), g.sem(ph, "ln_squared")
        var_ready = g.sem(ph, "ln_var_ready")
        root_ready = g.sem(ph, "ln_root_ready")
        block = ph.enter_context(nc.Block())

        @block.vector
        def _(dve):
            link = Chain(dve, chain)
            for half in halves:
                link(dve.tensor_reduce(m[:, half], h[:, half, :], AX, ALU.add))
                link(dve.tensor_scalar(m[:, half], m[:, half], 1.0 / C, None, ALU.mult))
                dve.tensor_tensor(h[:, half, :], h[:, half, :], bcast(m[:, half], C), ALU.subtract).then_inc(centred, 1)
            for n, half in enumerate(halves):
                dve.wait_ge(squared, n + 1)
                link(dve.tensor_reduce(v[:, half], scratch[:, half, :], AX, ALU.add))
            dve.tensor_scalar(v[:], v[:], 1.0 / C, LN_EPS, ALU.mult, ALU.add).then_inc(var_ready, 1)
            dve.wait_ge(root_ready, 1)
            link(dve.reciprocal(m[:], v[:]))
            link(dve.tensor_tensor(dst[:], h[:], bcast(m[:], C), ALU.mult))
            if scale is not None:
                link(dve.tensor_tensor(dst[:], dst[:], rows(scale[:], NB), ALU.mult))
                link(dve.tensor_tensor(dst[:], dst[:], rows(shift[:], NB), ALU.add))

        @block.scalar
        def _(act):
            for n, half in enumerate(halves):
                act.wait_ge(centred, n + 1)
                act.activation(scratch[:, half, :], h[:, half, :], ACT.Square).then_inc(squared, 1)
            act.wait_ge(var_ready, 1)
            act.activation(v[:], v[:], ACT.Sqrt).then_inc(root_ready, 1)


def clear_tables(g):
    with ExitStack() as ph:
        cleared = g.sem(ph, "cleared")
        block = ph.enter_context(g.nc.Block())

        @block.sync
        def _(sp):
            for table in g.sums:
                sp.dma_start(table.rearrange("(p j) c -> p (j c)", p=P), g.t["zeros"][:]).then_inc(cleared, 16)
            sp.wait_ge(cleared, 16 * TABLES)


def collect_sums(g, total, scratch, tables):
    nc, NB, N = g.nc, g.NB, g.N
    with ExitStack() as ph:
        loaded = [g.sem(ph, f"sums_loaded{u}") for u in range(len(tables))]
        chain = g.sem(ph, "sums_chain")
        block = ph.enter_context(nc.Block())
        B = len(scratch) if scratch else 1

        @block.sync
        def _(sp):
            for u, table in enumerate(tables):
                to = total if u == 0 else scratch[(u - 1) % B]
                if u > B:
                    sp.wait_ge(chain, u - B)
                sp.dma_start(to[:], table[0:N, :].rearrange("(p j) c -> p j c", p=P)).then_inc(loaded[u], 16)
            sp.wait_ge(loaded[0], 16)

        @block.vector
        def _(dve):
            link = Chain(dve, chain)
            dve.wait_ge(loaded[0], 16)
            for u in range(1, len(tables)):
                dve.wait_ge(loaded[u], 16)
                link(dve.tensor_tensor(total[:], total[:], scratch[(u - 1) % B][:], ALU.add))


class Scatter:

    def __init__(self, g, ph, key):
        nc = g.nc
        self.g, self.key_f, self.once = g, g.t[key + "_f"], g.t[key + "_once"]
        sb = lambda name, shape, dt=F32: ph.enter_context(g.sbuf(name, shape, dt))
        self.key_slot = sb("key_slot", [P, K])
        self.once_slot = sb("once_slot", [P, K], I32)
        self.same = sb("same", [P, K, P])
        self.msg = sb("msg", [P, K, W])
        self.tile_sums = sb("tile_sums", [P, K, W])
        self.key_ps = ph.enter_context(g.psum("key_ps", [P, GK + 1, 128], F32))
        self.sum_ps = ph.enter_context(g.psum("sum_ps", [P, 512], F32))
        sem = lambda name: g.sem(ph, name)
        self.keys_staged, self.key_rows, self.same_ready = sem("keys_staged"), sem("key_rows"), sem("same_ready")
        self.msg_ready, self.summed, self.sums_out = sem("msg_ready"), sem("summed"), sem("sums_out")
        self.once_staged, self.rows_out, self.tick = sem("once_staged"), sem("rows_out"), sem("tick")
        self.scattered, self.base = g.scattered, g.scattered_so_far
        g.scattered_so_far += 16 * g.S * (K // TABLES)

    def stage_keys(self, dve, s):
        dve.wait_ge(self.summed, s * G + 1)
        dve.tensor_copy(self.key_slot[:], self.key_f[:, bass.ds(s, 1), :].rearrange("p o k -> p (o k)"))\
            .then_inc(self.keys_staged, 1)

    def compare(self, dve, s):
        for i in range(G):
            at = slice(i * GK, (i + 1) * GK)
            dve.wait_ge(self.key_rows, s * G + (i + 1))
            dve.wait_ge(self.keys_staged, s + 1)
            dve.tensor_tensor(self.same[:, at, :], self.key_ps[:, 0:GK, 0:P], bcast(self.key_slot[:, at], P),
                              ALU.is_equal).then_inc(self.same_ready, 1)

    def stage_once(self, dve, s):
        dve.wait_ge(self.rows_out, s + 1)
        dve.tensor_copy(self.once_slot[:], self.once[:, bass.ds(s, 1), :].rearrange("p o k -> p (o k)"))\
            .then_inc(self.once_staged, 1)

    def key_rows_and_sums(self, pe, s):
        for i in range(G):
            pe.wait_ge(self.keys_staged, s + 1)
            pe.wait_ge(self.same_ready, s * G + (i + 1))
            for k in range(GK):
                ins = pe.transpose(self.key_ps[:, k, 0:P],
                                   self.key_slot[:, i * GK + k:i * GK + k + 1].to_broadcast([P, P]),
                                   self.g.t["ident"][0:P, 0:P])
            ins.then_inc(self.key_rows, 1)
        for i in range(G):
            pe.wait_ge(self.same_ready, s * G + (i + 2))
            pe.wait_ge(self.msg_ready, s * G + (i + 1))
            pe.wait_ge(self.sums_out, s * G + (i + 1))
            for k in range(GK):
                t = i * GK + k
                ins = pe.matmul(self.sum_ps[:, k * W:(k + 1) * W], self.same[:, t, :], self.msg[:, t, :],
                                start=True, stop=True)
            ins.then_inc(self.summed, 1)

    def sums_to_sbuf(self, act, s):
        for i in range(G):
            act.wait_ge(self.summed, s * G + (i + 2))
            act.wait_ge(self.rows_out, s + 1)
            act.copy(self.tile_sums[:, i * GK:(i + 1) * GK, :].rearrange("p k w -> p (k w)"),
                     self.sum_ps[:, 0:GK * W]).then_inc(self.sums_out, 1)

    def release(self, pool, s):
        if s is not None:
            for u in range(TABLES):
                pool.wait_ge(self.scattered[u], self.base + 16 * (s * (K // TABLES)))
        pool.sem_inc(self.rows_out, 1)

    def scatter(self, pool, s):
        for k in range(K):
            u = k % TABLES
            pool.wait_ge(self.sums_out, s * G + (k // GK + 2))
            pool.wait_ge(self.once_staged, s + 1)
            if k >= TABLES:
                pool.wait_ge(self.scattered[u], self.base + 16 * (s * (K // TABLES) + k // TABLES))
            pool.sem_inc(self.tick, 1)
            pool.indirect_dma_start(out=self.g.sums[u][:, :],
                                    out_offset=bass.IndirectOffsetOnAxis(ap=self.once_slot[:, k:k + 1], axis=0),
                                    in_=self.tile_sums[:, k, :], in_offset=None, compute_op=ALU.add)\
                .then_inc(self.scattered[u], 16)

    def give_ahead(self, eng, who):
        if who == "dve":
            eng.sem_inc(self.same_ready, 1)
        if who == "act":
            eng.sem_inc(self.sums_out, 1)
        if who == "pe":
            eng.sem_inc(self.summed, 1)


class Gather:

    def __init__(self, g, ph, name, table, key, arrived=0):
        self.table, self.key_i = table, g.t[key + "_i"]
        self.slot = ph.enter_context(g.sbuf(name + "_slot", [P, K], I32))
        self.got = ph.enter_context(g.sbuf(name + "_got", [P, K, C], F32))
        self.staged = g.sem(ph, name + "_staged")
        self.used = g.sem(ph, name + "_used")
        self.tick = g.sem(ph, name + "_tick")
        self.arrived, self.base = g.arrived[arrived], g.arrived_so_far[arrived]
        g.arrived_so_far[arrived] += 16 * GK * g.S

    def stage(self, dve, s):
        dve.tensor_copy(self.slot[:], self.key_i[:, bass.ds(s, 1), :].rearrange("p o k -> p (o k)"))\
            .then_inc(self.staged, 1)

    def gather(self, pool, s):
        for k in range(K):
            if k % GK == 0:
                pool.wait_ge(self.staged, s + 1)
                pool.wait_ge(self.used, s * G + 1)
                pool.sem_inc(self.tick, 1)
            pool.indirect_dma_start(out=self.got[:, k, :], out_offset=None, in_=self.table[:, :],
                                    in_offset=bass.IndirectOffsetOnAxis(ap=self.slot[:, k:k + 1], axis=0))\
                .then_inc(self.arrived[k // GK], 16)


def edges_l0(g):
    nc, S = g.nc, g.S
    t = g.t
    ea_dram = g.ins["edge_attr_64"].rearrange("(s p k) c -> s p k c", p=P, k=K)
    ts_dram = g.ins["edge_weight"].rearrange("(s n) -> s n", n=P * K)
    D = ea_dram.shape[3]
    with ExitStack() as ph:
        sb = lambda name, shape: ph.enter_context(g.sbuf(name, shape, F32))
        ps = lambda name: ph.enter_context(g.psum(name, [C, 512], F32))
        sc = Scatter(g, ph, "dst")
        ga = Gather(g, ph, "xa", g.xa, "src")
        ea = sb("ea", [P, K, D])
        ts = sb("ts", [1, P * K])
        eaT = sb("eaT", [D, K, P])
        h1T = sb("h1T", [C, K, P])
        gateT = sb("gateT", [C, K, P])
        efT = sb("efT", [C, K, P])
        ea_ps, h1_ps, ts_ps, ef_ps, pre_ps = ps("ea_ps"), ps("h1_ps"), ps("ts_ps"), ps("ef_ps"), ps("pre_ps")
        sem = lambda name: g.sem(ph, name)
        ea_in, ea_turned, eaT_out = sem("ea_in"), sem("ea_turned"), sem("eaT_out")
        ts_in, ts_spread, gate_out = sem("ts_in"), sem("ts_spread"), sem("gate_out")
        h1_ready, h1_out, ef_ready, ef_out = sem("h1_ready"), sem("h1_out"), sem("ef_ready"), sem("ef_out")
        pre_ready, added, tick = sem("pre_ready"), sem("added"), sem("pe_tick")
        block = ph.enter_context(nc.Block())
        ts_tiles = ts[:].rearrange("o (p k) -> o k p", k=K)

        @block.sync
        def _(sp):
            with sp.Fori(0, S) as s:
                sp.wait_ge(ea_turned, s * G + 1)
                sp.dma_start(ea[:], ea_dram[bass.ds(s, 1)].rearrange("o p k c -> p (o k) c")).then_inc(ea_in, 16)
                sp.wait_ge(ts_spread, s * G + 1)
                sp.dma_start(ts[:], ts_dram[bass.ds(s, 1), :]).then_inc(ts_in, 16)

        @block.tensor
        def _(pe):
            pe.sem_inc(ea_turned, 1)
            pe.sem_inc(ts_spread, 1)
            sc.give_ahead(pe, "pe")
            with pe.Fori(0, S) as s:
                for i in range(G):
                    pe.wait_ge(ea_in, 16 * s + 16)
                    pe.wait_ge(eaT_out, s * G + (i + 1))
                    pe.sem_inc(tick, 1)
                    for k in range(GK):
                        ins = pe.transpose(ea_ps[0:D, k * P:(k + 1) * P], ea[:, i * GK + k, :], t["ident"][0:P, 0:P])
                    ins.then_inc(ea_turned, 1)
                    pe.wait_ge(ts_in, 16 * s + 16)
                    pe.wait_ge(gate_out, s * G + (i + 1))
                    pe.matmul(ts_ps[:, 0:GK * P], t["Wt_row"][:], ts_tiles[:, i * GK:(i + 1) * GK, :],
                              start=True, stop=True).then_inc(ts_spread, 1)
                for i in range(G):
                    pe.wait_ge(eaT_out, s * G + (i + 2))
                    pe.wait_ge(h1_out, s * G + (i + 1))
                    pe.matmul(h1_ps[:, 0:GK * P], t["L0_gnn_We1"][:],
                              eaT[:, i * GK:(i + 1) * GK, :].rearrange("c k p -> c (k p)"),
                              start=True, stop=True).then_inc(h1_ready, 1)
                for i in range(G):
                    pe.wait_ge(h1_out, s * G + (i + 2))
                    pe.wait_ge(ef_out, s * G + (i + 1))
                    pe.matmul(ef_ps[:, 0:GK * P], t["L0_gnn_We2"][:],
                              h1T[:, i * GK:(i + 1) * GK, :].rearrange("c k p -> c (k p)"),
                              start=True, stop=True).then_inc(ef_ready, 1)
                for i in range(G):
                    pe.wait_ge(ef_out, s * G + (i + 2))
                    pe.wait_ge(added, s * G + (i + 1))
                    for k in range(GK):
                        ins = pe.matmul(pre_ps[0:P, k * C:(k + 1) * C], efT[:, i * GK + k, :], t["Wn1_edge"][:],
                                        start=True, stop=True)
                    ins.then_inc(pre_ready, 1)
                sc.key_rows_and_sums(pe, s)

        @block.scalar
        def _(act):
            for x in (eaT_out, gate_out, h1_out):
                act.sem_inc(x, 1)
            sc.give_ahead(act, "act")
            with act.Fori(0, S) as s:
                for i in range(G):
                    at = slice(i * GK, (i + 1) * GK)
                    act.wait_ge(ea_turned, s * G + (i + 2))
                    act.copy(eaT[:, at, :].rearrange("c k p -> c (k p)"), ea_ps[0:D, 0:GK * P]).then_inc(eaT_out, 1)
                    act.wait_ge(ts_spread, s * G + (i + 2))
                    act.activation(gateT[:, at, :].rearrange("c k p -> c (k p)"), ts_ps[:, 0:GK * P], ACT.Sigmoid,
                                   bias=t["L0_gnn_bt"][:, 0:1]).then_inc(gate_out, 1)
                for i in range(G):
                    act.wait_ge(h1_ready, s * G + (i + 1))
                    act.activation(h1T[:, i * GK:(i + 1) * GK, :].rearrange("c k p -> c (k p)"), h1_ps[:, 0:GK * P],
                                   ACT.Relu, bias=t["L0_gnn_be1"][:, 0:1]).then_inc(h1_out, 1)
                for i in range(G):
                    at = slice(i * GK, (i + 1) * GK)
                    act.wait_ge(added, s * G + (i + 2))
                    act.activation(sc.msg[:, at, 0:C], ga.got[:, at, :], ACT.Relu).then_inc(sc.msg_ready, 1)
                    act.wait_ge(sc.msg_ready, s * G + (i + 1))
                    act.sem_inc(ga.used, 1)
                sc.sums_to_sbuf(act, s)

        @block.vector
        def _(dve):
            dve.sem_inc(ef_out, 1)
            dve.sem_inc(added, 1)
            dve.memset(sc.msg[:, :, C:W], 1.0)
            sc.give_ahead(dve, "dve")
            ga.stage(dve, 0)
            with dve.Fori(0, S) as s:
                sc.stage_keys(dve, s)
                for i in range(G):
                    at = slice(i * GK, (i + 1) * GK)
                    dve.wait_ge(ef_ready, s * G + (i + 1))
                    dve.wait_ge(gate_out, s * G + (i + 2))
                    dve.scalar_tensor_tensor(out=efT[:, at, :].rearrange("c k p -> c (k p)"), in0=ef_ps[:, 0:GK * P],
                                             scalar=t["L0_gnn_be2"][:, 0:1],
                                             in1=gateT[:, at, :].rearrange("c k p -> c (k p)"),
                                             op0=ALU.add, op1=ALU.mult).then_inc(ef_out, 1)
                for i in range(G):
                    at = slice(i * GK, (i + 1) * GK)
                    dve.wait_ge(pre_ready, s * G + (i + 1))
                    dve.wait_ge(ga.arrived[i], 16 * GK * s + (ga.base + 16 * GK))
                    dve.tensor_tensor(ga.got[:, at, :].rearrange("p k c -> p (k c)"), pre_ps[0:P, 0:GK * C],
                                      ga.got[:, at, :].rearrange("p k c -> p (k c)"), ALU.add).then_inc(added, 1)
                sc.compare(dve, s)
                ga.stage(dve, s + 1)
                sc.stage_once(dve, s)

        @block.gpsimd
        def _(pool):
            pool.sem_inc(ga.used, 1)
            sc.release(pool, None)
            ga.gather(pool, 0)
            ga.gather(pool, 1)
            sc.scatter(pool, 0)
            with pool.Fori(1, S - 1) as s:
                ga.gather(pool, s + 1)
                sc.release(pool, s)
                sc.scatter(pool, s)
            sc.release(pool, S - 1)
            sc.scatter(pool, S - 1)
            for u in range(TABLES):
                pool.wait_ge(sc.scattered[u], sc.base + 16 * S * (K // TABLES))
    g.clear_semaphores()


def edges_l1_scores(g):
    nc, S, t = g.nc, g.S, g.t
    len_dram = g.ins["edge_weight1"].rearrange("(s n) o -> s (n o)", n=P * K)
    with ExitStack() as ph:
        sb = lambda name, shape: ph.enter_context(g.sbuf(name, shape, F32))
        gq = Gather(g, ph, "q", g.q, "src")
        gk = Gather(g, ph, "k", g.k, "dst", arrived=1)
        row = sb("len_row", [1, P * K])
        hidT = sb("hidT", [C, K, P])
        dots = sb("dots", [P, K, H])
        len_ps = ph.enter_context(g.psum("len_ps", [C, 512], F32))
        bias_ps = ph.enter_context(g.psum("bias_ps", [P, GK, H], F32))
        sem = lambda name: g.sem(ph, name)
        row_in, spread, hid_out = sem("row_in"), sem("spread"), sem("hid_out")
        bias_ready, chain, scored = sem("bias_ready"), sem("chain"), sem("scored")
        block = ph.enter_context(nc.Block())
        row_tiles = row[:].rearrange("o (p k) -> o k p", k=K)

        @block.sync
        def _(sp):
            with sp.Fori(0, S) as s:
                sp.wait_ge(spread, s * G + 1)
                sp.dma_start(row[:], len_dram[bass.ds(s, 1), :]).then_inc(row_in, 16)

        @block.tensor
        def _(pe):
            pe.sem_inc(spread, 1)
            with pe.Fori(0, S) as s:
                for i in range(G):
                    pe.wait_ge(row_in, 16 * s + 16)
                    pe.wait_ge(hid_out, s * G + (i + 1))
                    pe.matmul(len_ps[:, 0:GK * P], t["We1_row"][:], row_tiles[:, i * GK:(i + 1) * GK, :],
                              start=True, stop=True).then_inc(spread, 1)
                for i in range(G):
                    pe.wait_ge(hid_out, s * G + (i + 2))
                    pe.wait_ge(scored, s * G + (i + 1))
                    for k in range(GK):
                        pe.matmul(bias_ps[:, k, :], hidT[:, i * GK + k, :], t["L1_gnn_We2_T"][:], start=True, stop=False)
                        ins = pe.matmul(bias_ps[:, k, :], t["ones"][0:1, 0:P], t["be2_row"][:], start=False, stop=True)
                    ins.then_inc(bias_ready, 1)

        @block.scalar
        def _(act):
            act.sem_inc(hid_out, 1)
            with act.Fori(0, S) as s:
                act.wait_ge(bias_ready, s * G + 1)
                for i in range(G):
                    act.wait_ge(spread, s * G + (i + 2))
                    act.activation(hidT[:, i * GK:(i + 1) * GK, :].rearrange("c k p -> c (k p)"), len_ps[:, 0:GK * P],
                                   ACT.Silu, bias=t["L1_gnn_be1"][:, 0:1]).then_inc(hid_out, 1)

        @block.vector
        def _(dve):
            dve.sem_inc(scored, 1)
            dve.sem_inc(bias_ready, 1)
            gq.stage(dve, 0)
            gk.stage(dve, 0)
            with dve.Fori(0, S) as s:
                for i in range(G):
                    at = slice(i * GK, (i + 1) * GK)
                    step = s * (4 * G) + 4 * i
                    dve.wait_ge(gq.arrived[i], 16 * GK * s + (gq.base + 16 * GK))
                    dve.wait_ge(gk.arrived[i], 16 * GK * s + (gk.base + 16 * GK))
                    dve.tensor_tensor(gq.got[:, at, :], gq.got[:, at, :], gk.got[:, at, :], ALU.mult).then_inc(chain, 1)
                    dve.wait_ge(chain, step + 1)
                    dve.tensor_reduce(dots[:, at, :].rearrange("p k h -> p (k h)"),
                                      gq.got[:, at, :].rearrange("p k (h d) -> p (k h) d", h=H), AX, ALU.add)\
                        .then_inc(chain, 1)
                    dve.wait_ge(chain, step + 2)
                    dve.sem_inc(gq.used, 1)
                    dve.sem_inc(gk.used, 1)
                    dve.wait_ge(bias_ready, s * G + (i + 2))
                    dve.scalar_tensor_tensor(out=dots[:, at, :], in0=dots[:, at, :], scalar=float((C // H) ** -0.5),
                                             in1=bias_ps[:], op0=ALU.mult, op1=ALU.add).then_inc(chain, 1)
                    dve.wait_ge(chain, step + 3)
                    dve.sem_inc(scored, 1)
                    dve.tensor_tensor(g.scores[:, bass.ds(s * K + i * GK, GK), :], dots[:, at, :],
                                      bcast(g.cut[:, bass.ds(s * K + i * GK, GK)], H), ALU.mult).then_inc(chain, 1)
                    dve.wait_ge(chain, step + 4)
                nxt = s + 1
                gq.stage(dve, nxt)
                gk.stage(dve, nxt)

        @block.gpsimd
        def _(pool):
            pool.sem_inc(gq.used, 1)
            pool.sem_inc(gk.used, 1)
            with pool.Fori(0, S) as s:
                gq.gather(pool, s)
                gk.gather(pool, s)
            for i in range(G):
                pool.wait_ge(gq.arrived[i], gq.base + 16 * GK * S)
                pool.wait_ge(gk.arrived[i], gk.base + 16 * GK * S)
    g.clear_semaphores()


def cutoff(g, pairs=()):
    nc, S = g.nc, g.S
    with ExitStack() as ph:
        sb = lambda name: ph.enter_context(g.sbuf(name, [P, S * K], F32))
        length, folded, inside = sb("length"), sb("folded"), sb("inside")
        periods = ph.enter_context(g.sbuf("periods", [P, S * K], I32))
        loaded, chain = g.sem(ph, "len_loaded"), g.sem(ph, "cut_chain")
        folded_ready, sin_ready, written = g.sem(ph, "folded_ready"), g.sem(ph, "sin_ready"), g.sem(ph, "tables_written")
        block = ph.enter_context(nc.Block())
        per = 2.0 * CUTOFF

        @block.sync
        def _(sp):
            sp.dma_start(length[:].rearrange("p (s k) -> p s k", k=K),
                         g.ins["edge_weight1"].rearrange("(s p k) o -> p s (k o)", p=P, k=K)).then_inc(loaded, 16)
            for table, feats in pairs:
                sp.dma_start(table.rearrange("(p j) c -> p j c", p=P), feats[:]).then_inc(written, 16)
            if pairs:
                sp.wait_ge(written, 16 * len(pairs))

        @block.vector
        def _(dve):
            link = Chain(dve, chain)
            dve.wait_ge(loaded, 16)
            link(dve.tensor_scalar(inside[:], length[:], CUTOFF, 0.5, ALU.is_lt, ALU.mult))
            link(dve.tensor_scalar(folded[:], length[:], 1.0 / per, None, ALU.mult))
            link(dve.tensor_copy(periods[:], folded[:]))
            link(dve.tensor_copy(folded[:], periods[:]))
            link(dve.scalar_tensor_tensor(out=length[:], in0=folded[:], scalar=-per, in1=length[:],
                                          op0=ALU.mult, op1=ALU.add))
            link(dve.tensor_scalar(folded[:], length[:], -1.0, None, ALU.mult))
            link(dve.tensor_tensor(folded[:], folded[:], length[:], ALU.max))
            link(dve.tensor_scalar(folded[:], folded[:], -CUTOFF, None, ALU.add))
            link(dve.tensor_scalar(length[:], folded[:], -1.0, None, ALU.mult))
            link(dve.tensor_tensor(folded[:], folded[:], length[:], ALU.max))
            dve.tensor_scalar(folded[:], folded[:], float(np.pi / CUTOFF), float(-np.pi / 2), ALU.mult, ALU.add)\
                .then_inc(folded_ready, 1)
            dve.wait_ge(sin_ready, 1)
            link(dve.tensor_scalar(folded[:], folded[:], 1.0, None, ALU.add))
            link(dve.tensor_tensor(g.cut[:], folded[:], inside[:], ALU.mult))

        @block.scalar
        def _(act):
            act.wait_ge(folded_ready, 1)
            act.activation(folded[:], folded[:], ACT.Sin).then_inc(sin_ready, 1)


def head_maximum(g):
    nc = g.nc
    with ExitStack() as ph:
        m = ph.enter_context(g.sbuf("m", [P, H], F32))
        mT = ph.enter_context(g.sbuf("mT", [H, 1], F32))
        diag = ph.enter_context(g.sbuf("diag", [H, H], F32))
        ps = ph.enter_context(g.psum("max_ps", [P, 2, 512], F32))
        dve_step, pe_step = g.sem(ph, "max_dve"), g.sem(ph, "max_pe")
        block = ph.enter_context(nc.Block())

        @block.vector
        def _(dve):
            dve.tensor_reduce(m[:], g.scores[:].rearrange("p t h -> p h t"), AX, ALU.max).then_inc(dve_step, 1)
            dve.wait_ge(pe_step, 1)
            dve.tensor_reduce(mT[:], ps[0:H, 0, 0:P], AX, ALU.max).then_inc(dve_step, 1)
            dve.wait_ge(dve_step, 2)
            dve.tensor_scalar(diag[:], g.t["ident"][0:H, 0:H], mT[:, 0:1], None, ALU.mult).then_inc(dve_step, 1)
            dve.wait_ge(pe_step, 2)
            dve.tensor_copy(g.top[:], ps[:, 1, 0:H]).then_inc(dve_step, 1)
            dve.wait_ge(dve_step, 4)

        @block.tensor
        def _(pe):
            pe.wait_ge(dve_step, 1)
            pe.transpose(ps[0:H, 0, 0:P], m[:], g.t["ident"][0:P, 0:P]).then_inc(pe_step, 1)
            pe.wait_ge(dve_step, 3)
            pe.matmul(ps[:, 1, 0:H], g.t["ones"][0:H, 0:P], diag[:], start=True, stop=True).then_inc(pe_step, 1)


def edges_simple(g, table, key_from, key_to, weighted):
    nc, S, t = g.nc, g.S, g.t
    with ExitStack() as ph:
        sc = Scatter(g, ph, key_to)
        ga = Gather(g, ph, "row", table, key_from)
        chain, exp_in, exp_out = g.sem(ph, "chain"), g.sem(ph, "exp_in"), g.sem(ph, "exp_out")
        below = ph.enter_context(g.sbuf("below", [P, K, H], F32))
        expd = ph.enter_context(g.sbuf("expd", [P, K, H], F32))
        block = ph.enter_context(nc.Block())

        @block.tensor
        def _(pe):
            sc.give_ahead(pe, "pe")
            with pe.Fori(0, S) as s:
                sc.key_rows_and_sums(pe, s)

        @block.scalar
        def _(act):
            sc.give_ahead(act, "act")
            with act.Fori(0, S) as s:
                if weighted:
                    act.wait_ge(exp_in, s + 1)
                    act.activation(expd[:], below[:], ACT.Exp).then_inc(exp_out, 1)
                sc.sums_to_sbuf(act, s)

        @block.vector
        def _(dve):
            if not weighted:
                dve.memset(sc.msg[:, :, C:W], 0.0)
            sc.give_ahead(dve, "dve")
            ga.stage(dve, 0)
            with dve.Fori(0, S) as s:
                sc.stage_keys(dve, s)
                if weighted:
                    dve.tensor_tensor(below[:], g.scores[:, bass.ds(s * K, K), :], rows(g.top[:], K), ALU.subtract)\
                        .then_inc(exp_in, 1)
                    dve.wait_ge(exp_out, s + 1)
                    dve.tensor_copy(sc.msg[:, :, C:W], expd[:]).then_inc(chain, 1)
                for i in range(G):
                    at = slice(i * GK, (i + 1) * GK)
                    dve.wait_ge(ga.arrived[i], 16 * GK * s + (ga.base + 16 * GK))
                    if weighted:
                        dve.wait_ge(chain, s + 1)
                        ins = dve.tensor_tensor(
                            sc.msg[:, at, 0:C].rearrange("p k (h d) -> p k h d", h=H),
                            ga.got[:, at, :].rearrange("p k (h d) -> p k h d", h=H),
                            expd[:, at, :].unsqueeze(3).to_broadcast([P, GK, H, C // H]), ALU.mult)
                    else:
                        ins = dve.tensor_copy(sc.msg[:, at, 0:C], ga.got[:, at, :])
                    ins.then_inc(sc.msg_ready, 1)
                    dve.wait_ge(sc.msg_ready, s * G + (i + 1))
                    dve.sem_inc(ga.used, 1)
                sc.compare(dve, s)
                ga.stage(dve, s + 1)
                sc.stage_once(dve, s)

        @block.gpsimd
        def _(pool):
            pool.sem_inc(ga.used, 1)
            sc.release(pool, None)
            ga.gather(pool, 0)
            ga.gather(pool, 1)
            sc.scatter(pool, 0)
            with pool.Fori(1, S - 1) as s:
                ga.gather(pool, s + 1)
                sc.release(pool, s)
                sc.scatter(pool, s)
            sc.release(pool, S - 1)
            sc.scatter(pool, S - 1)
            for u in range(TABLES):
                pool.wait_ge(sc.scattered[u], sc.base + 16 * S * (K // TABLES))
    g.clear_semaphores()


def on_vector(g, steps):
    with ExitStack() as ph:
        done = g.sem(ph, "step_done")
        block = ph.enter_context(g.nc.Block())

        @block.vector
        def _(dve):
            for n, (who, f) in enumerate(steps):
                if who == "dve":
                    if n:
                        dve.wait_ge(done, n)
                    f(dve).then_inc(done, 1)
            dve.wait_ge(done, len(steps))

        @block.scalar
        def _(act):
            for n, (who, f) in enumerate(steps):
                if who == "act":
                    if n:
                        act.wait_ge(done, n)
                    f(act).then_inc(done, 1)


def attention_out(g, ph, tables):
    nc, NB, t = g.nc, g.NB, g.t
    x = t["x_sb"]
    sb = lambda name, shape: ph.enter_context(g.sbuf(name, shape, F32))
    total = sb("total", [P, NB, W])
    part = [sb(f"part{i}", [P, NB, W]) for i in range(2)]
    hid, scr, den = sb("hid", [P, NB, C]), sb("scr", [P, NB, C]), sb("den", [P, NB, H])
    collect_sums(g, total, part, tables)
    on_vector(g, [
        ("dve", lambda e: e.tensor_scalar(den[:], total[:, :, C:W], 1e-8, None, ALU.add)),
        ("dve", lambda e: e.reciprocal(den[:], den[:])),
        ("dve", lambda e: e.tensor_tensor(hid[:].rearrange("p j (h d) -> p j h d", h=H),
                                          total[:, :, 0:C].rearrange("p j (h d) -> p j h d", h=H),
                                          den[:].unsqueeze(3).to_broadcast([P, NB, H, C // H]), ALU.mult)),
        ("dve", lambda e: e.tensor_tensor(scr[:], x[:], rows(t["L1_gnn_bo"][:], NB), ALU.add)),
    ])
    node_linear(g, "l1", hid, [(t["L1_gnn_Wo_T"], scr, scr)])
    layer_norm(g, scr, hid, scale=t["L1_gnn_ln_g"], shift=t["L1_gnn_ln_b"])
    on_vector(g, [("dve", lambda e: e.tensor_tensor(scr[:], scr[:], x[:], ALU.add))])
    layer_norm(g, scr, hid, dst=x)


def degrees(g, per):
    on_vector(g, [
        ("dve", lambda e: e.tensor_scalar(per[:], g.count[:], 1.0, None, ALU.max)),
        ("dve", lambda e: e.reciprocal(per[:], per[:])),
        ("dve", lambda e: e.tensor_scalar(g.dinv[:], g.count[:], 1.0, None, ALU.add)),
        ("act", lambda e: e.activation(g.dinv[:], g.dinv[:], ACT.Sqrt)),
        ("dve", lambda e: e.reciprocal(g.dinv[:], g.dinv[:])),
    ])


def convolution_out(g, total, self_loop, hid):
    x, NB, t = g.t["x_sb"], g.NB, g.t
    scr = self_loop
    on_vector(g, [
        ("dve", lambda e: e.tensor_tensor(scr[:], total, self_loop[:], ALU.add)),
        ("dve", lambda e: e.tensor_tensor(scr[:], scr[:], bcast(g.dinv[:], C), ALU.mult)),
        ("dve", lambda e: e.tensor_tensor(scr[:], scr[:], rows(t["L3_gnn_b"][:], NB), ALU.add)),
        ("dve", lambda e: e.tensor_scalar(hid[:], scr[:], 20.0, None, ALU.min)),
        ("act", lambda e: e.activation(hid[:], hid[:], ACT.Exp)),
        ("dve", lambda e: e.scalar_tensor_tensor(out=hid[:], in0=hid[:], scalar=2.0, in1=hid[:],
                                                 op0=ALU.add, op1=ALU.mult)),
        ("dve", lambda e: e.tensor_tensor(scr[:], scr[:], hid[:], ALU.mult)),
        ("dve", lambda e: e.tensor_scalar(hid[:], hid[:], 2.0, None, ALU.add)),
        ("dve", lambda e: e.reciprocal(hid[:], hid[:])),
        ("dve", lambda e: e.tensor_tensor(scr[:], scr[:], hid[:], ALU.mult)),
        ("dve", lambda e: e.tensor_tensor(scr[:], scr[:], x[:], ALU.add)),
    ])
    layer_norm(g, scr, hid, dst=x)


def general_gnn(g):
    nc, N, NB, S, t = g.nc, g.N, g.NB, g.S, g.t
    x, count, dinv = t["x_sb"], g.count, g.dinv
    sb = lambda c, name, shape: c.enter_context(g.sbuf(name, shape, F32))
    with ExitStack() as ph:
        xa = sb(ph, "xa_sb", [P, NB, C])
        node_linear(g, "xa", x, [(t["Wn1_node"], t["L0_gnn_bn1"], xa)])
        to_table(g, [(g.xa, xa)])
        clear_tables(g)
    mark_duplicates(g)
    edges_l0(g)
    with ExitStack() as ph:
        total = sb(ph, "total", [P, NB, W])
        part = [sb(ph, f"part{i}", [P, NB, W]) for i in range(2)]
        hid, scr = sb(ph, "hid", [P, NB, C]), sb(ph, "scr", [P, NB, C])
        collect_sums(g, total, part, g.sums)
        on_vector(g, [
            ("dve", lambda e: e.tensor_copy(count[:], total[:, :, C:C + 1].rearrange("p j o -> p (j o)"))),
            ("dve", lambda e: e.tensor_copy(hid[:], total[:, :, 0:C])),
            ("dve", lambda e: e.tensor_tensor(scr[:], bcast(count[:], C), rows(t["L0_gnn_bn2"][:], NB), ALU.mult)),
            ("dve", lambda e: e.scalar_tensor_tensor(out=scr[:], in0=x[:], scalar=2.0, in1=scr[:], op0=ALU.mult, op1=ALU.add)),
        ])
        node_linear(g, "l0", hid, [(t["L0_gnn_Wn2"], scr, scr)])
        layer_norm(g, scr, hid, dst=x)
    g.clear_semaphores()
    with ExitStack() as lay:
        g.scores = sb(lay, "scores", [P, S * K, H])
        g.top = sb(lay, "top", [P, H])
        with ExitStack() as ph:
            qkv = [sb(ph, n, [P, NB, C]) for n in ("q_sb", "k_sb", "v_sb")]
            node_linear(g, "qkv", x, [(t[f"L1_gnn_W{n}_T"], t[f"L1_gnn_b{n}"], o) for n, o in zip("qkv", qkv)])
            to_table(g, list(zip((g.q, g.k, g.v), qkv)))
            clear_tables(g)
        with ExitStack() as ph:
            g.cut = sb(ph, "cut", [P, S * K])
            cutoff(g)
            g.clear_semaphores()
            edges_l1_scores(g)
        head_maximum(g)
        edges_simple(g, g.v, "dst", "src", weighted=True)
    with ExitStack() as ph:
        attention_out(g, ph, g.sums)
    to_table(g, [(g.x2, x)])
    clear_tables(g)
    g.clear_semaphores()
    edges_simple(g, g.x2, "src", "dst", weighted=False)
    with ExitStack() as ph:
        total = sb(ph, "total", [P, NB, W])
        part = [sb(ph, f"part{i}", [P, NB, W]) for i in range(2)]
        hid, scr, per = sb(ph, "hid", [P, NB, C]), sb(ph, "scr", [P, NB, C]), sb(ph, "per", [P, NB])
        collect_sums(g, total, part, g.sums)
        degrees(g, per)
        on_vector(g, [
            ("dve", lambda e: e.tensor_tensor(hid[:], total[:, :, 0:C], bcast(per[:], C), ALU.mult)),
            ("dve", lambda e: e.tensor_tensor(scr[:], x[:], rows(t["b_l2"][:], NB), ALU.add)),
        ])
        node_linear(g, "l2n", hid, [(t["L2_gnn_w_neigh_T"], scr, scr)])
        node_linear(g, "l2s", x, [(t["L2_gnn_w_self_T"], scr, scr)])
        layer_norm(g, scr, hid, dst=x)
    with ExitStack() as lay:
        h3 = sb(lay, "h3_sb", [P, NB, C])
        zero_row = sb(lay, "zero_row", [P, C])
        on_vector(g, [("dve", lambda e: e.memset(zero_row[:], 0.0))])
        node_linear(g, "h3", x, [(t["L3_gnn_W"], zero_row, h3)])
        on_vector(g, [("dve", lambda e: e.tensor_tensor(h3[:], h3[:], bcast(dinv[:], C), ALU.mult))])
        to_table(g, [(g.h3, h3)])
        clear_tables(g)
        g.clear_semaphores()
        edges_simple(g, g.h3, "src", "dst", weighted=False)
        total = sb(lay, "total", [P, NB, W])
        part = [sb(lay, f"part{i}", [P, NB, W]) for i in range(2)]
        hid = sb(lay, "hid", [P, NB, C])
        collect_sums(g, total, part, g.sums)
        convolution_out(g, total[:, :, 0:C], h3, hid)
    g.clear_semaphores()


def windows(g, ctx):
    nc, S, ins, t = g.nc, g.S, g.ins, g.t
    L = P * K
    keep = lambda name, shape, dt=F32: ctx.enter_context(g.sbuf(name, shape, dt))
    t["rank_f"] = keep("rank_f", [P, S, K])
    t["cell_f"] = keep("cell_f", [P, S, K])
    t["block_f"] = keep("block_f", [P, S, K])
    t["first4"] = keep("first4", [P, S * K, 4], BF16)
    t["node_i"] = keep("node_i", [R, S + 1], I32)
    t["iota_r"] = keep("iota_r", [P, R])
    t["iota_h"] = keep("iota_h", [P, max(PARTS) * R], F16)
    t["part_f"] = keep("part_f", [P, 1])
    t["Wt9"] = keep("Wt9", [9, C], BF16)
    t["We1_9"] = keep("We1_9", [9, C], BF16)
    t["be2_3"] = keep("be2_3", [3, GK * H], BF16)
    t["ones_b"] = keep("ones_b", [3, P], BF16)
    t["fast_ok"] = keep("fast_ok", [1, 1], I32)
    dram = lambda name, shape, dt=F32: nc.dram_tensor(name, shape, dt, kind="Internal").ap()
    rank_dram, first_dram = dram("rank_dram", (S, L)), dram("first_dram", (S, L))
    g.rank_rows = dram("rank_rows", (S, L), BF16)
    g.time9, g.len9 = dram("time9", (S, 9, L), BF16), dram("len9", (S, 9, L), BF16)
    wt9_dram, we9_dram = dram("wt9_dram", (3, 3, C), BF16), dram("we9_dram", (3, 3, C), BF16)
    be3_dram = dram("be3_dram", (3, H), BF16)

    with ExitStack() as ph:
        sb = lambda name, shape, dt=F32: ph.enter_context(g.sbuf(name, shape, dt))
        raw = sb("raw", [S, L], I32)
        d, change, rank = sb("d", [S, L]), sb("change", [S, L]), sb("rank", [S, L])
        rank_b = sb("rank_b", [S, K, P], BF16)
        bad, worse = sb("bad", [S, 1]), sb("worse", [S, 1])
        row = {n: sb(n + "_in", [S, L]) for n in ("time", "len")}
        rest = sb("rest", [S, K, P])
        parts = {n: sb(n + "_parts", [S, 3, L], BF16) for n in ("time", "len")}
        lefts = {"Wt_row": sb("Wt_left", [1, C]), "We1_row": sb("We1_left", [1, C]), "be2_row": sb("be2_left", [1, H])}
        wparts = {n: sb(n + "_parts", [1, 3, C], BF16) for n in ("Wt_row", "We1_row")}
        bparts = sb("be2_parts", [1, 3, H], BF16)
        loaded, chain, pool_done = g.sem(ph, "win_loaded"), g.sem(ph, "win_chain"), g.sem(ph, "win_pool")
        ready, stored, back = g.sem(ph, "win_ready"), g.sem(ph, "win_stored"), g.sem(ph, "win_back")
        turned, consts_in = g.sem(ph, "win_turned"), g.sem(ph, "win_consts_in")
        ints = sb("ints", [P, S, K], I32)
        quot, over, hi6 = sb("quot", [P, S, K]), sb("over", [P, S, K]), sb("hi6", [P, S, K])
        firsts = sb("firsts", [P, S, K])
        flag_ps = ph.enter_context(g.psum("flag_ps", [1, 512], F32))
        flag_f = sb("flag_f", [1, 1])
        iota_i = sb("iota_i", [P, max(PARTS) * R], I32)
        rounded, taken, lefts_ready = g.sem(ph, "win_rounded"), g.sem(ph, "win_taken"), g.sem(ph, "win_lefts_ready")
        splits = [(row[n][:].rearrange("s (p k) -> s k p", k=K),
                   lambda j, n=n: parts[n][:, j, :].rearrange("s (k p) -> s k p", k=K)) for n in ("time", "len")]
        splits += [(lefts[n][:], lambda j, n=n: wparts[n][:, j, :]) for n in ("Wt_row", "We1_row")]
        splits += [(lefts["be2_row"][:], lambda j: bparts[:, j, :])]
        block = ph.enter_context(nc.Block())

        @block.sync
        def _(sp):
            sp.dma_start(raw[:], ins["dst"].rearrange("(s n) -> s n", n=L)).then_inc(loaded, 16)
            sp.dma_start(row["time"][:], ins["edge_weight"].rearrange("(s n) -> s n", n=L)).then_inc(loaded, 16)
            sp.dma_start(row["len"][:], ins["edge_weight1"].rearrange("(s n) o -> s (n o)", n=L)).then_inc(loaded, 16)
            sp.wait_ge(ready, 1)
            sp.dma_start(rank_dram, rank[:]).then_inc(stored, 16)
            sp.dma_start(first_dram, change[:]).then_inc(stored, 16)
            sp.dma_start(g.rank_rows, rank_b[:].rearrange("s k p -> s (k p)")).then_inc(stored, 16)
            sp.wait_ge(stored, 48)
            sp.dma_start(t["rank_f"][:], rank_dram.rearrange("s (p k) -> p s k", k=K)).then_inc(back, 16)
            sp.dma_start(firsts[:], first_dram.rearrange("s (p k) -> p s k", k=K)).then_inc(back, 16)
            sp.wait_ge(rounded, 3 * len(splits))
            for j in range(3):
                sp.dma_start(g.time9[:, 3 * j:3 * j + 3, :], parts["time"][:]).then_inc(stored, 16)
                sp.dma_start(g.len9[:, 3 * j:3 * j + 3, :], parts["len"][:]).then_inc(stored, 16)
                sp.dma_start(wt9_dram[:, j, :].unsqueeze(0), wparts["Wt_row"][:]).then_inc(stored, 16)
                sp.dma_start(we9_dram[:, j, :].unsqueeze(0), wparts["We1_row"][:]).then_inc(stored, 16)
            sp.dma_start(be3_dram.unsqueeze(0), bparts[:]).then_inc(stored, 16)
            sp.wait_ge(stored, 48 + 13 * 16)
            sp.dma_start(t["Wt9"][:], wt9_dram.rearrange("i j c -> (i j) c")).then_inc(consts_in, 16)
            sp.dma_start(t["We1_9"][:], we9_dram.rearrange("i j c -> (i j) c")).then_inc(consts_in, 16)
            for k in range(GK):
                sp.dma_start(t["be2_3"][:, k * H:(k + 1) * H], be3_dram).then_inc(consts_in, 16)
            sp.wait_ge(consts_in, (2 + GK) * 16)
            sp.wait_ge(back, 2 * 16)

        @block.gpsimd
        def _(pool):
            pool.iota(iota_i[:], pattern=[[1, max(PARTS) * R]], base=0, channel_multiplier=0).then_inc(pool_done, 1)
            for j in range(2):
                for m, (x, parts_of) in enumerate(splits):
                    pool.wait_ge(rounded, j * len(splits) + m + 1)
                    pool.tensor_tensor(x, x, parts_of(j), ALU.subtract).then_inc(taken, 1)

        @block.scalar
        def _(act):
            for n, left in lefts.items():
                act.copy(left[:], t[n][:]).then_inc(lefts_ready, 1)
            act.wait_ge(loaded, 48)
            act.wait_ge(lefts_ready, len(lefts))
            for j in range(3):
                for m, (x, parts_of) in enumerate(splits):
                    if j:
                        act.wait_ge(taken, (j - 1) * len(splits) + m + 1)
                    act.copy(parts_of(j), x).then_inc(rounded, 1)

        @block.tensor
        def _(pe):
            pe.wait_ge(chain, FLAG_STEP)
            pe.transpose(flag_ps[0:1, 0:S], bad[:], t["ident"][0:S, 0:S]).then_inc(turned, 1)

        @block.vector
        def _(dve):
            link = Chain(dve, chain)
            dve.wait_ge(loaded, 48)
            link(dve.tensor_copy(d[:], raw[:]))
            link(dve.memset(change[:, 0:1], 0.0))
            link(dve.tensor_tensor(change[:, 1:L], d[:, 1:L], d[:, 0:L - 1], ALU.not_equal))
            link(dve.memset(rest[:], 0.0))
            link(dve.tensor_tensor_scan(rank[:], change[:], rest[:].rearrange("s k p -> s (k p)"), 0.0,
                                        ALU.add, ALU.add))
            link(dve.tensor_tensor(rest[:].rearrange("s k p -> s (k p)")[:, 1:L], d[:, 1:L], d[:, 0:L - 1], ALU.is_lt))
            link(dve.tensor_reduce(bad[:], rest[:].rearrange("s k p -> s (k p)"), AX, ALU.max))
            link(dve.tensor_scalar(worse[:], rank[:, L - 1:L], float(R) - 0.5, None, ALU.is_gt))
            link(dve.tensor_tensor(bad[:], bad[:], worse[:], ALU.max))
            assert link.n == FLAG_STEP
            link(dve.memset(change[:, 0:1], 1.0))
            dve.tensor_copy(rank_b[:], rank[:].rearrange("s (p k) -> s k p", k=K)).then_inc(ready, 1)
            dve.wait_ge(turned, 1)
            link(dve.tensor_reduce(flag_f[:], flag_ps[0:1, 0:S], AX, ALU.max))
            link(dve.tensor_scalar(flag_f[:], flag_f[:], -1.0, 1.0, ALU.mult, ALU.add))
            link(dve.tensor_copy(t["fast_ok"][:], flag_f[:]))

            link(dve.memset(t["ones_b"][:], 1.0))
            dve.wait_ge(pool_done, 1)
            link(dve.tensor_copy(t["iota_h"][:], iota_i[:]))
            link(dve.tensor_copy(t["iota_r"][:], iota_i[:, 0:R]))
            link(dve.tensor_scalar(t["part_f"][:], t["trash"][:], -float(g.N), None, ALU.add))
            link(dve.memset(t["node_i"][:, S:S + 1], 0))
            link(dve.tensor_scalar(quot[:], t["src_f"][:], 1.0 / g.NB, None, ALU.mult))
            link(dve.tensor_copy(ints[:], quot[:]))
            link(dve.tensor_copy(quot[:], ints[:]))
            link(dve.scalar_tensor_tensor(out=over[:], in0=quot[:], scalar=-float(g.NB), in1=t["src_f"][:],
                                          op0=ALU.mult, op1=ALU.add))
            link(dve.tensor_scalar(hi6[:], over[:], 0.0, None, ALU.is_lt))
            link(dve.tensor_tensor(t["block_f"][:], quot[:], hi6[:], ALU.subtract))
            link(dve.scalar_tensor_tensor(out=over[:], in0=hi6[:], scalar=float(g.NB), in1=over[:],
                                          op0=ALU.mult, op1=ALU.add))
            dve.wait_ge(back, 32)
            link(dve.scalar_tensor_tensor(out=t["cell_f"][:], in0=over[:], scalar=float(R), in1=t["rank_f"][:],
                                          op0=ALU.mult, op1=ALU.add))
            link(dve.tensor_scalar(quot[:], t["dst_f"][:], 1.0 / 64, None, ALU.mult))
            link(dve.tensor_copy(ints[:], quot[:]))
            link(dve.tensor_copy(quot[:], ints[:]))
            link(dve.tensor_scalar(hi6[:], quot[:], 64.0, None, ALU.mult))
            link(dve.tensor_tensor(over[:], t["dst_f"][:], hi6[:], ALU.subtract))
            f4 = lambda j: t["first4"][:, :, j:j + 1].rearrange("p (s k) o -> p s (k o)", k=K)
            link(dve.tensor_tensor(f4(0), hi6[:], firsts[:], ALU.mult))
            link(dve.tensor_tensor(f4(1), over[:], firsts[:], ALU.mult))
            link(dve.tensor_copy(f4(2), firsts[:]))
            link(dve.memset(t["first4"][:, :, 3:4], 1.0))


def edge_loop(eng, S, body, apart):
    for s in range(apart):
        body(s, s, False)
    with eng.Fori(apart, S - 1) as s:
        body(s, apart, False)
    body(S - 1, apart, True)


def there(s, S):
    return 0 <= s < S if isinstance(s, int) else True


def slots(eng, S, slot, ahead, apart=2):
    for n in range(-ahead, 0):
        slot(-1, n + G)
    for s in range(apart):
        for i in range(G):
            slot(s, i)
    with eng.Fori(apart, S - 1) as s:
        for i in range(G):
            slot(s, i)
    for i in range(G):
        slot(S - 1, i)


def on(stage, s, i, lag, S):
    j = i + lag
    if there(s + j // G, S):
        stage(s + j // G, j % G, s * G + j)


class Counts:

    def __init__(self, g, ph, part):
        self.g, self.part, self.n = g, part, PARTS[part] * R
        self.banks = -(-self.n // 512)
        sb = lambda name, shape, dt=F16: ph.enter_context(g.sbuf(name, shape, dt))
        self.block, self.cell = sb("block_ones", [P, K, P]), sb("cell_ones", [P, K, self.n])
        self.squares = sb("block_squares", [P, GK, P])
        self.out = sb("counts", [P, self.n])
        self.ps = ph.enter_context(g.psum("counts_ps", [P, self.banks, 512], F32))
        sem = lambda name: g.sem(ph, name)
        self.ready, self.blocks = sem("cells_ready"), sem("blocks_ready")
        self.squared = sem("blocks_squared")
        self.summed, self.copied, self.stored = sem("cells_summed"), sem("counts_out"), sem("counts_stored")

    def blocks_of(self, act, s, i, n):
        wait_count(act, self.blocks, n)
        for k in range(GK):
            ins = act.activation(self.squares[:, k, :], self.g.t["iota_h"][:, 0:P], ACT.Square, scale=-1.0,
                                 bias=self.g.t["block_f"][:, bass.ds(s, 1), i * GK + k:i * GK + k + 1]
                                 .rearrange("p o k -> p (o k)"))
        ins.then_inc(self.squared, 1)
        act.wait_ge(self.squared, n + 1)
        wait_count(act, self.summed, n - G + 1)
        act.activation(self.block[:, i * GK:(i + 1) * GK, :], self.squares[:], ACT.Relu, scale=-1.0,
                       bias=self.g.t["ones"][0:P, 0:1]).then_inc(self.blocks, 1)

    def blocks_on_vector(self, dve, s, i, n):
        wait_count(dve, self.summed, n - G + 1)
        for k in range(i * GK, (i + 1) * GK):
            ins = dve.tensor_scalar(self.block[:, k, :], self.g.t["iota_h"][:, 0:P],
                                    self.g.t["block_f"][:, bass.ds(s, 1), k:k + 1].rearrange("p o k -> p (o k)"),
                                    None, ALU.is_equal)
        ins.then_inc(self.blocks, 1)

    def cells_of(self, dve, s, i, n):
        t = self.g.t
        wait_count(dve, self.summed, n - G + 1)
        for k in range(i * GK, (i + 1) * GK):
            ins = dve.tensor_scalar(self.cell[:, k, :], t["iota_h"][:, 0:self.n],
                                    t["cell_f"][:, bass.ds(s, 1), k:k + 1].rearrange("p o k -> p (o k)"),
                                    None, ALU.is_equal)
        ins.then_inc(self.ready, 1)

    def products(self, pe, s, i, n, tiles=range(GK)):
        m = self.n // self.banks
        if tiles[0] == 0:
            pe.wait_ge(self.ready, n + 1)
            pe.wait_ge(self.blocks, n + 1)
            if i == 0:
                wait_count(pe, self.copied, s)
        for k in (i * GK + tile for tile in tiles):
            for b in range(self.banks):
                ins = pe.matmul(self.ps[:, b, 0:m], self.block[:, k, :], self.cell[:, k, b * m:(b + 1) * m],
                                start=(k == 0), stop=(k == K - 1))
        if tiles[-1] == GK - 1:
            ins.then_inc(self.summed, 1)

    def copy_out(self, act, s, i, n):
        act.wait_ge(self.summed, s * G + G)
        wait_count(act, self.stored, 16 * s)
        act.copy(self.out[:].rearrange("p (b m) -> p b m", b=self.banks), self.ps[:, :, 0:self.n // self.banks]).then_inc(self.copied, 1)

    def store(self, sp, s, i, n):
        at = R * sum(PARTS[:self.part])
        sp.wait_ge(self.copied, s + 1)
        sp.dma_start(self.g.counts[bass.ds(s, 1), :, at:at + self.n].rearrange("o p n -> (o p) n"), self.out[:])\
            .then_inc(self.stored, 16)


def shift_cells(g, part):
    on_vector(g, [("dve", lambda e: e.tensor_scalar(g.t["cell_f"][:], g.t["cell_f"][:], -float(PARTS[part] * R), None,
                                                    ALU.add))])


def fast_l0(g):
    nc, S, t = g.nc, g.S, g.t
    ea_dram = g.ins["edge_attr_64"].rearrange("(s p k) c -> s p k c", p=P, k=K)
    D = ea_dram.shape[3]
    table = g.fast_sums[0][0]
    with ExitStack() as ph:
        sb = lambda name, shape, dt=F32: ph.enter_context(g.sbuf(name, shape, dt))
        ps = lambda name: ph.enter_context(g.psum(name, [C, 512], F32))
        sem = lambda name: g.sem(ph, name)
        ea, ts = sb("ea", [P, K, D]), sb("ts", [9, K * P], BF16)
        eaT, h1T = sb("eaT", [D, K, P]), sb("h1T", [C, K, P])
        gateT, efT = sb("gateT", [C, K, P]), sb("efT", [C, K, P])
        xa, xa_slot = sb("xa_got", [P, K, C]), sb("xa_slot", [P, K], I32)
        msg, onehot = sb("msg", [P, K, C + 4]), sb("onehot", [P, K, R])
        sums, sumT = sb("sums", [R, C + 4]), sb("sumT", [C, R])
        spare = sb("spare", [R, 1])
        node_slot = sb("node_slot", [R, 1], I32)
        out_rows = sb("out_rows", [R, W])
        ea_ps, h1_ps, ts_ps, ef_ps = ps("ea_ps"), ps("h1_ps"), ps("ts_ps"), ps("ef_ps")
        pre_ps, sum_ps, row_ps = ps("pre_ps"), ps("sum_ps"), ps("row_ps")
        ct = Counts(g, ph, 0)
        ea_in, ts_in = [sem(f"ea_in{i}") for i in range(G)], [sem(f"ts_in{i}") for i in range(G)]
        ea_turned, eaT_out = sem("ea_turned"), sem("eaT_out")
        ts_spread, gate_out = sem("ts_spread"), sem("gate_out")
        h1_ready, h1_out, ef_ready, ef_out = sem("h1_ready"), sem("h1_out"), sem("ef_ready"), sem("ef_out")
        pre_ready, added, msg_ready = sem("pre_ready"), sem("added"), sem("msg_ready")
        onehot_ready, summed, sums_out, sums_turned = sem("onehot_ready"), sem("summed"), sem("sums_out"), sem("sums_turned")
        sumT_out, row_ready, row_out, chain, slot_ready = sem("sumT_out"), sem("row_ready"), sem("row_out"), sem("chain"), sem("slot_ready")
        staged, tick, pool_tick = sem("staged"), sem("pe_tick"), sem("pool_tick")
        cleared, cleared_later = sem("cleared"), sem("cleared_later")
        arrived, scattered = g.arrived[0], g.scattered[0]
        a_base, s_base = g.arrived_so_far[0], g.scatters[0]
        g.arrived_so_far[0] += 16 * GK * S
        g.scatters[0] += 16 * S
        block = ph.enter_context(nc.Block())
        grp = lambda i: slice(i * GK, (i + 1) * GK)
        flat = lambda buf, i: buf[:, grp(i), :].rearrange("c k p -> c (k p)")

        @block.sync
        def _(sp):
            def clear(tab, done):
                sp.dma_start(tab.rearrange("(p j) c -> p (j c)", p=P), t["zeros"][:, 0:26 * tab.shape[1]])\
                    .then_inc(done, 16)

            def load(s, i, n):
                wait_count(sp, ea_turned, n - G + 1)
                sp.dma_start(ea[:, grp(i), :], ea_dram[bass.ds(s, 1), :, grp(i), :].rearrange("o p k c -> p (o k) c"))\
                    .then_inc(ea_in[i], 16)
                wait_count(sp, ts_spread, n - G + 1)
                at = slice(i * GK * P, (i + 1) * GK * P)
                sp.dma_start(ts[:, at], g.time9[bass.ds(s, 1), :, at].rearrange("o j n -> (o j) n")).then_inc(ts_in[i], 16)

            def slot(s, i):
                on(load, s, i, 0, S)
                if i == 3:
                    on(lambda *a: ct.store(sp, *a), s, i, -2 * G, S)

            clear(table, cleared)
            slots(sp, S, slot, 0)
            ct.store(sp, S - 2, 0, 0)
            ct.store(sp, S - 1, 0, 0)
            later = [tab for tables in g.fast_sums[1:] for tab in tables]
            for tab in later:
                clear(tab, cleared_later)
            sp.wait_ge(cleared_later, 16 * len(later))
            sp.wait_ge(ct.stored, 16 * S)

        @block.tensor
        def _(pe):
            def turn(s, i, n):
                pe.wait_ge(ea_in[i], 16 * s + 16)
                wait_count(pe, eaT_out, n)
                pe.sem_inc(tick, 1)
                for k in range(GK):
                    ins = pe.transpose(ea_ps[0:D, k * P:(k + 1) * P], ea[:, i * GK + k, :], t["ident"][0:P, 0:P])
                ins.then_inc(ea_turned, 1)

            def spread(s, i, n):
                pe.wait_ge(ts_in[i], 16 * s + 16)
                wait_count(pe, gate_out, n)
                pe.matmul(ts_ps[:, 0:GK * P], t["Wt9"][:], ts[:, i * GK * P:(i + 1) * GK * P],
                          start=True, stop=True).then_inc(ts_spread, 1)

            def first(s, i, n):
                pe.wait_ge(eaT_out, n + 1)
                wait_count(pe, h1_out, n)
                pe.matmul(h1_ps[:, 0:GK * P], t["L0_gnn_We1"][:], flat(eaT, i), start=True, stop=True)\
                    .then_inc(h1_ready, 1)

            def second(s, i, n):
                pe.wait_ge(h1_out, n + 1)
                wait_count(pe, ef_out, n)
                pe.matmul(ef_ps[:, 0:GK * P], t["L0_gnn_We2"][:], flat(h1T, i), start=True, stop=True)\
                    .then_inc(ef_ready, 1)

            def before_relu(s, i, n):
                pe.wait_ge(ef_out, n + 1)
                wait_count(pe, added, n)
                for k in range(GK):
                    ins = pe.matmul(pre_ps[0:P, k * C:(k + 1) * C], efT[:, i * GK + k, :], t["Wn1_edge"][:],
                                    start=True, stop=True)
                ins.then_inc(pre_ready, 1)

            def add_up(s, i, n):
                pe.wait_ge(onehot_ready, n + 1)
                pe.wait_ge(msg_ready, n + 1)
                if i == 0:
                    wait_count(pe, sums_out, s)
                for k in range(i * GK, (i + 1) * GK):
                    ins = pe.matmul(sum_ps[0:R, 0:C + 4], onehot[:, k, :], msg[:, k, :], start=(k == 0), stop=(k == K - 1))
                ins.then_inc(summed, 1)

            def turn_sums(s, i, n):
                pe.wait_ge(sums_out, s + 1)
                wait_count(pe, row_out, s)
                pe.sem_inc(tick, 1)
                pe.transpose(row_ps[:, C:C + R], sums[:, 0:C], t["ident"][0:R, 0:R]).then_inc(sums_turned, 1)

            def rows_through(s, i, n):
                pe.wait_ge(sumT_out, s + 1)
                pe.matmul(row_ps[0:R, 0:C], sumT[:], t["L0_gnn_Wn2"][:], start=True, stop=True).then_inc(row_ready, 1)

            def slot(s, i):
                on(first, s, i, 3, S)
                on(turn, s, i, 4, S)
                on(second, s, i, 2, S)
                if i == 0:
                    on(turn_sums, s, i, -G, S)
                if i == 1:
                    on(rows_through, s, i, -G, S)
                on(spread, s, i, 3, S)
                on(before_relu, s, i, 1, S)
                on(add_up, s, i, 0, S)
                on(lambda *a: ct.products(pe, *a), s, i, 0, S)

            slots(pe, S, slot, 4)
            turn_sums(S - 1, 0, 0)
            rows_through(S - 1, 0, 0)

        @block.scalar
        def _(act):
            def turned_out(s, i, n):
                act.wait_ge(ea_turned, n + 1)
                act.copy(flat(eaT, i), ea_ps[0:D, 0:GK * P]).then_inc(eaT_out, 1)

            def gate(s, i, n):
                act.wait_ge(ts_spread, n + 1)
                wait_count(act, ef_out, n - G + 1)
                act.activation(flat(gateT, i), ts_ps[:, 0:GK * P], ACT.Sigmoid, bias=t["L0_gnn_bt"][:, 0:1])\
                    .then_inc(gate_out, 1)

            def hidden(s, i, n):
                act.wait_ge(h1_ready, n + 1)
                act.activation(flat(h1T, i), h1_ps[:, 0:GK * P], ACT.Relu, bias=t["L0_gnn_be1"][:, 0:1])\
                    .then_inc(h1_out, 1)

            def message(s, i, n):
                act.wait_ge(added, n + 1)
                wait_count(act, summed, n - G + 1)
                act.activation(msg[:, grp(i), 0:C], xa[:, grp(i), :], ACT.Relu).then_inc(msg_ready, 1)

            def copy_sums(s, i, n):
                act.wait_ge(summed, s * G + G)
                wait_count(act, sums_turned, s)
                wait_count(act, slot_ready, s)
                act.copy(sums[:], sum_ps[0:R, 0:C + 4]).then_inc(sums_out, 1)

            def copy_turned(s, i, n):
                act.wait_ge(sums_turned, s + 1)
                wait_count(act, row_ready, s)
                act.copy(sumT[:], row_ps[:, C:C + R]).then_inc(sumT_out, 1)

            def rows_out(s, i, n):
                act.wait_ge(row_ready, s + 1)
                wait_count(act, scattered, s_base + 16 * s)
                act.copy(out_rows[:, 0:C], row_ps[0:R, 0:C]).then_inc(row_out, 1)

            def slot(s, i):
                if i == 0:
                    on(copy_sums, s, i, -G, S)
                on(hidden, s, i, 3, S)
                on(turned_out, s, i, 4, S)
                on(gate, s, i, 3, S)
                if i == 0:
                    on(lambda *a: ct.copy_out(act, *a), s, i, -G, S)
                    on(copy_turned, s, i, -G, S)
                if i == 1:
                    on(rows_out, s, i, -G, S)
                on(message, s, i, 1, S)

            slots(act, S, slot, 4)
            copy_sums(S - 1, 0, 0)
            copy_turned(S - 1, 0, 0)
            rows_out(S - 1, 0, 0)
            ct.copy_out(act, S - 1, 0, 0)

        @block.vector
        def _(dve):
            def nodes_out(s, i, n):
                dve.wait_ge(sums_out, s + 1)
                c = s * 4
                dve.tensor_scalar(spare[:], sums[:, C + 2:C + 3], -1.0, 1.0, ALU.mult, ALU.add).then_inc(chain, 1)
                dve.wait_ge(chain, c + 1)
                dve.scalar_tensor_tensor(out=spare[:], in0=spare[:], scalar=t["trash"][0:R, 0:1], in1=sums[:, C:C + 1],
                                         op0=ALU.mult, op1=ALU.add).then_inc(chain, 1)
                dve.wait_ge(chain, c + 2)
                dve.tensor_tensor(spare[:], spare[:], sums[:, C + 1:C + 2], ALU.add).then_inc(chain, 1)
                dve.wait_ge(chain, c + 3)
                wait_count(dve, scattered, s_base + 16 * s)
                dve.tensor_copy(out_rows[:, C:C + 1], sums[:, C + 3:C + 4])
                dve.tensor_copy(t["node_i"][:, bass.ds(s, 1)], spare[:]).then_inc(chain, 1)
                dve.wait_ge(chain, c + 4)
                dve.tensor_copy(node_slot[:], spare[:]).then_inc(slot_ready, 1)

            def ranks(s, i, n):
                wait_count(dve, summed, n - G + 1)
                rank = t["rank_f"][:, bass.ds(s, 1), grp(i)].rearrange("p o k -> p (o k)")
                dve.tensor_tensor(onehot[:, grp(i), :], rows(t["iota_r"][:], GK), bcast(rank, R), ALU.is_equal)
                dve.tensor_copy(msg[:, grp(i), C:C + 4], t["first4"][:, bass.ds(s * K + i * GK, GK), :]).then_inc(onehot_ready, 1)

            def features(s, i, n):
                dve.wait_ge(ef_ready, n + 1)
                dve.wait_ge(gate_out, n + 1)
                wait_count(dve, pre_ready, n - G + 1)
                dve.scalar_tensor_tensor(out=flat(efT, i), in0=ef_ps[:, 0:GK * P], scalar=t["L0_gnn_be2"][:, 0:1],
                                         in1=flat(gateT, i), op0=ALU.add, op1=ALU.mult).then_inc(ef_out, 1)

            def add_node(s, i, n):
                dve.wait_ge(pre_ready, n + 1)
                dve.wait_ge(arrived[i], 16 * GK * s + (a_base + 16 * GK))
                dve.tensor_tensor(flat(xa, i), pre_ps[0:P, 0:GK * C], flat(xa, i), ALU.add).then_inc(added, 1)

            def stage(s, i, n):
                dve.tensor_copy(xa_slot[:, grp(i)], t["src_i"][:, bass.ds(s, 1), grp(i)]
                                .rearrange("p o k -> p (o k)")).then_inc(staged, 1)

            def slot(s, i):
                on(lambda *a: ct.blocks_on_vector(dve, *a), s, i, 1, S)
                on(lambda *a: ct.cells_of(dve, *a), s, i, 1, S)
                on(ranks, s, i, 2, S)
                if i == 1:
                    on(nodes_out, s, i, -G, S)
                on(features, s, i, 2, S)
                on(stage, s, i, G, S)
                on(add_node, s, i, 1, S)

            dve.memset(out_rows[:], 0.0)
            slots(dve, S, slot, G)
            nodes_out(S - 1, 0, 0)

        @block.gpsimd
        def _(pool):
            def gather(s, i, n):
                pool.wait_ge(staged, n + 1)
                wait_count(pool, msg_ready, n - G + 1)
                pool.sem_inc(pool_tick, 1)
                for k in range(i * GK, (i + 1) * GK):
                    pool.indirect_dma_start(out=xa[:, k, :], out_offset=None, in_=g.xa[:, :],
                                            in_offset=bass.IndirectOffsetOnAxis(ap=xa_slot[:, k:k + 1], axis=0))\
                        .then_inc(arrived[i], 16)

            def scatter(s, i, n):
                pool.wait_ge(slot_ready, s + 1)
                pool.wait_ge(row_out, s + 1)
                wait_count(pool, scattered, s_base + 16 * s)
                pool.sem_inc(pool_tick, 1)
                pool.indirect_dma_start(out=table[:, :], out_offset=bass.IndirectOffsetOnAxis(ap=node_slot[:], axis=0),
                                        in_=out_rows[:], in_offset=None, compute_op=ALU.add).then_inc(scattered, 16)

            def slot(s, i):
                on(gather, s, i, G, S)
                if i == 3:
                    on(scatter, s, i, -G, S)

            pool.wait_ge(cleared, 16)
            slots(pool, S, slot, G)
            scatter(S - 1, 0, 0)
            pool.wait_ge(scattered, s_base + 16 * S)
    g.clear_semaphores()


class Expand:

    def __init__(self, g, ph, table):
        nc, self.g, self.table = g.nc, g, table
        sb = lambda name, shape, dt=F32: ph.enter_context(g.sbuf(name, shape, dt))
        self.rank_row, self.onehotT = sb("rank_row", [R, K * P], BF16), sb("onehotT", [R, K, P], BF16)
        self.got, self.slot = sb("rows_got", [R, 3 * C], BF16), sb("rows_slot", [R, 1], I32)
        self.now = sb("rows_now", [R, 3 * C], BF16)
        self.ps = [ph.enter_context(g.psum(f"spread_ps{b}", [P, 512], F32)) for b in range(2)]
        sem = lambda name: g.sem(ph, name)
        self.row_in = [sem(f"rank_in{i}") for i in range(G)]
        self.ready, self.spread, self.used = sem("onehotT_ready"), sem("rows_spread"), sem("rows_used")
        self.staged, self.tick, self.copied = sem("rows_staged"), sem("rows_tick"), sem("rows_copied")
        self.arrived, self.base = g.arrived[1][0], g.window_arrived
        g.window_arrived += 16 * g.S

    def load(self, sp, s, i, n):
        wait_count(sp, self.ready, n - G + 1)
        at = slice(i * GK * P, (i + 1) * GK * P)
        sp.dma_start(self.rank_row[:, at], self.g.rank_rows[bass.ds(s, 1), at].rearrange("o n -> (o n)").partition_broadcast(R))\
            .then_inc(self.row_in[i], 16)

    def onehot(self, dve, s, i, n):
        dve.wait_ge(self.row_in[i], 16 * s + 16)
        wait_count(dve, self.spread, n - G + 1)
        dve.tensor_scalar(self.onehotT[:, i * GK:(i + 1) * GK, :].rearrange("r k p -> r (k p)"),
                          self.rank_row[:, i * GK * P:(i + 1) * GK * P], self.g.t["part_f"][0:R, 0:1], None, ALU.is_equal)\
            .then_inc(self.ready, 1)

    def stage(self, dve, s, i, n):
        wait_count(dve, self.arrived, self.base + 16 * s if not isinstance(s, int) or s > 0 else 0)
        dve.tensor_copy(self.slot[:], self.g.t["node_i"][:, bass.ds(s, 1)]).then_inc(self.staged, 1)

    def gather(self, pool, s, i, n):
        pool.wait_ge(self.staged, s + 1)
        wait_count(pool, self.copied, s)
        pool.sem_inc(self.tick, 1)
        pool.indirect_dma_start(out=self.got[:], out_offset=None, in_=self.table[:, :],
                                in_offset=bass.IndirectOffsetOnAxis(ap=self.slot[:], axis=0)).then_inc(self.arrived, 16)

    def copy(self, act, s, i, n):
        act.wait_ge(self.arrived, 16 * s + (self.base + 16))
        wait_count(act, self.spread, s * G)
        act.copy(self.now[:], self.got[:]).then_inc(self.copied, 1)

    def product(self, pe, s, i, n):
        if i == 0:
            pe.wait_ge(self.copied, s + 1)
        pe.wait_ge(self.ready, n + 1)
        wait_count(pe, self.used, n if i == 0 else n - 1)
        for k in range(GK):
            for j in range(3):
                ins = pe.matmul(self.ps[i % 2][:, k * C:(k + 1) * C], self.onehotT[:, i * GK + k, :],
                                self.now[:, j * C:(j + 1) * C], start=(j == 0), stop=(j == 2))
        ins.then_inc(self.spread, 1)


def fast_l1_scores(g):
    nc, S, t = g.nc, g.S, g.t
    with ExitStack() as ph:
        sb = lambda name, shape, dt=F32: ph.enter_context(g.sbuf(name, shape, dt))
        sem = lambda name: g.sem(ph, name)
        ex, ct = Expand(g, ph, g.k3), Counts(g, ph, 1)
        q, q_slot = sb("q_got", [P, K, C]), sb("q_slot", [P, K], I32)
        row, hidT, dots = sb("len_row", [9, K * P], BF16), sb("hidT", [C, K, P]), sb("dots", [P, K, H])
        prod = sb("prod", [P, GK, C])
        len_ps = ph.enter_context(g.psum("len_ps", [C, 512], F32))
        bias_ps = [ph.enter_context(g.psum(f"bias_ps{b}", [P, GK, H], F32)) for b in range(2)]
        row_in, spread, hid_out, bias_ready = [sem(f"row_in{i}") for i in range(G)], sem("len_spread"), sem("hid_out"), sem("bias_ready")
        reduced, scored, cut_done, staged, tick = sem("reduced"), sem("scored"), sem("cut_done"), sem("staged"), sem("pool_tick")
        arrived, a_base = g.arrived[0], g.arrived_so_far[0]
        g.arrived_so_far[0] += 16 * GK * S
        block = ph.enter_context(nc.Block())
        grp = lambda i: slice(i * GK, (i + 1) * GK)

        @block.sync
        def _(sp):
            def load(s, i, n):
                wait_count(sp, spread, n - G + 1)
                at = slice(i * GK * P, (i + 1) * GK * P)
                sp.dma_start(row[:, at], g.len9[bass.ds(s, 1), :, at].rearrange("o j n -> (o j) n")).then_inc(row_in[i], 16)
                ex.load(sp, s, i, n)

            def slot(s, i):
                on(load, s, i, G, S)
                if i == 1:
                    on(lambda *a: ct.store(sp, *a), s, i, -G, S)

            slots(sp, S, slot, G)
            ct.store(sp, S - 1, 0, 0)
            sp.wait_ge(ct.stored, 16 * S)

        @block.tensor
        def _(pe):
            def spread_len(s, i, n):
                pe.wait_ge(row_in[i], 16 * s + 16)
                wait_count(pe, hid_out, n)
                pe.matmul(len_ps[:, 0:GK * P], t["We1_9"][:], row[:, i * GK * P:(i + 1) * GK * P],
                          start=True, stop=True).then_inc(spread, 1)

            def bias_rows(s, i, n):
                pe.wait_ge(hid_out, n + 1)
                wait_count(pe, scored, n if i == 0 else n - 1)
                pe.matmul(bias_ps[i % 2][:].rearrange("p k h -> p (k h)"), t["ones_b"][:], t["be2_3"][:],
                          start=True, stop=False)

            def bias(s, i, n, k):
                ins = pe.matmul(bias_ps[i % 2][:, k, :], hidT[:, i * GK + k, :], t["L1_gnn_We2_T"][:],
                                start=False, stop=(k == GK - 1))
                if k == GK - 1:
                    ins.then_inc(bias_ready, 1)

            def slot(s, i):
                on(lambda *a: ex.product(pe, *a), s, i, 1, S)
                on(spread_len, s, i, 2, S)
                on(bias_rows, s, i, 1, S)
                for k in range(GK):
                    on(lambda *a: ct.products(pe, *a, tiles=(k,)), s, i, 0, S)
                    on(lambda *a: bias(*a, k), s, i, 1, S)

            slots(pe, S, slot, 2)

        @block.scalar
        def _(act):
            def hidden(s, i, n):
                act.wait_ge(spread, n + 1)
                wait_count(act, bias_ready, n - G + 1)
                act.activation(hidT[:, grp(i), :].rearrange("c k p -> c (k p)"), len_ps[:, 0:GK * P],
                               ACT.Silu, bias=t["L1_gnn_be1"][:, 0:1]).then_inc(hid_out, 1)

            def slot(s, i):
                if i == 0:
                    on(lambda *a: ct.copy_out(act, *a), s, i, -G, S)
                on(hidden, s, i, 2, S)
                if i == G - 2:
                    on(lambda *a: ex.copy(act, *a), s, i, 2, S)
                on(lambda *a: ct.blocks_of(act, *a), s, i, 1, S)

            slots(act, S, slot, 2)
            ct.copy_out(act, S - 1, 0, 0)

        @block.vector
        def _(dve):
            def score(s, i, n):
                dve.wait_ge(ex.spread, n + 1)
                dve.wait_ge(arrived[i], 16 * GK * s + (a_base + 16 * GK))
                dve.tensor_tensor(prod[:], q[:, grp(i), :],
                                  ex.ps[i % 2][:, 0:GK * C].rearrange("p (k c) -> p k c", k=GK), ALU.mult)\
                    .then_inc(ex.used, 1)

            def reduce(s, i, n):
                dve.wait_ge(ex.used, n + 1)
                dve.tensor_reduce(dots[:, grp(i), :].rearrange("p k h -> p (k h)"),
                                  prod[:].rearrange("p k (h d) -> p (k h) d", h=H), AX, ALU.add).then_inc(reduced, 1)

            def add_bias(s, i, n):
                dve.wait_ge(reduced, n + 1)
                dve.wait_ge(bias_ready, n + 1)
                dve.scalar_tensor_tensor(out=dots[:, grp(i), :], in0=dots[:, grp(i), :],
                                         scalar=float((C // H) ** -0.5), in1=bias_ps[i % 2][:],
                                         op0=ALU.mult, op1=ALU.add).then_inc(scored, 1)

            def cut_off(s, i, n):
                dve.wait_ge(scored, n + 1)
                dve.tensor_tensor(g.scores[:, bass.ds(s * K + i * GK, GK), :], dots[:, grp(i), :],
                                  bcast(g.cut[:, bass.ds(s * K + i * GK, GK)], H), ALU.mult).then_inc(cut_done, 1)

            def stage(s, i, n):
                dve.tensor_copy(q_slot[:, grp(i)], t["src_i"][:, bass.ds(s, 1), grp(i)]
                                .rearrange("p o k -> p (o k)")).then_inc(staged, 1)

            def slot(s, i):
                on(stage, s, i, G, S)
                on(score, s, i, 1, S)
                on(lambda *a: ex.onehot(dve, *a), s, i, 3, S)
                on(reduce, s, i, 1, S)
                on(lambda *a: ct.cells_of(dve, *a), s, i, 1, S)
                on(add_bias, s, i, 1, S)
                on(cut_off, s, i, 0, S)
                if i == G - 1:
                    on(lambda *a: ex.stage(dve, *a), s, i, G + 1, S)

            ex.stage(dve, 0, 0, 0)
            slots(dve, S, slot, G)
            dve.wait_ge(cut_done, S * G)

        @block.gpsimd
        def _(pool):
            def gather(s, i, n):
                pool.wait_ge(staged, n + 1)
                wait_count(pool, ex.used, n - G + 1)
                pool.sem_inc(tick, 1)
                for k in range(i * GK, (i + 1) * GK):
                    pool.indirect_dma_start(out=q[:, k, :], out_offset=None, in_=g.q[:, :],
                                            in_offset=bass.IndirectOffsetOnAxis(ap=q_slot[:, k:k + 1], axis=0))\
                        .then_inc(arrived[i], 16)

            def slot(s, i):
                on(gather, s, i, 0, S)
                if i == G - 1:
                    on(lambda *a: ex.gather(pool, *a), s, i, G, S)

            ex.gather(pool, 0, 0, 0)
            slots(pool, S, slot, 0)
    g.clear_semaphores()


def fast_l1_messages(g):
    nc, S, t = g.nc, g.S, g.t
    tables = g.fast_sums[1]
    T = len(tables)
    assert T == GK
    BEYOND = 8192.0
    assert g.N + P < BEYOND
    with ExitStack() as ph:
        sb = lambda name, shape, dt=F32: ph.enter_context(g.sbuf(name, shape, dt))
        sem = lambda name: g.sem(ph, name)
        ex, ct = Expand(g, ph, g.v3), Counts(g, ph, 2)
        below = sb("below", [P, K, H])
        key_slot, late, once = sb("key_slot", [P, K]), sb("late", [P, K]), sb("once", [P, K], I32)
        same, junk, spare = sb("same", [P, K, P]), sb("junk", [P, K, P]), sb("spare_row", [P, K])
        msg, tile_sums = sb("msg", [P, K, W]), sb("tile_sums", [P, K, W])
        key_ps = ph.enter_context(g.psum("key_ps", [P, GK + 1, 128], F32))
        sum_ps = [ph.enter_context(g.psum(f"sum_ps{b}", [P, 512], F32)) for b in range(2)]
        exp_in, exp_out, staged, key_rows = sem("exp_in"), sem("exp_out"), sem("staged"), sem("key_rows")
        compared, counted, spare_out, once_ready = sem("compared"), sem("counted"), sem("spare_out"), sem("once_ready")
        summed, sums_out, tick = sem("summed"), sem("sums_out"), sem("pool_tick")
        scattered, s_base = g.scattered, list(g.scatters)
        for u in range(T):
            g.scatters[u] += 16 * G * S
        block = ph.enter_context(nc.Block())
        grp = lambda i: slice(i * GK, (i + 1) * GK)

        def sent(eng, n):
            if not isinstance(n, int) or n >= 0:
                for u in range(T):
                    eng.wait_ge(scattered[u], 16 * n + (s_base[u] + 16))

        @block.sync
        def _(sp):
            def slot(s, i):
                on(lambda *a: ex.load(sp, *a), s, i, G, S)
                if i == 1:
                    on(lambda *a: ct.store(sp, *a), s, i, -G, S)

            slots(sp, S, slot, G)
            ct.store(sp, S - 1, 0, 0)
            sp.wait_ge(ct.stored, 16 * S)

        @block.tensor
        def _(pe):
            def keys(s, i, n):
                pe.wait_ge(staged, n + 1)
                wait_count(pe, compared, n)
                for k in range(GK):
                    ins = pe.transpose(key_ps[:, k, 0:P],
                                       key_slot[:, i * GK + k:i * GK + k + 1].to_broadcast([P, P]),
                                       t["ident"][0:P, 0:P])
                ins.then_inc(key_rows, 1)

            def tile_products(s, i, n):
                pe.wait_ge(compared, n + 1)
                pe.wait_ge(ex.used, n + 1)
                wait_count(pe, sums_out, n if i == 0 else n - 1)
                for k in range(GK):
                    ins = pe.matmul(sum_ps[i % 2][0:P, k * W:(k + 1) * W], same[:, i * GK + k, :],
                                    msg[:, i * GK + k, :], start=True, stop=True)
                ins.then_inc(summed, 1)

            def slot(s, i):
                on(lambda *a: ex.product(pe, *a), s, i, 1, S)
                on(keys, s, i, 3, S)
                on(tile_products, s, i, 0, S)
                on(lambda *a: ct.products(pe, *a), s, i, 0, S)

            slots(pe, S, slot, 3)

        @block.scalar
        def _(act):
            def weights(s, i, n):
                act.wait_ge(exp_in, n + 1)
                wait_count(act, summed, n - G + 1)
                act.activation(msg[:, grp(i), C:W], below[:, grp(i), :], ACT.Exp).then_inc(exp_out, 1)

            def sums_of(s, i, n):
                act.wait_ge(summed, n + 1)
                sent(act, n - G)
                act.copy(tile_sums[:, grp(i), :].rearrange("p k w -> p (k w)"), sum_ps[i % 2][0:P, 0:GK * W])\
                    .then_inc(sums_out, 1)

            def slot(s, i):
                if i == 0:
                    on(lambda *a: ct.copy_out(act, *a), s, i, -G, S)
                if i == G - 1:
                    on(lambda *a: ex.copy(act, *a), s, i, 1, S)
                on(weights, s, i, 2, S)
                on(lambda *a: ct.blocks_of(act, *a), s, i, 1, S)
                on(sums_of, s, i, 0, S)

            slots(act, S, slot, 2)
            ct.copy_out(act, S - 1, 0, 0)

        @block.vector
        def _(dve):
            def stage(s, i, n):
                wait_count(dve, key_rows, n - G + 1)
                wait_count(dve, once_ready, n - G + 1)
                dve.tensor_copy(key_slot[:, grp(i)], t["src_f"][:, bass.ds(s, 1), grp(i)].rearrange("p o k -> p (o k)"))\
                    .then_inc(staged, 1)

            def compare(s, i, n):
                dve.wait_ge(key_rows, n + 1)
                wait_count(dve, summed, n - G + 1)
                dve.tensor_tensor(same[:, grp(i), :], key_ps[:, 0:GK, 0:P], bcast(key_slot[:, grp(i)], P),
                                  ALU.is_equal).then_inc(compared, 1)

            def shifted(s, i, n):
                wait_count(dve, exp_out, n - G + 1)
                dve.tensor_tensor(below[:, grp(i), :], g.scores[:, bass.ds(s * K + i * GK, GK), :], rows(g.top[:], GK),
                                  ALU.subtract).then_inc(exp_in, 1)

            def count(s, i, n):
                dve.wait_ge(compared, n + 1)
                wait_count(dve, spare_out, n - G + 1)
                for k in range(i * GK, (i + 1) * GK):
                    ins = dve.scalar_tensor_tensor(out=junk[:, k, :], in0=same[:, k, :], scalar=1.0, in1=t["lower"][:],
                                                   op0=ALU.mult, op1=ALU.mult, accum_out=late[:, k:k + 1])
                ins.then_inc(counted, 1)

            def spare_row(s, i, n):
                dve.wait_ge(counted, n + 1)
                wait_count(dve, once_ready, n - G + 1)
                dve.tensor_scalar(spare[:, grp(i)], late[:, grp(i)], BEYOND, t["trash"][:, 0:1], ALU.mult, ALU.min)\
                    .then_inc(spare_out, 1)

            def list_rows(s, i, n):
                dve.wait_ge(spare_out, n + 1)
                sent(dve, n - G)
                dve.tensor_tensor(once[:, grp(i)], key_slot[:, grp(i)], spare[:, grp(i)], ALU.max).then_inc(once_ready, 1)

            def weigh(s, i, n):
                dve.wait_ge(ex.spread, n + 1)
                dve.wait_ge(exp_out, n + 1)
                wait_count(dve, summed, n - G + 1)
                dve.tensor_tensor(
                    msg[:, grp(i), 0:C].rearrange("p k (h d) -> p k h d", h=H),
                    ex.ps[i % 2][:, 0:GK * C].rearrange("p (k h d) -> p k h d", k=GK, h=H),
                    msg[:, grp(i), C:W].unsqueeze(3).to_broadcast([P, GK, H, C // H]), ALU.mult).then_inc(ex.used, 1)

            def slot(s, i):
                on(stage, s, i, 5, S)
                on(weigh, s, i, 1, S)
                on(spare_row, s, i, 2, S)
                on(compare, s, i, 3, S)
                on(list_rows, s, i, 2, S)
                on(lambda *a: ex.onehot(dve, *a), s, i, 3, S)
                on(count, s, i, 3, S)
                on(shifted, s, i, 3, S)
                if i == 1:
                    on(lambda *a: ex.stage(dve, *a), s, i, G, S)
                on(lambda *a: ct.cells_of(dve, *a), s, i, 1, S)

            slots(dve, S, slot, 5)

        @block.gpsimd
        def _(pool):
            def scatter(s, i, n):
                pool.wait_ge(once_ready, n + 1)
                pool.wait_ge(sums_out, n + 1)
                for u in range(T):
                    if not isinstance(n, int) or n > 0:
                        pool.wait_ge(scattered[u], 16 * n + s_base[u])
                    pool.sem_inc(tick, 1)
                    pool.indirect_dma_start(out=tables[u][:, :],
                                            out_offset=bass.IndirectOffsetOnAxis(ap=once[:, i * GK + u:i * GK + u + 1], axis=0),
                                            in_=tile_sums[:, i * GK + u, :], in_offset=None, compute_op=ALU.add)\
                        .then_inc(scattered[u], 16)

            def slot(s, i):
                if i == 1:
                    on(lambda *a: ex.gather(pool, *a), s, i, G, S)
                on(scatter, s, i, 0, S)

            slots(pool, S, slot, G)
            for u in range(T):
                pool.wait_ge(scattered[u], s_base[u] + 16 * G * S)
    g.clear_semaphores()


def split_features(g, pairs):
    with ExitStack() as ph:
        rounded, taken = g.sem(ph, "rounded"), g.sem(ph, "taken")
        block = ph.enter_context(g.nc.Block())
        M = len(pairs)

        @block.scalar
        def _(act):
            for j in range(3):
                for m, (x, parts) in enumerate(pairs):
                    if j:
                        act.wait_ge(taken, (j - 1) * M + m + 1)
                    act.copy(parts[:, :, j, :], x[:]).then_inc(rounded, 1)
            act.wait_ge(rounded, 3 * M)

        @block.vector
        def _(dve):
            for j in range(2):
                for m, (x, parts) in enumerate(pairs):
                    dve.wait_ge(rounded, j * M + m + 1)
                    dve.tensor_tensor(x[:], x[:], parts[:, :, j, :], ALU.subtract).then_inc(taken, 1)


def split_normed(g, x, parts):
    on_vector(g, [
        ("dve", lambda e: e.tensor_scalar(parts[0], x, NORM_SCALE, None, ALU.mult)),
        ("dve", lambda e: e.scalar_tensor_tensor(out=parts[1], in0=x, scalar=NORM_SCALE, in1=parts[0],
                                                 op0=ALU.mult, op1=ALU.subtract)),
    ])


def fast_sum_neighbours(g, x2, weight, tables):
    nc, S, NB, t = g.nc, g.S, g.NB, g.t
    WB = 5
    CB = 5
    steps, chunks = S // WB, NB // CB
    T = len(tables)
    assert S % WB == 0 and NB % CB == 0 and steps % 2 == 1

    def pairs(eng, body):
        body(0, 0, False)
        with eng.Fori(0, steps // 2) as h:
            body(h * 2 + 1, 1, True)
            body(h * 2 + 2, 0, True)

    with ExitStack() as ph:
        sb = lambda name, shape, dt=F32: ph.enter_context(g.sbuf(name, shape, dt))
        sem = lambda name: g.sem(ph, name)
        counts = sb("counts_in", [P, WB, NB * R], F16)
        aggT, out_rows, slot = sb("aggT", [C, WB * R]), sb("agg_rows", [R, WB, C]), sb("agg_slot", [R, WB], I32)
        agg_ps = [ph.enter_context(g.psum(f"agg_ps{b}", [C, 512], F32)) for b in range(2)]
        row_ps = ph.enter_context(g.psum("agg_row_ps", [R, 2, 512], F32))
        loaded = [sem(f"counts_loaded{c}") for c in range(chunks)]
        used, agg_out, row_ready, row_out = sem("counts_used"), sem("agg_out"), sem("agg_row_ready"), sem("agg_row_out")
        staged, tick = sem("agg_staged"), sem("agg_tick")
        scattered, s_base = g.scattered, list(g.scatters)
        turns = [len(range(u, WB, T)) for u in range(T)]
        for u in range(T):
            g.scatters[u] += 16 * turns[u] * steps
        block = ph.enter_context(nc.Block())

        def sent(eng, s):
            for u in range(T):
                eng.wait_ge(scattered[u], 16 * turns[u] * s + s_base[u])

        @block.sync
        def _(sp):
            def body(s, before, last):
                for c in range(chunks):
                    if before:
                        sp.wait_ge(used, (s - 1) * chunks + (c + 1))
                    at = slice(c * CB * R, (c + 1) * CB * R)
                    sp.dma_start(counts[:, :, at], g.counts[bass.ds(s * WB, WB), :, at].rearrange("w p n -> p w n"))\
                        .then_inc(loaded[c], 16)

            edge_loop(sp, steps, body, 1)

        @block.tensor
        def _(pe):
            def rows_through(s):
                pe.wait_ge(agg_out, s + 2)
                pe.wait_ge(row_out, s + 1)
                for w in range(WB):
                    ins = pe.matmul(row_ps[:, w // 4, (w % 4) * C:(w % 4 + 1) * C], aggT[:, w * R:(w + 1) * R], weight[:],
                                    start=True, stop=True)
                ins.then_inc(row_ready, 1)

            def body(s, b, before):
                if before:
                    pe.wait_ge(agg_out, s)
                for c in range(chunks):
                    pe.wait_ge(loaded[c], 16 * s + 16)
                    for j in range(c * CB, (c + 1) * CB):
                        for part in range(2):
                            ins = pe.matmul(agg_ps[b][:, 0:WB * R], x2[:, j, part, :], counts[:, :, j * R:(j + 1) * R],
                                            start=(j == 0 and part == 0), stop=(j == NB - 1 and part == 1))
                    ins.then_inc(used, 1)
                    if before and c == 1:
                        rows_through(s - 1)

            pairs(pe, body)
            rows_through(steps - 1)

        @block.vector
        def _(dve):
            def body(s, b, before):
                dve.wait_ge(used, s * chunks + chunks)
                if before:
                    dve.wait_ge(row_ready, s)
                dve.tensor_scalar(aggT[:], agg_ps[b][:, 0:WB * R], 1.0 / NORM_SCALE, None, ALU.mult).then_inc(agg_out, 1)
                if before:
                    sent(dve, s)
                dve.tensor_copy(slot[:], t["node_i"][:, bass.ds(s * WB, WB)]).then_inc(staged, 1)

            dve.sem_inc(agg_out, 1)
            pairs(dve, body)

        @block.scalar
        def _(act):
            def body(s, before, last):
                act.wait_ge(row_ready, s + 1)
                if before:
                    sent(act, s)
                act.copy(out_rows[:], row_ps[:].rearrange("r b (w c) -> r (b w) c", c=C)[:, 0:WB, :]).then_inc(row_out, 1)

            act.sem_inc(row_out, 1)
            edge_loop(act, steps, body, 1)

        @block.gpsimd
        def _(pool):
            def body(s, before, last):
                pool.wait_ge(staged, s + 1)
                pool.wait_ge(row_out, s + 2)
                for w in range(WB):
                    u = w % T
                    if before or w >= T:
                        pool.wait_ge(scattered[u], 16 * turns[u] * s + (s_base[u] + 16 * (w // T)))
                    pool.sem_inc(tick, 1)
                    pool.indirect_dma_start(out=tables[u][:, :],
                                            out_offset=bass.IndirectOffsetOnAxis(ap=slot[:, w:w + 1], axis=0),
                                            in_=out_rows[:, w, :], in_offset=None, compute_op=ALU.add)\
                        .then_inc(scattered[u], 16)

            edge_loop(pool, steps, body, 1)
            for u in range(T):
                pool.wait_ge(scattered[u], s_base[u] + 16 * turns[u] * steps)
    g.clear_semaphores()


def take_branch(g):
    with ExitStack() as ph:
        entered = g.sem(ph, "entered")
        block = ph.enter_context(g.nc.Block())

        @block.sync
        def _(sp):
            sp.sem_inc(entered, 1)

        @block.gpsimd
        def _(pool):
            pool.sem_inc(entered, 1)

        @block.scalar
        def _(act):
            act.sem_inc(entered, 1)

        @block.tensor
        def _(pe):
            pe.sem_inc(entered, 1)

        @block.vector
        def _(dve):
            dve.sem_inc(entered, 1)


def fast_gnn(g):
    nc, N, NB, S, t = g.nc, g.N, g.NB, g.S, g.t
    x, count, dinv = t["x_sb"], g.count, g.dinv
    sb = lambda c, name, shape, dt=F32: c.enter_context(g.sbuf(name, shape, dt))
    with ExitStack() as ph:
        xa = sb(ph, "xa_sb", [P, NB, C])
        node_linear(g, "xa", x, [(t["Wn1_node"], t["L0_gnn_bn1"], xa)])
        to_table(g, [(g.xa, xa)])
    g.clear_semaphores()
    fast_l0(g)
    shift_cells(g, 0)
    with ExitStack() as ph:
        total = sb(ph, "total", [P, NB, W])
        scr, hid = sb(ph, "scr", [P, NB, C]), sb(ph, "hid", [P, NB, C])
        collect_sums(g, total, None, g.fast_sums[0])
        on_vector(g, [
            ("dve", lambda e: e.tensor_copy(count[:], total[:, :, C:C + 1].rearrange("p j o -> p (j o)"))),
            ("dve", lambda e: e.tensor_tensor(scr[:], bcast(count[:], C), rows(t["L0_gnn_bn2"][:], NB), ALU.mult)),
            ("dve", lambda e: e.scalar_tensor_tensor(out=scr[:], in0=x[:], scalar=2.0, in1=scr[:], op0=ALU.mult, op1=ALU.add)),
            ("dve", lambda e: e.tensor_tensor(scr[:], scr[:], total[:, :, 0:C], ALU.add)),
        ])
        layer_norm(g, scr, hid, dst=x)
    g.clear_semaphores()
    with ExitStack() as lay:
        g.scores = sb(lay, "scores", [P, S * K, H])
        g.top = sb(lay, "top", [P, H])
        g.cut = sb(lay, "cut", [P, S * K])
        with ExitStack() as ph:
            qkv = [sb(ph, n, [P, NB, C]) for n in ("q_sb", "k_sb", "v_sb")]
            k3, v3 = sb(ph, "k3", [P, NB, 3, C], BF16), sb(ph, "v3", [P, NB, 3, C], BF16)
            node_linear(g, "qkv", x, [(t[f"L1_gnn_W{n}_T"], t[f"L1_gnn_b{n}"], o) for n, o in zip("qkv", qkv)])
            split_features(g, [(qkv[1], k3), (qkv[2], v3)])
            spare = t["zeros"][:].bitcast(BF16)[:, 0:3 * C].unsqueeze(1)
            cutoff(g, [(g.q, qkv[0]), (g.k3[0:N, :], k3[:].rearrange("p j a c -> p j (a c)")),
                       (g.v3[0:N, :], v3[:].rearrange("p j a c -> p j (a c)")),
                       (g.k3[N:N + P, :], spare), (g.v3[N:N + P, :], spare)])
        with ExitStack() as ph:
            g.clear_semaphores()
            fast_l1_scores(g)
        head_maximum(g)
        shift_cells(g, 1)
        g.clear_semaphores()
        fast_l1_messages(g)
    with ExitStack() as ph:
        attention_out(g, ph, g.fast_sums[1])
    with ExitStack() as ph:
        x2 = sb(ph, "x2", [P, NB, 2, C], F16)
        split_normed(g, x[:], [x2[:, :, j, :] for j in range(2)])
        g.clear_semaphores()
        fast_sum_neighbours(g, x2, t["L2_gnn_w_neigh_T"], g.fast_sums[2])
    with ExitStack() as ph:
        total, scr = sb(ph, "total", [P, NB, C]), sb(ph, "scr", [P, NB, C])
        part, per = sb(ph, "part", [P, NB, C]), sb(ph, "per", [P, NB])
        collect_sums(g, total, [part], g.fast_sums[2])
        degrees(g, per)
        on_vector(g, [
            ("dve", lambda e: e.tensor_tensor(total[:], total[:], bcast(per[:], C), ALU.mult)),
            ("dve", lambda e: e.tensor_tensor(scr[:], x[:], rows(t["b_l2"][:], NB), ALU.add)),
            ("dve", lambda e: e.tensor_tensor(scr[:], scr[:], total[:], ALU.add)),
        ])
        node_linear(g, "l2s", x, [(t["L2_gnn_w_self_T"], scr, scr)])
        layer_norm(g, scr, total, dst=x)
    g.clear_semaphores()
    with ExitStack() as lay:
        xd, self_loop = sb(lay, "xd", [P, NB, C]), sb(lay, "self_loop", [P, NB, C])
        zero_row = sb(lay, "zero_row", [P, C])
        on_vector(g, [("dve", lambda e: e.memset(zero_row[:], 0.0)),
                      ("dve", lambda e: e.tensor_tensor(xd[:], x[:], bcast(dinv[:], C), ALU.mult))])
        node_linear(g, "h3", xd, [(t["L3_gnn_W"], zero_row, self_loop)])
        with ExitStack() as ph:
            x2 = sb(ph, "x2", [P, NB, 2, C], F16)
            split_normed(g, xd[:], [x2[:, :, j, :] for j in range(2)])
            g.clear_semaphores()
            fast_sum_neighbours(g, x2, t["L3_gnn_W"], g.fast_sums[3])
        total, part = sb(lay, "total", [P, NB, C]), sb(lay, "part", [P, NB, C])
        collect_sums(g, total, [part], g.fast_sums[3])
        convolution_out(g, total[:], self_loop, part)


def gnn(nc, ins, out):
    g = Gnn(nc, ins, out)
    N, NB, S = g.N, g.NB, g.S
    table = lambda name, n, w, dt=F32: nc.dram_tensor(name, (n, w), dt, kind="Internal").ap()
    g.xa, g.q, g.k, g.v = (table(n + "_table", N, C) for n in ("xa", "q", "k", "v"))
    g.k3, g.v3 = table("k3_table", N + P, 3 * C, BF16), table("v3_table", N + P, 3 * C, BF16)
    g.x2, g.h3 = table("x2_table", N, C), table("h3_table", N, C)
    g.sums = [table(f"sums_table{u}", N + P, W) for u in range(TABLES)]
    g.fast_sums = [[table(f"fast_sums{n}_{u}", N + P, w) for u in range(m)]
                   for n, (m, w) in enumerate(((1, W), (GK, W), (2, C), (2, C)))]
    g.counts = nc.dram_tensor("counts_dram", (S, P, NB * R), F16, kind="Internal").ap()
    with ExitStack() as ctx:
        g.scattered = [ctx.enter_context(nc.semaphore(f"scattered{u}")) for u in range(TABLES)]
        g.arrived = [[ctx.enter_context(nc.semaphore(f"arrived{w}{i}")) for i in range(G)] for w in range(2)]
        load_and_lay_out(g, ctx)
        g.count = ctx.enter_context(g.sbuf("count", [P, NB], F32))
        g.dinv = ctx.enter_context(g.sbuf("dinv", [P, NB], F32))
        windows(g, ctx)
        g.clear_semaphores()
        fast = nc.values_load(g.t["fast_ok"][0:1, 0:1], min_val=0, max_val=1)
        with nc.If(fast):
            g.scattered_so_far, g.arrived_so_far = 0, [0, 0]
            g.scatters, g.window_arrived = [0] * TABLES, 0
            take_branch(g)
            fast_gnn(g)
        with nc.Else():
            g.scattered_so_far, g.arrived_so_far = 0, [0, 0]
            take_branch(g)
            general_gnn(g)
        to_table(g, [(g.out, g.t["x_sb"])])


_INS = ["x", "src", "dst", "edge_attr_64", "edge_weight", "edge_weight1",
        "L0_gnn_We1", "L0_gnn_be1", "L0_gnn_We2", "L0_gnn_be2", "L0_gnn_Wt", "L0_gnn_bt",
        "L0_gnn_Wn1", "L0_gnn_bn1", "L0_gnn_Wn2", "L0_gnn_bn2",
        "L1_gnn_Wq", "L1_gnn_bq", "L1_gnn_Wk", "L1_gnn_bk", "L1_gnn_Wv", "L1_gnn_bv",
        "L1_gnn_We1", "L1_gnn_be1", "L1_gnn_We2", "L1_gnn_be2", "L1_gnn_Wo", "L1_gnn_bo",
        "L1_gnn_ln_g", "L1_gnn_ln_b", "L2_gnn_w_self", "L2_gnn_b_self", "L2_gnn_w_neigh",
        "L2_gnn_b_neigh", "L3_gnn_W", "L3_gnn_b"]


def kernel(**inputs):
    import numpy as _np
    import concourse.bacc as _bacc
    from concourse import mybir as _mybir
    from concourse.bass_utils import run_bass_kernel_spmd as _run

    nc = _bacc.Bacc("TRN2", target_bir_lowering=False, num_devices=1)
    arrays, args = {}, {}
    for name in _INS:
        a = _np.ascontiguousarray(inputs[name])
        arrays[f"in_{name}_dram"] = a
        args[name] = nc.dram_tensor(f"in_{name}_dram", a.shape, _mybir.dt.from_np(a.dtype), kind="ExternalInput").ap()
    out = nc.dram_tensor("out_dram", inputs["x"].shape, _mybir.dt.float32, kind="ExternalOutput").ap()
    gnn(nc, args, out)
    r = _run(nc, [arrays], core_ids=[0])
    return r.results[0]["out_dram"]
```
